# Optimizing a Trainium2 kernel written in Bass

```python
import numpy as np
import jax
import jax.numpy as jnp

def _softmax(x, axis=-1):
    return jax.nn.softmax(x, axis=axis)

def _gelu(x):
    return jax.nn.gelu(x, approximate=True)

def _silu(x):
    return jax.nn.silu(x)

def _sigmoid(x):
    return jax.nn.sigmoid(x)

def _layernorm(x, axis=-1, eps=1e-05):
    m = jnp.mean(x, axis=axis, keepdims=True)
    v = jnp.var(x, axis=axis, keepdims=True)
    return (x - m) / jnp.sqrt(v + eps)

def _scatter_add(tgt, idx, src, axis=0):
    return tgt.at[idx].add(src)

def _segment_sum(src, seg, n):
    return jax.ops.segment_sum(src, seg, n)
kernel_name = 'mk_xattn_ffn_d4_seqx_r8_482905'

def setup_inputs(seed: int=0):
    np.random.seed(seed)
    _w = jnp.asarray

    def _rec_inputs():
        import jax
        import jax.numpy as jnp
        _rk = jax.random.key(seed)
        x = -0.0002928 + 1 * jax.random.normal(jax.random.fold_in(_rk, 1), (32, 128, 128), jnp.float32)
        _lenS = 128 - jax.random.randint(jax.random.fold_in(_rk, 7), (32,), 0, max(1, 128 // 4) + 1, jnp.int32)
        _lenS2 = 128 - jax.random.randint(jax.random.fold_in(_rk, 8), (32,), 0, max(1, 128 // 4) + 1, jnp.int32)
        _ctx_1024P = jax.random.normal(jax.random.fold_in(_rk, 11), (32, 16, 128), jnp.float32)
        _ctx_1024c = jax.random.dirichlet(jax.random.fold_in(_rk, 511), 0.3 * jnp.ones((16,), jnp.float32), (32, 128))
        _ctx_1024t = jnp.einsum('bsk,bkd->bsd', _ctx_1024c, _ctx_1024P)
        _ctx_1024t = _ctx_1024t * jax.lax.rsqrt(jnp.mean(jnp.square(_ctx_1024t)) + 1e-12) * 0.953939
        ctx_1024 = -1.39393e-06 + 0.999914 * (_ctx_1024t + 0.3 * jax.random.normal(jax.random.fold_in(_rk, 611), (32, 128, 128), jnp.float32))
        return (x, ctx_1024)
    x, ctx_1024 = _rec_inputs()

    def _L0_xattn_setup():
        import jax, jax.numpy as jnp
        import numpy as np
        B, S, E, NH = (2, 256, 128, 4)
        HD = E // NH

        def _mlstm_head(q, k, v, ig, fg, eps=1e-06):
            s, dh = q.shape
            log_f = jax.nn.log_sigmoid(fg)
            cs = jnp.concatenate([jnp.zeros((1, 1), log_f.dtype), jnp.cumsum(log_f, axis=0)], axis=0)
            neg = jnp.asarray(-0.7 * jnp.finfo(cs.dtype).max, cs.dtype)
            log_d = jnp.where(jnp.tri(s, dtype=bool), (cs - cs.T)[1:, 1:] + ig.T, neg)
            m = jnp.max(log_d, axis=-1, keepdims=True)
            d = jnp.exp(log_d - m)
            c = q @ (k.T / jnp.sqrt(dh)) * d
            n = jnp.maximum(jnp.sum(c, axis=-1, keepdims=True), jnp.exp(-m))
            return c / (n + eps) @ v
        key = jax.random.key(seed)
        ks = jax.random.split(key, 8)
        return {'q': jax.random.normal(ks[0], (B, S, E), jnp.float32), 'k': jax.random.normal(ks[1], (B, S, E), jnp.float32), 'v': jax.random.normal(ks[2], (B, S, E), jnp.float32), 'igate_kernel': jax.random.normal(ks[3], (3 * E, NH), jnp.float32) * 0.02, 'igate_bias': jax.random.normal(ks[4], (NH,), jnp.float32) * 0.1, 'fgate_kernel': jax.random.normal(ks[5], (3 * E, NH), jnp.float32) * 0.02, 'fgate_bias': jnp.linspace(3.0, 6.0, NH, dtype=jnp.float32), 'rms_scale': jax.random.normal(ks[6], (HD,), jnp.float32) * 0.02}
    _L0_xattn_all = _L0_xattn_setup()
    _L0_xattn_in = {k: v for k, v in _L0_xattn_all.items() if k in ('igate_kernel', 'igate_bias', 'fgate_kernel', 'fgate_bias', 'rms_scale')}
    del _L0_xattn_all

    def _L0_ffn_setup():
        import jax, jax.numpy as jnp
        import numpy as np
        CHUNK = 128
        NUM_BITS = 6
        key = jax.random.key(seed)
        k1, k2, k3 = jax.random.split(key, 3)
        B, L, D, E = (4, 512, 128, 64)
        x = jax.random.normal(k1, (B, L, D), dtype=jnp.float32)
        expert_weights = jax.random.normal(k2, (E, D, D), dtype=jnp.float32) * 0.02
        hyperplanes = jax.random.normal(k3, (D, NUM_BITS), dtype=jnp.float32)
        return {'x': x, 'expert_weights': expert_weights, 'hyperplanes': hyperplanes}
    _L0_ffn_all = _L0_ffn_setup()
    _L0_ffn_in = {k: v for k, v in _L0_ffn_all.items() if k in ('expert_weights', 'hyperplanes')}
    del _L0_ffn_all

    def _L1_xattn_setup():
        import jax, jax.numpy as jnp
        import numpy as np
        DIM = 128
        NUM_HEADS = 16
        DIM_HEAD = 64
        INNER = NUM_HEADS * DIM_HEAD
        SCALE = DIM_HEAD ** (-0.5)

        def _layernorm(x, gamma, beta, eps=1e-05):
            mu = jnp.mean(x, axis=-1, keepdims=True)
            var = jnp.mean(jnp.square(x - mu), axis=-1, keepdims=True)
            return (x - mu) * jax.lax.rsqrt(var + eps) * gamma + beta
        key = jax.random.key(seed)
        ks = jax.random.split(key, 8)
        B, SQ, SK = (2, 256, 512)
        x = jax.random.normal(ks[0], (B, SQ, DIM), dtype=jnp.float32)
        context = jax.random.normal(ks[1], (B, SK, DIM), dtype=jnp.float32)
        ln_gamma = jnp.ones((DIM,), jnp.float32)
        ln_beta = jnp.zeros((DIM,), jnp.float32)
        w_q = jax.random.normal(ks[2], (DIM, INNER), dtype=jnp.float32) / np.sqrt(DIM)
        w_kv = jax.random.normal(ks[3], (DIM, 2 * INNER), dtype=jnp.float32) / np.sqrt(DIM)
        w_out = jax.random.normal(ks[4], (INNER, DIM), dtype=jnp.float32) / np.sqrt(INNER)
        b_out = jnp.zeros((DIM,), jnp.float32)
        gate = jnp.array([0.5], jnp.float32)
        return {'x': x, 'context': context, 'ln_gamma': ln_gamma, 'ln_beta': ln_beta, 'w_q': w_q, 'w_kv': w_kv, 'w_out': w_out, 'b_out': b_out, 'gate': gate}
    _L1_xattn_all = _L1_xattn_setup()
    _L1_xattn_in = {k: v for k, v in _L1_xattn_all.items() if k in ('ln_gamma', 'ln_beta', 'w_q', 'w_kv', 'w_out', 'b_out', 'gate')}
    del _L1_xattn_all

    def _L1_ffn_setup():
        import jax, jax.numpy as jnp
        import numpy as np
        NUM_EXPERTS = 8
        IN_FEATURES = 128
        HIDDEN_FEATURES = 512
        GATE_DIM = 16
        EPS = 0.0001
        key = jax.random.key(seed)
        ks = jax.random.split(key, 7)
        hidden_states = jax.random.normal(ks[0], (1, 256, IN_FEATURES), dtype=jnp.float32)
        wg_red = jax.random.normal(ks[1], (GATE_DIM, IN_FEATURES), dtype=jnp.float32) * 0.02
        wg = jax.random.normal(ks[2], (NUM_EXPERTS, GATE_DIM), dtype=jnp.float32)
        w1 = jax.random.uniform(ks[3], (NUM_EXPERTS, IN_FEATURES, HIDDEN_FEATURES), dtype=jnp.float32)
        b1 = jax.random.uniform(ks[4], (NUM_EXPERTS, HIDDEN_FEATURES), dtype=jnp.float32)
        w2 = jax.random.uniform(ks[5], (NUM_EXPERTS, HIDDEN_FEATURES, IN_FEATURES), dtype=jnp.float32)
        b2 = jax.random.uniform(ks[6], (NUM_EXPERTS, IN_FEATURES), dtype=jnp.float32)
        return {'hidden_states': hidden_states, 'wg_red': wg_red, 'wg': wg, 'w1': w1, 'b1': b1, 'w2': w2, 'b2': b2}
    _L1_ffn_all = _L1_ffn_setup()
    _L1_ffn_in = {k: v for k, v in _L1_ffn_all.items() if k in ('wg_red', 'wg', 'w1', 'b1', 'w2', 'b2')}
    del _L1_ffn_all

    def _L2_xattn_setup():
        import jax, jax.numpy as jnp
        import numpy as np
        D_MODEL = 128
        N_HEADS = 16
        HEAD_SIZE = D_MODEL // N_HEADS
        key = jax.random.key(seed)
        ks = jax.random.split(key, 10)
        B, Lx, Ly = (2, 256, 256)
        s = 0.02
        x = jax.random.normal(ks[0], (B, Lx, D_MODEL), dtype=jnp.float32)
        y = jax.random.normal(ks[1], (B, Ly, D_MODEL), dtype=jnp.float32)
        Wq = jax.random.normal(ks[2], (N_HEADS, D_MODEL, HEAD_SIZE), dtype=jnp.float32) * s
        bq = jax.random.normal(ks[3], (N_HEADS, HEAD_SIZE), dtype=jnp.float32) * s
        Wk = jax.random.normal(ks[4], (N_HEADS, D_MODEL, HEAD_SIZE), dtype=jnp.float32) * s
        bk = jax.random.normal(ks[5], (N_HEADS, HEAD_SIZE), dtype=jnp.float32) * s
        Wv = jax.random.normal(ks[6], (N_HEADS, D_MODEL, HEAD_SIZE), dtype=jnp.float32) * s
        bv = jax.random.normal(ks[7], (N_HEADS, HEAD_SIZE), dtype=jnp.float32) * s
        Wo = jax.random.normal(ks[8], (D_MODEL, D_MODEL), dtype=jnp.float32) * s
        bo = jax.random.normal(ks[9], (D_MODEL,), dtype=jnp.float32) * s
        return {'x': x, 'y': y, 'Wq': Wq, 'bq': bq, 'Wk': Wk, 'bk': bk, 'Wv': Wv, 'bv': bv, 'Wo': Wo, 'bo': bo}
    _L2_xattn_all = _L2_xattn_setup()
    _L2_xattn_in = {k: v for k, v in _L2_xattn_all.items() if k in ('Wq', 'bq', 'Wk', 'bk', 'Wv', 'bv', 'Wo', 'bo')}
    del _L2_xattn_all

    def _L2_ffn_setup():
        import jax, jax.numpy as jnp
        import numpy as np
        TOP_K = 4
        N_GROUP = 4
        TOPK_GROUP = 2
        ROUTED_SCALING = 1.0

        def _route(x_flat, gate_weight, e_bias):
            T = x_flat.shape[0]
            E = gate_weight.shape[0]
            logits = jnp.einsum('th,eh->te', x_flat, gate_weight)
            scores = jax.nn.sigmoid(logits)
            scores_for_choice = scores + e_bias[None, :]
            grp = scores_for_choice.reshape(T, N_GROUP, E // N_GROUP)
            top2, _ = jax.lax.top_k(grp, 2)
            group_scores = top2.sum(axis=-1)
            _, group_idx = jax.lax.top_k(group_scores, TOPK_GROUP)
            group_mask = jax.nn.one_hot(group_idx, N_GROUP, dtype=scores.dtype).sum(axis=1)
            score_mask = jnp.repeat(group_mask, E // N_GROUP, axis=1)
            tmp_scores = jnp.where(score_mask > 0, scores_for_choice, 0.0)
            _, topk_idx = jax.lax.top_k(tmp_scores, TOP_K)
            topk_weight = jnp.take_along_axis(scores, topk_idx, axis=1)
            denom = topk_weight.sum(axis=-1, keepdims=True) + 1e-20
            topk_weight = topk_weight / denom * ROUTED_SCALING
            return (topk_idx, topk_weight)
        key = jax.random.key(seed)
        k1, k2, k3, k4, k5 = jax.random.split(key, 5)
        B, S, H, I, E = (1, 256, 128, 64, 16)
        hidden_states = jax.random.normal(k1, (B, S, H), dtype=jnp.float32)
        gate_weight = jax.random.normal(k2, (E, H), dtype=jnp.float32) * (1.0 / np.sqrt(H))
        e_bias = jnp.zeros((E,), dtype=jnp.float32)
        gate_proj = jax.random.normal(k3, (E, I, H), dtype=jnp.float32) * 0.02
        up_proj = jax.random.normal(k4, (E, I, H), dtype=jnp.float32) * 0.02
        down_proj = jax.random.normal(k5, (E, H, I), dtype=jnp.float32) * 0.02
        return {'hidden_states': hidden_states, 'gate_weight': gate_weight, 'e_bias': e_bias, 'gate_proj': gate_proj, 'up_proj': up_proj, 'down_proj': down_proj}
    _L2_ffn_all = _L2_ffn_setup()
    _L2_ffn_in = {k: v for k, v in _L2_ffn_all.items() if k in ('gate_weight', 'e_bias', 'gate_proj', 'up_proj', 'down_proj')}
    del _L2_ffn_all

    def _L3_xattn_setup():
        import jax, jax.numpy as jnp
        import numpy as np
        NUM_HEADS = 16
        D_MODEL = 128
        HEAD_DIM = D_MODEL // NUM_HEADS
        SCALE = float(np.sqrt(HEAD_DIM))
        EPS = 1e-05

        def layernorm(x, g, b):
            mu = jnp.mean(x, axis=-1, keepdims=True)
            var = jnp.mean(jnp.square(x - mu), axis=-1, keepdims=True)
            return (x - mu) * jax.lax.rsqrt(var + EPS) * g + b
        key = jax.random.key(seed)
        ks = jax.random.split(key, 8)
        B, Nq, Nc = (2, 256, 256)
        s = 0.02
        return {'x_query': jax.random.normal(ks[0], (B, Nq, D_MODEL), jnp.float32), 'x_context': jax.random.normal(ks[1], (B, Nc, D_MODEL), jnp.float32), 'Wq': jax.random.normal(ks[2], (D_MODEL, D_MODEL), jnp.float32) * s, 'Wkv': jax.random.normal(ks[3], (D_MODEL, 2 * D_MODEL), jnp.float32) * s, 'Wp': jax.random.normal(ks[4], (D_MODEL, D_MODEL), jnp.float32) * s, 'bp': jnp.zeros((D_MODEL,), jnp.float32), 'ln_g': jnp.ones((HEAD_DIM,), jnp.float32), 'ln_b': jnp.zeros((HEAD_DIM,), jnp.float32)}
    _L3_xattn_all = _L3_xattn_setup()
    _L3_xattn_in = {k: v for k, v in _L3_xattn_all.items() if k in ('Wq', 'Wkv', 'Wp', 'bp', 'ln_g', 'ln_b')}
    del _L3_xattn_all

    def _L3_ffn_setup():
        import jax, jax.numpy as jnp
        import numpy as np
        from jax import lax
        TOP_K = 4
        N_GROUP = 4
        TOPK_GROUP = 2
        ROUTED_SCALE = 2.5
        NEG_INF = -1000000000.0

        def _route(xf, router_weight, router_bias):
            T = xf.shape[0]
            E = router_weight.shape[0]
            logits = xf @ router_weight.T
            scores = jax.nn.sigmoid(logits)
            s_choice = scores + router_bias
            per_group = E // N_GROUP
            sg = s_choice.reshape(T, N_GROUP, per_group)
            group_scores = lax.top_k(sg, 2)[0].sum(-1)
            _, gidx = lax.top_k(group_scores, TOPK_GROUP)
            gmask = jnp.zeros((T, N_GROUP), dtype=bool).at[jnp.arange(T)[:, None], gidx].set(True)
            masked = jnp.where(gmask[:, :, None], sg, NEG_INF).reshape(T, E)
            _, topk_idx = lax.top_k(masked, TOP_K)
            w = jnp.take_along_axis(scores, topk_idx, axis=1)
            w = w / (w.sum(-1, keepdims=True) + 1e-20) * ROUTED_SCALE
            combine = jnp.zeros((T, E), dtype=xf.dtype).at[jnp.arange(T)[:, None], topk_idx].add(w)
            return combine
        key = jax.random.key(seed)
        ks = jax.random.split(key, 6)
        B, S, H, I, E = (2, 256, 128, 64, 16)
        x = jax.random.normal(ks[0], (B, S, H), dtype=jnp.float32)
        router_weight = jax.random.normal(ks[1], (E, H), dtype=jnp.float32) * 0.02
        router_bias = jnp.zeros((E,), dtype=jnp.float32)
        w_gate = jax.random.normal(ks[2], (E, I, H), dtype=jnp.float32) * 0.02
        w_up = jax.random.normal(ks[3], (E, I, H), dtype=jnp.float32) * 0.02
        w_down = jax.random.normal(ks[4], (E, H, I), dtype=jnp.float32) * 0.02
        return {'x': x, 'router_weight': router_weight, 'router_bias': router_bias, 'w_gate': w_gate, 'w_up': w_up, 'w_down': w_down}
    _L3_ffn_all = _L3_ffn_setup()
    _L3_ffn_in = {k: v for k, v in _L3_ffn_all.items() if k in ('router_weight', 'router_bias', 'w_gate', 'w_up', 'w_down')}
    del _L3_ffn_all
    return {'x': x, 'ctx_1024': ctx_1024, 'L0_xattn_igate_kernel': _L0_xattn_in['igate_kernel'], 'L0_xattn_igate_bias': _L0_xattn_in['igate_bias'], 'L0_xattn_fgate_kernel': _L0_xattn_in['fgate_kernel'], 'L0_xattn_fgate_bias': _L0_xattn_in['fgate_bias'], 'L0_xattn_rms_scale': _L0_xattn_in['rms_scale'], 'L0_ffn_expert_weights': _L0_ffn_in['expert_weights'], 'L0_ffn_hyperplanes': _L0_ffn_in['hyperplanes'], 'L1_xattn_ln_gamma': _L1_xattn_in['ln_gamma'], 'L1_xattn_ln_beta': _L1_xattn_in['ln_beta'], 'L1_xattn_w_q': _L1_xattn_in['w_q'], 'L1_xattn_w_kv': _L1_xattn_in['w_kv'], 'L1_xattn_w_out': _L1_xattn_in['w_out'], 'L1_xattn_b_out': _L1_xattn_in['b_out'], 'L1_xattn_gate': _L1_xattn_in['gate'], 'L1_ffn_wg_red': _L1_ffn_in['wg_red'], 'L1_ffn_wg': _L1_ffn_in['wg'], 'L1_ffn_w1': _L1_ffn_in['w1'], 'L1_ffn_b1': _L1_ffn_in['b1'], 'L1_ffn_w2': _L1_ffn_in['w2'], 'L1_ffn_b2': _L1_ffn_in['b2'], 'L2_xattn_Wq': _L2_xattn_in['Wq'], 'L2_xattn_bq': _L2_xattn_in['bq'], 'L2_xattn_Wk': _L2_xattn_in['Wk'], 'L2_xattn_bk': _L2_xattn_in['bk'], 'L2_xattn_Wv': _L2_xattn_in['Wv'], 'L2_xattn_bv': _L2_xattn_in['bv'], 'L2_xattn_Wo': _L2_xattn_in['Wo'], 'L2_xattn_bo': _L2_xattn_in['bo'], 'L2_ffn_gate_weight': _L2_ffn_in['gate_weight'], 'L2_ffn_e_bias': _L2_ffn_in['e_bias'], 'L2_ffn_gate_proj': _L2_ffn_in['gate_proj'], 'L2_ffn_up_proj': _L2_ffn_in['up_proj'], 'L2_ffn_down_proj': _L2_ffn_in['down_proj'], 'L3_xattn_Wq': _L3_xattn_in['Wq'], 'L3_xattn_Wkv': _L3_xattn_in['Wkv'], 'L3_xattn_Wp': _L3_xattn_in['Wp'], 'L3_xattn_bp': _L3_xattn_in['bp'], 'L3_xattn_ln_g': _L3_xattn_in['ln_g'], 'L3_xattn_ln_b': _L3_xattn_in['ln_b'], 'L3_ffn_router_weight': _L3_ffn_in['router_weight'], 'L3_ffn_router_bias': _L3_ffn_in['router_bias'], 'L3_ffn_w_gate': _L3_ffn_in['w_gate'], 'L3_ffn_w_up': _L3_ffn_in['w_up'], 'L3_ffn_w_down': _L3_ffn_in['w_down']}

def reference(x, ctx_1024, L0_xattn_igate_kernel, L0_xattn_igate_bias, L0_xattn_fgate_kernel, L0_xattn_fgate_bias, L0_xattn_rms_scale, L0_ffn_expert_weights, L0_ffn_hyperplanes, L1_xattn_ln_gamma, L1_xattn_ln_beta, L1_xattn_w_q, L1_xattn_w_kv, L1_xattn_w_out, L1_xattn_b_out, L1_xattn_gate, L1_ffn_wg_red, L1_ffn_wg, L1_ffn_w1, L1_ffn_b1, L1_ffn_w2, L1_ffn_b2, L2_xattn_Wq, L2_xattn_bq, L2_xattn_Wk, L2_xattn_bk, L2_xattn_Wv, L2_xattn_bv, L2_xattn_Wo, L2_xattn_bo, L2_ffn_gate_weight, L2_ffn_e_bias, L2_ffn_gate_proj, L2_ffn_up_proj, L2_ffn_down_proj, L3_xattn_Wq, L3_xattn_Wkv, L3_xattn_Wp, L3_xattn_bp, L3_xattn_ln_g, L3_xattn_ln_b, L3_ffn_router_weight, L3_ffn_router_bias, L3_ffn_w_gate, L3_ffn_w_up, L3_ffn_w_down):
    import jax
    import jax.numpy as jnp

    def _L0_xattn_ref(q, k, v, igate_kernel, igate_bias, fgate_kernel, fgate_bias, rms_scale):
        import jax, jax.numpy as jnp
        import numpy as np
        B, S, E, NH = (2, 256, 128, 4)
        HD = E // NH

        def _mlstm_head(q, k, v, ig, fg, eps=1e-06):
            s, dh = q.shape
            log_f = jax.nn.log_sigmoid(fg)
            cs = jnp.concatenate([jnp.zeros((1, 1), log_f.dtype), jnp.cumsum(log_f, axis=0)], axis=0)
            neg = jnp.asarray(-0.7 * jnp.finfo(cs.dtype).max, cs.dtype)
            log_d = jnp.where(jnp.tri(s, dtype=bool), (cs - cs.T)[1:, 1:] + ig.T, neg)
            m = jnp.max(log_d, axis=-1, keepdims=True)
            d = jnp.exp(log_d - m)
            c = q @ (k.T / jnp.sqrt(dh)) * d
            n = jnp.maximum(jnp.sum(c, axis=-1, keepdims=True), jnp.exp(-m))
            return c / (n + eps) @ v
        b, s, e = q.shape
        nh = igate_kernel.shape[1]
        hd = e // nh
        gate_in = jnp.concatenate((q, k, v), axis=-1)
        ig = (gate_in @ igate_kernel + igate_bias).swapaxes(-1, -2)[..., None]
        fg = (gate_in @ fgate_kernel + fgate_bias).swapaxes(-1, -2)[..., None]
        qh = q.reshape(b, s, nh, hd).swapaxes(1, 2)
        kh = k.reshape(b, s, nh, hd).swapaxes(1, 2)
        vh = v.reshape(b, s, nh, hd).swapaxes(1, 2)
        h = jax.vmap(jax.vmap(_mlstm_head))(qh, kh, vh, ig, fg)
        var = jnp.mean(jnp.square(h.astype(jnp.float32)), axis=-1, keepdims=True)
        h = (h * jax.lax.rsqrt(var + 1e-06)).astype(h.dtype) * (1.0 + rms_scale)
        return h.swapaxes(1, 2).reshape(b, s, e)

    def _L0_ffn_ref(x, expert_weights, hyperplanes):
        import jax, jax.numpy as jnp
        import numpy as np
        CHUNK = 128
        NUM_BITS = 6
        B, L, D = x.shape
        C = L // CHUNK
        xr = x.reshape(B, C, CHUNK, D)
        chunk_emb = xr.mean(axis=2)
        proj = chunk_emb @ hyperplanes
        bits = (proj > 0).astype(jnp.int32)
        powers = (2 ** jnp.arange(NUM_BITS)).astype(jnp.int32)
        e1 = jnp.sum(bits * powers, axis=-1)
        weakest = jnp.argmin(jnp.abs(proj), axis=-1)
        flip = (2 ** weakest).astype(jnp.int32)
        e2 = jnp.bitwise_xor(e1, flip)
        out = jnp.zeros_like(xr)
        for idx in (e1, e2):
            w = expert_weights[idx]
            out = out + jnp.einsum('bcld,bcde->bcle', xr, w)
        out = out * 0.5
        return out.reshape(B, L, D)

    def _L1_xattn_ref(x, context, ln_gamma, ln_beta, w_q, w_kv, w_out, b_out, gate):
        import jax, jax.numpy as jnp
        import numpy as np
        DIM = 128
        NUM_HEADS = 16
        DIM_HEAD = 64
        INNER = NUM_HEADS * DIM_HEAD
        SCALE = DIM_HEAD ** (-0.5)

        def _layernorm(x, gamma, beta, eps=1e-05):
            mu = jnp.mean(x, axis=-1, keepdims=True)
            var = jnp.mean(jnp.square(x - mu), axis=-1, keepdims=True)
            return (x - mu) * jax.lax.rsqrt(var + eps) * gamma + beta
        B, SQ, _ = x.shape
        SK = context.shape[1]
        xn = _layernorm(x, ln_gamma, ln_beta)
        q = (xn @ w_q).reshape(B, SQ, NUM_HEADS, DIM_HEAD)
        kv = context @ w_kv
        k, v = jnp.split(kv, 2, axis=-1)
        k = k.reshape(B, SK, NUM_HEADS, DIM_HEAD)
        v = v.reshape(B, SK, NUM_HEADS, DIM_HEAD)
        scores = jnp.einsum('bqhd,bkhd->bhqk', q * SCALE, k)
        attn = jax.nn.softmax(scores, axis=-1)
        out = jnp.einsum('bhqk,bkhd->bqhd', attn, v).reshape(B, SQ, INNER)
        out = out @ w_out + b_out
        return out * jnp.tanh(gate[0])

    def _L1_ffn_ref(hidden_states, wg_red, wg, w1, b1, w2, b2):
        import jax, jax.numpy as jnp
        import numpy as np
        NUM_EXPERTS = 8
        IN_FEATURES = 128
        HIDDEN_FEATURES = 512
        GATE_DIM = 16
        EPS = 0.0001
        b, t, c = hidden_states.shape
        x = hidden_states.reshape(-1, c)
        xr = x @ wg_red.T
        wg_unit = wg / jnp.maximum(jnp.linalg.norm(wg, axis=1, keepdims=True), EPS)
        logits = xr @ wg_unit.T
        gates = jax.nn.softmax(logits, axis=1)
        indices_s = jnp.argmax(gates, axis=1)
        scores = jnp.max(gates, axis=1)
        E = wg.shape[0]
        out = jnp.zeros_like(x)
        for e in range(E):
            mask = (indices_s == e).astype(x.dtype)[:, None]
            h = jax.nn.gelu(x @ w1[e] + b1[e], approximate=False)
            out = out + mask * (h @ w2[e] + b2[e])
        out = out * scores[:, None]
        return out.reshape(b, t, c)

    def _L2_xattn_ref(x, y, Wq, bq, Wk, bk, Wv, bv, Wo, bo):
        import jax, jax.numpy as jnp
        import numpy as np
        D_MODEL = 128
        N_HEADS = 16
        HEAD_SIZE = D_MODEL // N_HEADS
        Q = jnp.einsum('bxd,hde->bhxe', x, Wq) + bq[None, :, None, :]
        K = jnp.einsum('byd,hde->bhye', y, Wk) + bk[None, :, None, :]
        V = jnp.einsum('byd,hde->bhye', y, Wv) + bv[None, :, None, :]
        scale = 1.0 / jnp.sqrt(jnp.float32(HEAD_SIZE))
        scores = jnp.einsum('bhxe,bhye->bhxy', Q, K) * scale
        attn = jax.nn.softmax(scores, axis=-1)
        ctx = jnp.einsum('bhxy,bhye->bhxe', attn, V)
        B, H, Lx, hs = ctx.shape
        ctx = jnp.transpose(ctx, (0, 2, 1, 3)).reshape(B, Lx, H * hs)
        return ctx @ Wo + bo

    def _L2_ffn_ref(hidden_states, gate_weight, e_bias, gate_proj, up_proj, down_proj):
        import jax, jax.numpy as jnp
        import numpy as np
        TOP_K = 4
        N_GROUP = 4
        TOPK_GROUP = 2
        ROUTED_SCALING = 1.0

        def _route(x_flat, gate_weight, e_bias):
            T = x_flat.shape[0]
            E = gate_weight.shape[0]
            logits = jnp.einsum('th,eh->te', x_flat, gate_weight)
            scores = jax.nn.sigmoid(logits)
            scores_for_choice = scores + e_bias[None, :]
            grp = scores_for_choice.reshape(T, N_GROUP, E // N_GROUP)
            top2, _ = jax.lax.top_k(grp, 2)
            group_scores = top2.sum(axis=-1)
            _, group_idx = jax.lax.top_k(group_scores, TOPK_GROUP)
            group_mask = jax.nn.one_hot(group_idx, N_GROUP, dtype=scores.dtype).sum(axis=1)
            score_mask = jnp.repeat(group_mask, E // N_GROUP, axis=1)
            tmp_scores = jnp.where(score_mask > 0, scores_for_choice, 0.0)
            _, topk_idx = jax.lax.top_k(tmp_scores, TOP_K)
            topk_weight = jnp.take_along_axis(scores, topk_idx, axis=1)
            denom = topk_weight.sum(axis=-1, keepdims=True) + 1e-20
            topk_weight = topk_weight / denom * ROUTED_SCALING
            return (topk_idx, topk_weight)
        B, S, H = hidden_states.shape
        E = gate_proj.shape[0]
        x = hidden_states.reshape(-1, H).astype(jnp.float32)
        topk_idx, topk_weight = _route(x, gate_weight, e_bias)
        combine = (jax.nn.one_hot(topk_idx, E, dtype=x.dtype) * topk_weight[..., None]).sum(axis=1)
        g = jnp.einsum('th,eih->tei', x, gate_proj)
        u = jnp.einsum('th,eih->tei', x, up_proj)
        act = jax.nn.silu(g) * u
        expert_out = jnp.einsum('tei,ehi->teh', act, down_proj)
        y = jnp.einsum('teh,te->th', expert_out, combine)
        return y.reshape(B, S, H)

    def _L3_xattn_ref(x_query, x_context, Wq, Wkv, Wp, bp, ln_g, ln_b):
        import jax, jax.numpy as jnp
        import numpy as np
        NUM_HEADS = 16
        D_MODEL = 128
        HEAD_DIM = D_MODEL // NUM_HEADS
        SCALE = float(np.sqrt(HEAD_DIM))
        EPS = 1e-05

        def layernorm(x, g, b):
            mu = jnp.mean(x, axis=-1, keepdims=True)
            var = jnp.mean(jnp.square(x - mu), axis=-1, keepdims=True)
            return (x - mu) * jax.lax.rsqrt(var + EPS) * g + b
        B, Nq, _ = x_query.shape
        Nc = x_context.shape[1]
        H, D = (NUM_HEADS, HEAD_DIM)
        q = (x_query @ Wq).reshape(B, Nq, H, D).transpose(0, 2, 1, 3)
        kv = (x_context @ Wkv).reshape(B, Nc, 2, H, D)
        k = kv[:, :, 0].transpose(0, 2, 1, 3)
        v = kv[:, :, 1].transpose(0, 2, 1, 3)
        q = layernorm(q, ln_g, ln_b)
        k = layernorm(k, ln_g, ln_b)
        q = q * SCALE
        attn = jnp.einsum('bhqd,bhkd->bhqk', q, k)
        attn = jax.nn.softmax(attn, axis=-1)
        out = jnp.einsum('bhqk,bhkd->bhqd', attn, v)
        out = out.transpose(0, 2, 1, 3).reshape(B, Nq, H * D)
        return out @ Wp + bp

    def _L3_ffn_ref(x, router_weight, router_bias, w_gate, w_up, w_down):
        import jax, jax.numpy as jnp
        import numpy as np
        from jax import lax
        TOP_K = 4
        N_GROUP = 4
        TOPK_GROUP = 2
        ROUTED_SCALE = 2.5
        NEG_INF = -1000000000.0

        def _route(xf, router_weight, router_bias):
            T = xf.shape[0]
            E = router_weight.shape[0]
            logits = xf @ router_weight.T
            scores = jax.nn.sigmoid(logits)
            s_choice = scores + router_bias
            per_group = E // N_GROUP
            sg = s_choice.reshape(T, N_GROUP, per_group)
            group_scores = lax.top_k(sg, 2)[0].sum(-1)
            _, gidx = lax.top_k(group_scores, TOPK_GROUP)
            gmask = jnp.zeros((T, N_GROUP), dtype=bool).at[jnp.arange(T)[:, None], gidx].set(True)
            masked = jnp.where(gmask[:, :, None], sg, NEG_INF).reshape(T, E)
            _, topk_idx = lax.top_k(masked, TOP_K)
            w = jnp.take_along_axis(scores, topk_idx, axis=1)
            w = w / (w.sum(-1, keepdims=True) + 1e-20) * ROUTED_SCALE
            combine = jnp.zeros((T, E), dtype=xf.dtype).at[jnp.arange(T)[:, None], topk_idx].add(w)
            return combine
        B, S, H = x.shape
        E = w_gate.shape[0]
        xf = x.reshape(-1, H)
        combine = _route(xf, router_weight, router_bias)
        out = jnp.zeros_like(xf)
        for e in range(E):
            g = xf @ w_gate[e].T
            u = xf @ w_up[e].T
            y_e = jax.nn.silu(g) * u @ w_down[e].T
            out = out + combine[:, e:e + 1] * y_e
        return out.reshape(B, S, H)
    x = x + _L0_xattn_ref(_layernorm(x, axis=-1), ctx_1024, ctx_1024, L0_xattn_igate_kernel, L0_xattn_igate_bias, L0_xattn_fgate_kernel, L0_xattn_fgate_bias, L0_xattn_rms_scale)
    x = x + _L0_ffn_ref(_layernorm(x, axis=-1), L0_ffn_expert_weights, L0_ffn_hyperplanes)
    x = x + _L1_xattn_ref(_layernorm(x, axis=-1), ctx_1024, L1_xattn_ln_gamma, L1_xattn_ln_beta, L1_xattn_w_q, L1_xattn_w_kv, L1_xattn_w_out, L1_xattn_b_out, L1_xattn_gate)
    x = x + _L1_ffn_ref(_layernorm(x, axis=-1), L1_ffn_wg_red, L1_ffn_wg, L1_ffn_w1, L1_ffn_b1, L1_ffn_w2, L1_ffn_b2)
    x = x + _L2_xattn_ref(_layernorm(x, axis=-1), ctx_1024, L2_xattn_Wq, L2_xattn_bq, L2_xattn_Wk, L2_xattn_bk, L2_xattn_Wv, L2_xattn_bv, L2_xattn_Wo, L2_xattn_bo)
    x = x + _L2_ffn_ref(_layernorm(x, axis=-1), L2_ffn_gate_weight, L2_ffn_e_bias, L2_ffn_gate_proj, L2_ffn_up_proj, L2_ffn_down_proj)
    x = x + _L3_xattn_ref(_layernorm(x, axis=-1), ctx_1024, L3_xattn_Wq, L3_xattn_Wkv, L3_xattn_Wp, L3_xattn_bp, L3_xattn_ln_g, L3_xattn_ln_b)
    x = x + _L3_ffn_ref(_layernorm(x, axis=-1), L3_ffn_router_weight, L3_ffn_router_bias, L3_ffn_w_gate, L3_ffn_w_up, L3_ffn_w_down)
    return x

_drawn_inputs = setup_inputs


def setup_inputs(seed=0):
    import zlib

    import numpy as np

    out = dict(_drawn_inputs(seed))
    spreads = {'L1_xattn_ln_gamma': (1.0, 0.6),
     'L1_xattn_ln_beta': (0.0, 2.0),
     'L1_xattn_b_out': (0.0, 0.561),
     'L2_ffn_e_bias': (0.0, 2.0),
     'L3_xattn_bp': (0.0, 2.0),
     'L3_xattn_ln_g': (1.0, 0.6),
     'L3_xattn_ln_b': (0.0, 2.0),
     'L3_ffn_router_bias': (0.0, 2.0)}
    factors = {'L0_xattn_igate_bias': 64.0,
     'L0_xattn_fgate_kernel': 6.024,
     'L0_xattn_rms_scale': 5.305,
     'L1_ffn_b1': 8.0,
     'L1_ffn_b2': 64.0,
     'L2_xattn_Wq': 24.248,
     'L2_xattn_bq': 64.0,
     'L2_xattn_Wk': 24.125,
     'L2_xattn_bk': 64.0,
     'L2_xattn_Wv': 8.0,
     'L2_xattn_bv': 64.0,
     'L2_xattn_Wo': 8.0,
     'L2_xattn_bo': 64.0,
     'L2_ffn_gate_weight': 43.413,
     'L2_ffn_gate_proj': 37.756,
     'L2_ffn_up_proj': 35.066,
     'L2_ffn_down_proj': 34.365,
     'L3_xattn_Wq': 30.823,
     'L3_xattn_Wkv': 22.629,
     'L3_xattn_Wp': 23.188,
     'L3_ffn_router_weight': 30.397,
     'L3_ffn_w_gate': 24.357,
     'L3_ffn_w_up': 22.752,
     'L3_ffn_w_down': 22.399}
    for name, (base, spread) in spreads.items():
        noise = np.random.default_rng([zlib.crc32(name.encode()), seed]).standard_normal(out[name].shape)
        drawn = base * np.exp(spread * noise) if base else spread * noise
        out[name] = jnp.asarray(drawn.astype(out[name].dtype))
    for name, factor in factors.items():
        out[name] = (out[name] * factor).astype(out[name].dtype)
    return out
```

```python
from contextlib import ExitStack

import concourse.bass as bass
from concourse import mybir

P = 128
B = 32
D = 128
F32 = mybir.dt.float32
I32 = mybir.dt.int32
ALU = mybir.AluOpType
ACT = mybir.ActivationFunctionType
AX = mybir.AxisListType
LN_EPS = 1e-5


def run_ticks(eng, units, ticks, stages, body_units=2, head=None):
    stages = [(s + (None,))[:3] for s in stages]
    lag_max = max(lag for _, lag, _ in stages)
    if head is None:
        head = -(-(lag_max + 2 * ticks) // (ticks * body_units)) * body_units
    total = units * ticks

    def step(u0, t, base):
        for fn, lag, at in stages:
            k = t - lag
            if isinstance(u0, int) and not 0 <= u0 * ticks + k < total:
                continue
            du, g = k // ticks, k % ticks
            if at is None or g == at:
                u = u0 + du if du > 0 else (u0 - (-du) if du < 0 else u0)
                fn(u, (base + du) % 2, g)

    for u in range(head):
        for t in range(ticks):
            step(u, t, u)
    turns = (units - head) // body_units
    if turns > 0:
        with eng.Fori(head, head + (turns - 1) * body_units + 1, body_units) as u:
            for j in range(body_units):
                for t in range(ticks):
                    step(u, t + j * ticks, 0)
    done = head + turns * body_units
    for u in range(done, units + -(-lag_max // ticks)):
        for t in range(ticks):
            step(u, t, u)


def wait(eng, sem, value):
    if isinstance(value, int) and value <= 0:
        return
    eng.wait_ge(sem, value)


class Chain:

    def __init__(self, eng, sem, per_unit=0, unit=0):
        self.eng, self.sem, self.base, self.k = eng, sem, unit * per_unit, 0

    def __call__(self, ins, alone=None):
        self.k += 1
        ins.then_inc(self.sem, 1)
        if alone is not None:
            wait_alone(self.eng, alone, self.sem, self.base + self.k)
        else:
            self.eng.wait_ge(self.sem, self.base + self.k)


def row(t, u):
    if isinstance(u, int):
        return t[:, u, :]
    return t[:, bass.ds(u, 1), :].rearrange("p a b -> p (a b)")


def cols(t, u, n, first=0, count=None):
    count = n if count is None else count
    if isinstance(u, int):
        return t[:, u * n + first:u * n + first + count]
    return t[:, bass.ds(u * n + first, count)]


def bcast_last(ap, n):
    return ap.unsqueeze(2).broadcast_to([ap.shape[0], ap.shape[1], n])


def bcast_mid(ap, m):
    return ap.unsqueeze(1).broadcast_to([ap.shape[0], m, ap.shape[1]])


def wait_alone(dve, R, sem, value):
    wait(dve, sem, value)
    if not isinstance(value, int):
        dve.memset(R.carrier[:, :], 0.0)


class Memory:

    def __init__(self, nc, ctx, tag):
        self.nc, self.ctx, self.tag, self.sems = nc, ctx, tag, []

    def sb(self, name, *shape, dt=F32):
        return self.ctx.enter_context(self.nc.sbuf_tensor(f"{self.tag}_{name}", [P, *shape], dt))

    def sem(self, name):
        sem = self.ctx.enter_context(self.nc.semaphore(f"{self.tag}_{name}"))
        self.sems.append(sem)
        return sem

    def clear_semaphores(self):
        nums = sorted(sem.num for sem in self.sems)
        with self.nc.Block() as block:
            @block.gpsimd
            def _(pool):
                first = nums[0]
                for a, b in zip(nums, nums[1:] + [None]):
                    if b != a + 1:
                        pool.sem_clear(range(first, a + 1))
                        first = b


class NextNorm:

    def __init__(self, nc, m, R, bank, gamma_beta=None, sums=None):
        self.nc, self.R, self.tp, self.gb, self.sums = nc, R, bank, gamma_beta, sums
        self.rounds = 2 if gamma_beta is not None else 1
        self.stats = m.sb("ln_stats", 2, 6)
        self.mean_var = m.sb("ln_mean_var", 2, 2 * self.rounds)
        self.var = m.sb("ln_var", 2, self.rounds)
        self.rstd = m.sb("ln_rstd", 2, self.rounds)
        self.xn = m.sb("ln_xn", 2, D)
        self.chain = [m.sem(f"ln_chain{r}") for r in range(self.rounds)]
        self.var_ready = [m.sem(f"ln_var_ready{r}") for r in range(self.rounds)]
        self.rstd_ready = [m.sem(f"ln_rstd_ready{r}") for r in range(self.rounds)]
        self.xn1_ready = m.sem("ln_xn1_ready")
        self.xn_ready = m.sem("ln_xn_ready")
        self.transposed = m.sem("ln_transposed")
        self.stored = m.sem("ln_stored")

    def statistics(self, eng, u, d, r=0):
        nc = self.nc
        link = Chain(eng, self.chain[r], 2, u)
        if r:
            wait_alone(eng, self.R, self.xn1_ready, u + 1)
        src = self.xn[:, d, :] if r else row(self.R.X, u)
        link(nc.vector.bn_stats(self.stats[:, d, :], src), alone=self.R)
        link(nc.vector.bn_aggr(self.mean_var[:, d, 2 * r:2 * r + 2], self.stats[:, d, :]))
        nc.vector.tensor_scalar(self.var[:, d, r:r + 1], self.mean_var[:, d, 2 * r + 1:2 * r + 2], LN_EPS, None,
                                ALU.add).then_inc(self.var_ready[r], 1)

    def root(self, eng, u, d, r=0):
        eng.wait_ge(self.var_ready[r], u + 1)
        self.nc.gpsimd.tensor_tensor(self.rstd[:, d, r:r + 1], self.var[:, d, r:r + 1], self.R.minus_half[:, 0:1],
                                     ALU.pow).then_inc(self.rstd_ready[r], 1)

    def normalise(self, eng, u, d, r=0):
        last = r == self.rounds - 1
        if r == 0:
            wait(eng, self.transposed, u - 1)
        eng.wait_ge(self.rstd_ready[r], u + 1)
        src = self.xn[:, d, :] if r else row(self.R.X, u)
        self.nc.vector.tensor_scalar(self.xn[:, d, :], src, self.mean_var[:, d, 2 * r:2 * r + 1],
                                     self.rstd[:, d, r:r + 1], ALU.subtract, ALU.mult) \
            .then_inc(self.xn_ready if last else self.xn1_ready, 1)

    def transpose(self, eng, u, d):
        eng.wait_ge(self.xn_ready, u + 1)
        wait(eng, self.stored, u)
        self.nc.tensor.transpose(self.tp, self.xn[:, d, :], self.R.ident[:, :]).then_inc(self.transposed, 1)

    def store(self, eng, u, d):
        eng.wait_ge(self.transposed, u + 1)
        kw = {}
        if self.gb is not None:
            kw = dict(scale=self.gb[:, 0:1], bias=self.gb[:, 1:2])
        if self.sums is not None:
            kw = dict(accum_out=cols(self.sums, u, 1))
        self.nc.scalar.activation(row(self.R.XNT, u), self.tp, ACT.Identity, **kw).then_inc(self.stored, 1)


class Resident:
    pass


def phase_input(nc, R, A):
    with ExitStack() as ctx:
        m = Memory(nc, ctx, "in")
        norm = NextNorm(nc, m, R, R.bank[7][:, 128:256])
        x_in = m.sem("x_in")
        iota_p, made, copied = m.sem("iota_p"), m.sem("made"), m.sem("copied")
        with nc.Block() as block:
            @block.sync
            def _(sp):
                sp.dma_start(R.X[:, :, :], A["x"]).then_inc(x_in, 16)
                for name, (dst, src, sem) in R.loads.items():
                    sp.dma_start(dst, src).then_inc(sem, 16)

            @block.gpsimd
            def _(pool):
                link = Chain(pool, made)
                pool.wait_ge(R.constants, 1)
                link(nc.gpsimd.memset(R.ones[:, :], 1.0))
                link(nc.gpsimd.affine_select(out=R.ident[:, :], in_=R.ones[:, :], compare_op=ALU.is_equal, fill=0.0,
                                             base=0, pattern=[[1, P]], channel_multiplier=-1))
                link(nc.gpsimd.affine_select(out=R.upto[:, :], in_=R.ones[:, :], compare_op=ALU.is_ge, fill=0.0,
                                             base=0, pattern=[[1, P]], channel_multiplier=-1))
                link(nc.gpsimd.memset(R.future[:, :], 0.0))
                link(nc.gpsimd.affine_select(out=R.future[:, :], in_=R.future[:, :], compare_op=ALU.is_ge, fill=1e30,
                                             base=0, pattern=[[1, P]], channel_multiplier=-1))
                link(nc.gpsimd.memset(R.head_of4[:, :, :], 1.0))
                link(nc.gpsimd.affine_select(out=R.head_of4[:, :, :], in_=R.head_of4[:, :, :], compare_op=ALU.is_ge,
                                             fill=0.0, base=0, pattern=[[-32, 4], [0, P]], channel_multiplier=1))
                link(nc.gpsimd.affine_select(out=R.head_of4[:, :, :], in_=R.head_of4[:, :, :], compare_op=ALU.is_ge,
                                             fill=0.0, base=31, pattern=[[32, 4], [0, P]], channel_multiplier=-1))
                link(nc.gpsimd.memset(R.head_of_quad[:, :, :], 0.0))
                for g in range(4):
                    for j in range(4):
                        link(nc.gpsimd.affine_select(out=R.pick[:, :], in_=R.ones[:, :], compare_op=ALU.is_ge, fill=0.0,
                                                     base=-(32 * g + 8 * j), pattern=[[0, P]], channel_multiplier=1))
                        link(nc.gpsimd.affine_select(out=R.pick[:, :], in_=R.pick[:, :], compare_op=ALU.is_ge, fill=0.0,
                                                     base=32 * g + 8 * j + 7, pattern=[[0, P]], channel_multiplier=-1))
                        link(nc.gpsimd.tensor_tensor(R.head_of_quad[:, j, :], R.head_of_quad[:, j, :], R.pick[:, :],
                                                     ALU.add))
                run_ticks(pool, B, 1, [(lambda u, d, g: norm.root(pool, u, d), 1)])

            @block.vector
            def _(dve):
                nc.vector.memset(R.minus_half[:, :], -0.5).then_inc(R.constants, 1)
                dve.wait_ge(x_in, 16)
                run_ticks(dve, B, 1, [(lambda u, d, g: norm.statistics(dve, u, d), 0),
                                      (lambda u, d, g: norm.normalise(dve, u, d), 1)])

            @block.tensor
            def _(pe):
                pe.wait_ge(made, 2)
                run_ticks(pe, B, 1, [(lambda u, d, g: norm.transpose(pe, u, d), 1)])

            @block.scalar
            def _(act):
                nc.scalar.preload_act_table(ACT.Exp)
                run_ticks(act, B, 1, [(lambda u, d, g: norm.store(act, u, d), 1)])
        m.clear_semaphores()


def phase_l0_xattn(nc, R, A):
    NH, HD = 4, 32
    with ExitStack() as ctx:
        m = Memory(nc, ctx, "m0")
        scratch = nc.dram_tensor("running_max_rows", (B, NH * P), F32)
        gates = m.sb("gates", B, 2 * NH)
        ig, fg = m.sb("ig", B * NH), m.sb("fg", B * NH)
        t0, t1, logf = m.sb("t0", B * NH), m.sb("t1", B * NH), m.sb("logf", B * NH)
        csum, gpre = m.sb("csum", B * NH), m.sb("gpre", B * NH)
        gT, maxT = m.sb("gT", P), m.sb("maxT", P)
        floor_n = m.sb("floor_n", B * NH)
        ctxT_all = m.sb("ctxT_all", B, P)
        s_ctx = m.sem("ctx_all")
        s_gate, s_dve, s_act, s_pe, s_scr = m.sem("gate"), m.sem("dve"), m.sem("act"), m.sem("pe"), m.sem("scr")
        gp = R.bank[0][:, 0:B * 2 * NH]
        with nc.Block() as block:
            @block.sync
            def _(sp):
                sp.dma_start(ctxT_all[:, :, :], A["ctxT"]).then_inc(s_ctx, 16)
                sp.wait_ge(s_dve, 10)
                sp.dma_start(scratch.ap().rearrange("b (h t) -> (b h) t", h=NH), maxT[:, :]).then_inc(s_scr, 16)
                sp.wait_ge(s_scr, 16)

            @block.tensor
            def _(pe):
                R.arrived(pe, "gate_w")
                pe.wait_ge(s_ctx, 16)
                for b in range(B):
                    for c, lhs in enumerate((R.XNT, ctxT_all, ctxT_all)):
                        mm = nc.tensor.matmul(gp[:, b * 8:b * 8 + 8], lhs[:, b, :], R.gate_w[:, c, :],
                                              start=c == 0, stop=c == 2)
                mm.then_inc(s_gate, 1)
                pe.wait_ge(s_dve, 6)
                nc.tensor.matmul(R.bank[1][:, 0:P], R.upto[:, :], logf[:, :], start=True, stop=True).then_inc(s_pe, 1)
                pe.wait_ge(s_dve, 8)
                nc.tensor.transpose(R.bank[2][:, 0:P], gpre[:, :], R.ident[:, :]).then_inc(s_pe, 1)
                pe.wait_ge(s_dve, 10)
                nc.tensor.transpose(R.bank[3][:, 0:P], maxT[:, :], R.ident[:, :]).then_inc(s_pe, 1)

            @block.vector
            def _(dve):
                link = Chain(dve, s_dve)
                R.arrived(dve, "gate_b")
                dve.wait_ge(s_gate, 1)
                gv = gp.rearrange("p (b k) -> p b k", k=2 * NH)
                link(nc.vector.tensor_tensor(ig[:, :].rearrange("p (b h) -> p b h", h=NH), gv[:, :, 0:NH],
                                             bcast_mid(R.gate_b[:, 0:NH], B), ALU.add))
                link(nc.vector.tensor_tensor(fg[:, :].rearrange("p (b h) -> p b h", h=NH), gv[:, :, NH:],
                                             bcast_mid(R.gate_b[:, NH:], B), ALU.add))
                link(nc.vector.tensor_scalar(t0[:, :], fg[:, :], -1.0, None, ALU.mult))
                link(nc.vector.tensor_tensor(t0[:, :], t0[:, :], fg[:, :], ALU.min))
                link(nc.vector.tensor_scalar(fg[:, :], fg[:, :], 0.0, None, ALU.min))
                dve.wait_ge(s_act, 2)
                link(nc.vector.tensor_tensor(logf[:, :], fg[:, :], t1[:, :], ALU.subtract))
                dve.wait_ge(s_pe, 1)
                link(nc.vector.tensor_copy(csum[:, :], R.bank[1][:, 0:P]))
                link(nc.vector.tensor_tensor(gpre[:, :], ig[:, :], csum[:, :], ALU.subtract))
                dve.wait_ge(s_pe, 2)
                link(nc.vector.tensor_copy(gT[:, :], R.bank[2][:, 0:P]))
                link(nc.vector.tensor_tensor_scan(maxT[:, :], gT[:, :], gT[:, :], -3.0e38, ALU.max, ALU.max))
                dve.wait_ge(s_pe, 3)
                nc.vector.tensor_tensor(t0[:, :], R.bank[3][:, 0:P], csum[:, :], ALU.add).then_inc(s_dve, 1)

            @block.scalar
            def _(act):
                act.wait_ge(s_dve, 4)
                nc.scalar.activation(t1[:, :], t0[:, :], ACT.Exp).then_inc(s_act, 1)
                act.wait_ge(s_act, 1)
                nc.scalar.activation(t1[:, :], t1[:, :], ACT.Ln, bias=1.0).then_inc(s_act, 1)
                act.wait_ge(s_dve, 11)
                nc.scalar.activation(floor_n[:, :], t0[:, :], ACT.Exp, scale=-1.0).then_inc(s_act, 1)

        norm = NextNorm(nc, m, R, R.bank[7][:, 128:256], sums=R.token_sums)
        ct, cn, mb = m.sb("ct", 2, P), m.sb("cn", 2, D), m.sb("mb", 2, NH * P)
        mbm, dT, qm, cT = (m.sb(n, 2, NH * P) for n in ("mbm", "dT", "qm", "cT"))
        vaug = m.sb("vaug", 2, NH, HD + 1)
        den, sq, hn, ss, vv, rr = (m.sb("den", 2, NH), m.sb("sq", 2, D), m.sb("hn", 2, D), m.sb("ss", 2, NH),
                                   m.sb("vv", 2, NH), m.sb("rr", 2, NH))
        s_in = [m.sem("in0"), m.sem("in1")]
        s_ones, s_v, s_mbm, s_dT, s_qm, s_sc, s_cT, s_hp, s_hn, s_vv, s_rr, s_l0, s_l1, s_res, s_rms = (
            m.sem(n) for n in ("ones", "v", "mbm", "dT", "qm", "sc", "cT", "hp", "hn", "vv", "rr", "l0", "l1",
                               "res", "rms"))
        INV = 1.0 / float(32) ** 0.5
        with nc.Block() as block:
            @block.sync
            def _(sp):
                def load(u, d, g):
                    wait(sp, s_sc, u - 1)
                    wait(sp, s_v, u - 1)
                    wait(sp, s_mbm, u - 1)
                    sp.dma_start(ct[:, d, :], row(A["ctxT"], u)).then_inc(s_in[d], 16)
                    sp.dma_start(cn[:, d, :], row(A["ctx"], u)).then_inc(s_in[d], 16)
                    src = scratch.ap()[u, :] if isinstance(u, int) else \
                        scratch.ap()[bass.ds(u, 1), :].rearrange("a n -> (a n)")
                    sp.dma_start(mb[:, d, :], src.partition_broadcast(P)).then_inc(s_in[d], 16)
                run_ticks(sp, B, 1, [(load, 0)])

            def inputs(eng, u, d):
                n = (u // 2 + 1) * 48 if isinstance(u, int) else u * 24 + (48 - 24 * d)
                eng.wait_ge(s_in[d], n)

            @block.gpsimd
            def _(pool):
                nc.gpsimd.memset(vaug[:, :, :, :], 1.0).then_inc(s_ones, 1)
                pool.wait_ge(s_ones, 1)

                def prepare(u, d, g):
                    inputs(pool, u, d)
                    wait(pool, s_hp, u - 1)
                    nc.gpsimd.tensor_tensor(vaug[:, d, :, 0:HD], cn[:, d, :].rearrange("p (h e) -> p h e", h=NH),
                                            R.ones[:, :].rearrange("p (h e) -> p h e", h=NH), ALU.mult) \
                        .then_inc(s_v, 1)
                    wait(pool, s_dT, u - 1)
                    nc.gpsimd.tensor_tensor(mbm[:, d, :].rearrange("p (h t) -> p h t", h=NH),
                                            mb[:, d, :].rearrange("p (h t) -> p h t", h=NH),
                                            bcast_mid(R.future[:, :], NH), ALU.add).then_inc(s_mbm, 1)

                def root(u, d, g):
                    pool.wait_ge(s_vv, u + 1)
                    nc.gpsimd.tensor_tensor(rr[:, d, :], vv[:, d, :], R.minus_half[:, 0:NH], ALU.pow) \
                        .then_inc(s_rr, 1)

                run_ticks(pool, B, 1, [(root, 2), (lambda u, d, g: norm.root(pool, u, d), 3), (prepare, 0)])

            @block.vector
            def _(dve):
                def mask_q(u, d, g):
                    wait(dve, s_sc, u - 1)
                    nc.vector.tensor_tensor(qm[:, d, :].rearrange("p (h t) -> p h t", h=NH),
                                            bcast_mid(row(R.XNT, u), NH), R.head_of4[:, :, :], ALU.mult) \
                        .then_inc(s_qm, 1)

                def weigh(u, d, g):
                    dve.wait_ge(s_sc, u + 1)
                    dve.wait_ge(s_dT, u + 1)
                    wait(dve, s_hp, u - 1)
                    nc.vector.scalar_tensor_tensor(out=cT[:, d, :], in0=R.bank[d][:, 0:NH * P], scalar=INV,
                                                   in1=dT[:, d, :], op0=ALU.mult, op1=ALU.mult).then_inc(s_cT, 1)

                def heads(u, d, g):
                    dve.wait_ge(s_hp, u + 1)
                    hp = R.bank[2 + d][:, 0:NH * (HD + 1)].rearrange("p (h e) -> p h e", h=NH)
                    link = Chain(dve, s_l0, 5, u)
                    link(nc.vector.tensor_tensor(den[:, d, :].unsqueeze(2), hp[:, :, HD:HD + 1],
                                                 cols(floor_n, u, NH).unsqueeze(2), ALU.max))
                    link(nc.vector.tensor_scalar(den[:, d, :], den[:, d, :], 1e-6, None, ALU.add))
                    link(nc.vector.reciprocal(den[:, d, :], den[:, d, :]))
                    hv = hn[:, d, :].rearrange("p (h e) -> p h e", h=NH)
                    nc.vector.tensor_tensor(hv, hp[:, :, 0:HD], bcast_last(den[:, d, :], HD), ALU.mult) \
                        .then_inc(s_hn, 1)
                    dve.wait_ge(s_hn, u + 1)
                    link(nc.vector.tensor_tensor(sq[:, d, :], hn[:, d, :], hn[:, d, :], ALU.mult))
                    link(nc.vector.tensor_reduce(ss[:, d, :], sq[:, d, :].rearrange("p (h e) -> p h e", h=NH),
                                                 AX.X, ALU.add))
                    nc.vector.tensor_scalar(vv[:, d, :], ss[:, d, :], 1.0 / HD, 1e-6, ALU.mult, ALU.add) \
                        .then_inc(s_vv, 1)

                def residual(u, d, g):
                    dve.wait_ge(s_rr, u + 1)
                    link = Chain(dve, s_l1, 3, u)
                    hv = hn[:, d, :].rearrange("p (h e) -> p h e", h=NH)
                    link(nc.vector.tensor_tensor(hv, hv, bcast_last(rr[:, d, :], HD), ALU.mult))
                    link(nc.vector.tensor_tensor(hv, hv, bcast_mid(R.rms[:, 0:HD], NH), ALU.mult))
                    link(nc.vector.tensor_tensor(row(R.X, u), row(R.X, u), hn[:, d, :], ALU.add), alone=R)
                    norm.statistics(dve, u, d)

                R.arrived(dve, "rms")
                nc.vector.tensor_scalar(R.rms[:, :], R.rms[:, :], 1.0, None, ALU.add).then_inc(s_rms, 1)
                dve.wait_ge(s_rms, 1)
                run_ticks(dve, B, 1, [(mask_q, 0), (heads, 2), (weigh, 1), (residual, 3),
                                      (lambda u, d, g: norm.normalise(dve, u, d), 4)])

            @block.tensor
            def _(pe):
                def scores(u, d, g):
                    inputs(pe, u, d)
                    pe.wait_ge(s_qm, u + 1)
                    wait(pe, s_cT, u - 1)
                    nc.tensor.matmul(R.bank[d][:, 0:NH * P], ct[:, d, :], qm[:, d, :], start=True, stop=True) \
                        .then_inc(s_sc, 1)

                def values(u, d, g):
                    pe.wait_ge(s_cT, u + 1)
                    pe.wait_ge(s_v, u + 1)
                    wait(pe, s_hn, u - 1)
                    for h in range(NH):
                        mm = nc.tensor.matmul(R.bank[2 + d][:, h * (HD + 1):(h + 1) * (HD + 1)],
                                              cT[:, d, h * P:(h + 1) * P], vaug[:, d, h, :], start=True, stop=True)
                    mm.then_inc(s_hp, 1)

                run_ticks(pe, B, 1, [(scores, 0), (values, 1), (lambda u, d, g: norm.transpose(pe, u, d), 5)])

            @block.scalar
            def _(act):
                nc.scalar.preload_act_table(ACT.Exp)

                def decay(u, d, g):
                    act.wait_ge(s_mbm, u + 1)
                    wait(act, s_cT, u - 1)
                    for h in range(NH):
                        ins = nc.scalar.activation(dT[:, d, h * P:(h + 1) * P], mbm[:, d, h * P:(h + 1) * P], ACT.Exp,
                                                   scale=-1.0, bias=cols(gpre, u, NH, h, 1))
                    ins.then_inc(s_dT, 1)

                run_ticks(act, B, 1, [(decay, 0), (lambda u, d, g: norm.store(act, u, d), 5)])
        m.clear_semaphores()


def phase_l0_ffn(nc, R, A):
    BITS = 6
    with ExitStack() as ctx:
        m = Memory(nc, ctx, "f0")
        power = m.sb("power", BITS)
        proj, bit, size, weakest, run = (m.sb(n, BITS) for n in ("proj", "bit", "size", "weakest", "run"))
        least, code = m.sb("least", 1), m.sb("code", 2)
        expert = m.sb("expert", 2 * B, dt=I32)
        s_pow, s_pe, s_dve, s_code = m.sem("pow"), m.sem("pe"), m.sem("dve"), m.sem("code")
        rows = slice(0, B)
        with nc.Block() as block:
            @block.gpsimd
            def _(pool):
                for k in range(BITS):
                    nc.gpsimd.memset(power[rows, k:k + 1], float(2 ** k)).then_inc(s_pow, 1)

            @block.tensor
            def _(pe):
                R.arrived(pe, "hyper")
                nc.tensor.matmul(R.bank[0][rows, 0:BITS], R.token_sums[:, :], R.hyper[:, :], start=True, stop=True) \
                    .then_inc(s_pe, 1)
                pe.wait_ge(s_code, 1)
                for k in range(2):
                    mm = nc.tensor.transpose(R.bank[1][0:1, k * B:(k + 1) * B], code[rows, k:k + 1],
                                             R.ident[rows, rows])
                mm.then_inc(s_pe, 1)

            @block.vector
            def _(dve):
                link = Chain(dve, s_dve)
                V = nc.vector
                dve.wait_ge(s_pe, 1)
                link(V.tensor_scalar(proj[rows, :], R.bank[0][rows, 0:BITS], 1.0 / P, None, ALU.mult))
                link(V.tensor_scalar(bit[rows, :], proj[rows, :], 0.0, None, ALU.is_gt))
                link(V.tensor_scalar(size[rows, :], proj[rows, :], -1.0, None, ALU.mult))
                link(V.tensor_tensor(size[rows, :], size[rows, :], proj[rows, :], ALU.max))
                link(V.tensor_reduce(least[rows, :], size[rows, :], AX.X, ALU.min))
                link(V.tensor_scalar(weakest[rows, :], size[rows, :], least[rows, 0:1], None, ALU.is_equal))
                link(V.tensor_tensor_scan(run[rows, :], weakest[rows, :], weakest[rows, :], 0.0, ALU.add, ALU.bypass))
                link(V.tensor_scalar(run[rows, :], run[rows, :], 1.0, None, ALU.is_equal))
                link(V.tensor_tensor(weakest[rows, :], weakest[rows, :], run[rows, :], ALU.mult))
                dve.wait_ge(s_pow, BITS)
                link(V.tensor_scalar(run[rows, :], bit[rows, :], -2.0, 1.0, ALU.mult, ALU.add))
                link(V.tensor_tensor(run[rows, :], run[rows, :], weakest[rows, :], ALU.mult))
                link(V.tensor_tensor(run[rows, :], run[rows, :], bit[rows, :], ALU.add))
                link(V.tensor_tensor(run[rows, :], run[rows, :], power[rows, :], ALU.mult))
                link(V.tensor_tensor(bit[rows, :], bit[rows, :], power[rows, :], ALU.mult))
                link(V.tensor_reduce(code[rows, 0:1], bit[rows, :], AX.X, ALU.add))
                V.tensor_reduce(code[rows, 1:2], run[rows, :], AX.X, ALU.add).then_inc(s_code, 1)
                dve.wait_ge(s_pe, 2)
                V.tensor_copy(expert[0:1, :], R.bank[1][0:1, 0:2 * B])

        norm = NextNorm(nc, m, R, R.bank[7][:, 128:256], gamma_beta=R.l1_gb)
        xs, w = m.sb("xs", 2, P), m.sb("w", 2, 2, D)
        s_w = [m.sem("w0"), m.sem("w1")]
        s_xs, s_y, s_x = m.sem("xs"), m.sem("y"), m.sem("x")
        with nc.Block() as block:
            @block.sync
            def _(sp):
                def load(u, d, g):
                    wait(sp, s_y, u - 1)
                    for k in range(2):
                        at = expert[0:1, k * B + u:k * B + u + 1] if isinstance(u, int) else \
                            expert[0:1, bass.ds(u + k * B, 1)]
                        e = sp.value_load(at, min_val=0, max_val=63)
                        sp.dma_start(w[:, d, k, :], A["experts"][bass.ds(e, 1), :, :].rearrange("a p n -> p (a n)")) \
                            .then_inc(s_w[d], 16)
                run_ticks(sp, B, 1, [(load, 0)])

            @block.gpsimd
            def _(pool):
                run_ticks(pool, B, 1, [(lambda u, d, g: norm.root(pool, u, d), 1),
                                       (lambda u, d, g: norm.root(pool, u, d, 1), 2)])

            @block.vector
            def _(dve):
                def copy_x(u, d, g):
                    wait(dve, s_y, u - 1)
                    nc.vector.tensor_scalar(xs[:, d, :], row(R.XNT, u), 1.0, None, ALU.mult).then_inc(s_xs, 1)

                def residual(u, d, g):
                    dve.wait_ge(s_y, u + 1)
                    link = Chain(dve, s_x, 1, u)
                    link(nc.vector.scalar_tensor_tensor(out=row(R.X, u), in0=R.bank[d][:, 0:D], scalar=0.5,
                                                        in1=row(R.X, u), op0=ALU.mult, op1=ALU.add), alone=R)
                    norm.statistics(dve, u, d)

                def again(u, d, g):
                    norm.normalise(dve, u, d)
                    norm.statistics(dve, u, d, 1)

                run_ticks(dve, B, 1, [(copy_x, 0), (residual, 1), (again, 2),
                                      (lambda u, d, g: norm.normalise(dve, u, d, 1), 3)])

            @block.tensor
            def _(pe):
                def product(u, d, g):
                    pe.wait_ge(s_xs, u + 1)
                    n = (u // 2 + 1) * 32 if isinstance(u, int) else u * 16 + (32 - 16 * d)
                    pe.wait_ge(s_w[d], n)
                    wait(pe, s_x, u - 1)
                    for k in range(2):
                        mm = nc.tensor.matmul(R.bank[d][:, 0:D], xs[:, d, :], w[:, d, k, :], start=k == 0, stop=k == 1)
                    mm.then_inc(s_y, 1)

                run_ticks(pe, B, 1, [(product, 0), (lambda u, d, g: norm.transpose(pe, u, d), 3)])

            @block.scalar
            def _(act):
                R.arrived(act, "l1_gb")
                run_ticks(act, B, 1, [(lambda u, d, g: norm.store(act, u, d), 3)])
        m.clear_semaphores()


def phase_attention(nc, R, A, kind):
    wide = kind == 1
    HD = 64 if wide else 8
    NH, NQ, HQ = 16, 4, 4
    scale = 64 ** -0.5 if wide else (8 ** -0.5 if kind == 2 else float(8) ** 0.5)
    S = 8 if kind == 3 else 4
    PV_PER_O = 1 if wide else 4
    PARTS = 2 if wide else 1
    Y = S + 5 + PARTS
    W = R.w[f"l{kind}"]
    with ExitStack() as ctx:
        m = Memory(nc, ctx, f"a{kind}")
        norm = NextNorm(nc, m, R, R.bank[7][:, 128:256])
        C = NH * HD // P
        ct = m.sb("ct", 2, P)
        qT = m.sb("qT", 2, C, P)
        kT = m.sb("kT", 2, C, P) if wide else m.sb("k_masked", 2, HQ, P)
        OH = HD + 1
        WIDE_ROW = OH if wide else NH * OH
        OWN = OH if wide else WIDE_ROW + OH
        vals = m.sb("vals", 2, NH * OWN)

        def own(d, h0=0, h1=NH, e0=0, e1=HD):
            return vals[:, d, h0 * OWN:h1 * OWN].rearrange("p (h e) -> p h e", e=OWN)[:, :, e0:e1]

        neg_max = m.sb("neg_max", 2, HQ)
        scaled_q = m.sb("scaled_q", 2)
        prob, probT = m.sb("prob", 2, HQ * P), m.sb("probT", 2, HQ * P)
        rden = m.sb("rden", 2, NH)
        heads, headsT = m.sb("heads", 2, NH * HD), m.sb("headsT", NH * HD)
        t_res = m.sb("t_res", 2, D)
        names = ("zeros ones q k v qe ke ve scores maxed exped ptr ptc pv o_link o oT oTc y res_link bias "
                 "xs qkn qk_link qk_var qk_rstd qkd qkT gate").split()
        s = {n: m.sem(n) for n in names}
        s_ct = [m.sem("ct0"), m.sem("ct1")]
        if kind == 3:
            xs = m.sb("xs", 2, P)
            cen, sq = m.sb("cen", 2, 2 * D), m.sb("sq", 2, 2 * D)
            qk_sum, qk_var, qk_rstd = m.sb("qk_sum", 2, 32), m.sb("qk_var", 2, 32), m.sb("qk_rstd", 2, 32)
            gb_head = m.sb("gb_head", 2, HQ)

        def pair_count(u, d, n):
            return (u // 2 + 1) * n if isinstance(u, int) else u * (n // 2) + (n - n // 2 * d)

        def quad(u, g):
            return u * NQ + g

        def head_no(g, i):
            return 2 * (4 * (g // 2) + i) + g % 2 if wide else 4 * g + i

        with nc.Block() as block:
            @block.sync
            def _(sp):
                def load(u, d, g):
                    wait(sp, s["k"] if wide else s["v"], 3 * u - 3 if wide else u - 1)
                    sp.dma_start(ct[:, d, :], row(A["ctxT"], u)).then_inc(s_ct[d], 16)
                run_ticks(sp, B, 1, [(load, 0)])

            @block.gpsimd
            def _(pool):
                nc.gpsimd.memset(vals[:, :, :], 0.0).then_inc(s["zeros"], 1)
                pool.wait_ge(s["zeros"], 1)
                for d in range(2):
                    nc.gpsimd.memset(own(d, e0=HD, e1=OH), 1.0).then_inc(s["ones"], 1)

                def qk_root(u, d, g):
                    pool.wait_ge(s["qk_var"], u + 1)
                    nc.gpsimd.tensor_tensor(qk_rstd[:, d, :], qk_var[:, d, :], R.minus_half[:, 0:32], ALU.pow) \
                        .then_inc(s["qk_rstd"], 1)

                st = [(lambda u, d, g: norm.root(pool, u, d), Y, 3)]
                if kind == 3:
                    st += [(qk_root, 2, 0)]
                run_ticks(pool, B, NQ, st)

            @block.vector
            def _(dve):
                V = nc.vector

                def evac_wide(part):
                    def fn(u, d, g):
                        dve.wait_ge(s["k"], 3 * u + part + 1)
                        if part < 2:
                            wait(dve, s["scores"], 4 * u - 4)
                            dst = (qT, kT)[part][:, d, 4:8, :].rearrange("p c t -> p (c t)")
                            src = R.bank[1][:, :]
                        else:
                            wait(dve, s["pv"], 4 * u - 4)
                            dst = own(d, 8, 16)
                            src = R.bank[1][:, :].rearrange("p (h e) -> p h e", e=HD)
                        if part == 0:
                            V.tensor_scalar(dst, src, scale, None, ALU.mult).then_inc(s["ke"], 1)
                        else:
                            V.tensor_copy(dst, src).then_inc(s["ke"], 1)
                    return fn

                def mask_k(u, d, g):
                    dve.wait_ge(s["k"], u + 1)
                    wait(dve, s["scores"], 4 * u - 4)
                    V.scalar_tensor_tensor(out=kT[:, d, :, :], in0=bcast_mid(R.bank[1][:, 0:P], HQ),
                                           scalar=W["bqk"][:, 1:2], in1=R.head_of_quad[:, :, :], op0=ALU.add,
                                           op1=ALU.mult).then_inc(s["ke"], 1)

                def evac_v(u, d, g):
                    dve.wait_ge(s["v"], u + 1)
                    wait(dve, s["pv"], 4 * u - 4)
                    src = R.bank[1 if kind == 2 else 0][:, 256:384].rearrange("p (h e) -> p h e", e=HD)
                    if kind == 2:
                        V.tensor_tensor(own(d), src, W["bv"][:, :].rearrange("p (h e) -> p h e", e=HD),
                                        ALU.add).then_inc(s["ve"], 1)
                    else:
                        V.tensor_copy(own(d), src).then_inc(s["ve"], 1)

                def copy_x(u, d, g):
                    wait(dve, s["q"], u - 1)
                    V.tensor_scalar(xs[:, d, :], row(R.XNT, u), 1.0, None, ALU.mult).then_inc(s["xs"], 1)

                def qk_stats(u, d, g):
                    dve.wait_ge(s["q"], u + 1)
                    wait(dve, s["qkT"], u - 1)
                    link = Chain(dve, s["qk_link"], 5, u)
                    qk = R.bank[1][:, 0:2 * D].rearrange("p (n e) -> p n e", e=HD)
                    c3, s3 = (t[:, d, :].rearrange("p (n e) -> p n e", e=HD) for t in (cen, sq))
                    link(V.tensor_reduce(qk_sum[:, d, :], qk, AX.X, ALU.add))
                    link(V.tensor_scalar(qk_sum[:, d, :], qk_sum[:, d, :], 1.0 / HD, None, ALU.mult))
                    link(V.tensor_tensor(c3, qk, bcast_last(qk_sum[:, d, :], HD), ALU.subtract))
                    link(V.tensor_tensor(s3, c3, c3, ALU.mult))
                    link(V.tensor_reduce(qk_var[:, d, :], s3, AX.X, ALU.add))
                    V.tensor_scalar(qk_var[:, d, :], qk_var[:, d, :], 1.0 / HD, LN_EPS, ALU.mult, ALU.add) \
                        .then_inc(s["qk_var"], 1)

                def qk_norm(u, d, g):
                    dve.wait_ge(s["qk_rstd"], u + 1)
                    c3 = cen[:, d, :].rearrange("p (n e) -> p n e", e=HD)
                    V.tensor_tensor(c3, c3, bcast_last(qk_rstd[:, d, :], HD), ALU.mult).then_inc(s["qkn"], 1)

                def row_max(u, d, g):
                    k, b = quad(u, g), g % 2
                    dve.wait_ge(s["scores"], k + 1)
                    wait(dve, s["exped"], k - 1)
                    sc = R.bank[2 + b][:, :].rearrange("p (h t) -> p h t", h=HQ)
                    V.tensor_reduce(neg_max[:, b, :], sc, AX.X, ALU.max, negate=True).then_inc(s["maxed"], 1)

                def normalise_heads(u, d, g):
                    k = quad(u, g)
                    n = u * (NQ // PV_PER_O) + (g if wide else 0)
                    dve.wait_ge(s["pv"], k + 1)
                    if g == 0 or not wide:
                        wait(dve, s["oT"], PARTS * (u - 1))
                    link = Chain(dve, s["o_link"], 1, n)
                    hs = HQ if wide else NH
                    o = R.bank[6][:, 0:hs * (HD + 1)].rearrange("p (h e) -> p h e", e=HD + 1)
                    r = rden[:, d, 4 * g:4 * g + 4] if wide else rden[:, d, :]
                    link(V.reciprocal(r.unsqueeze(2), o[:, :, HD:HD + 1]))
                    if wide:
                        dst = heads[:, d, :].rearrange("p (c two e) -> p c two e", two=2, e=HD)[
                            :, 4 * (g // 2):4 * (g // 2) + 4, g % 2, :]
                    else:
                        dst = heads[:, d, :].rearrange("p (h e) -> p h e", e=HD)
                    V.tensor_tensor(dst, o[:, :, 0:HD], bcast_last(r, HD), ALU.mult).then_inc(s["o"], 1)

                def residual(u, d, g):
                    dve.wait_ge(s["y"], u + 1)
                    link = Chain(dve, s["res_link"], 2, u)
                    y = R.bank[7][:, 0:D]
                    if wide:
                        link(V.scalar_tensor_tensor(out=t_res[:, d, :], in0=y, scalar=W["gate"][:, 0:1],
                                                    in1=W["bo"][:, :], op0=ALU.mult, op1=ALU.add))
                    else:
                        link(V.tensor_tensor(t_res[:, d, :], y, W["bo"][:, :], ALU.add))
                    link(V.tensor_tensor(row(R.X, u), row(R.X, u), t_res[:, d, :], ALU.add), alone=R)
                    norm.statistics(dve, u, d)

                R.arrived(dve, f"l{kind}_bo")
                if wide:
                    dve.wait_ge(s["gate"], 1)
                    V.tensor_scalar(W["bo"][:, :], W["bo"][:, :], W["gate"][:, 0:1], None, ALU.mult) \
                        .then_inc(s["bias"], 1)
                    dve.wait_ge(s["bias"], 1)
                    st = [(evac_wide(0), 0, 0), (evac_wide(1), 0, 1), (evac_wide(2), 0, 3)]
                elif kind == 2:
                    R.arrived(dve, "l2_bqk")
                    V.tensor_scalar(scaled_q[:, 0:1], W["bqk"][:, 0:1], scale, None, ALU.mult).then_inc(s["bias"], 1)
                    R.arrived(dve, "l2_bv")
                    st = [(mask_k, 0, 0), (evac_v, 0, 3)]
                else:
                    R.arrived(dve, "l3_gb")
                    V.tensor_scalar(scaled_q[:, :], W["gb"][:, :], scale, None, ALU.mult).then_inc(s["bias"], 1)
                    for i in range(2):
                        V.tensor_scalar(gb_head[:, i, :], R.head_of_quad[:, :, 0:1].rearrange("p h t -> p (h t)"),
                                        W["gb"][:, i:i + 1], None, ALU.mult).then_inc(s["bias"], 1)
                    st = [(copy_x, 0, 0), (qk_stats, 2, 0), (qk_norm, 5, 0)]
                dve.wait_ge(s["ones"], 2)
                st = [(lambda u, d, g: norm.normalise(dve, u, d), Y + 1, 3), (row_max, S)] + st
                st += [(normalise_heads, S + 3) + (() if wide else (3,)), (residual, Y, 3)]
                st += [(evac_v, 4, 3)] if kind == 3 else []
                run_ticks(dve, B, NQ, st)

            @block.tensor
            def _(pe):
                T = nc.tensor

                def context_here(u, d):
                    pe.wait_ge(s_ct[d], pair_count(u, d, 16))

                def project_wide(part):
                    def fn(u, d, g):
                        if part == 0:
                            context_here(u, d)
                        for half, (free, done) in enumerate((("qe", "q"), ("ke", "k"))):
                            wait(pe, s[free], 3 * u + part)
                            bank = R.bank[half]
                            if part == 2:
                                mm = T.matmul(bank[:, :], ct[:, d, :], W["kv"][:, 1024 + 512 * half:1536 + 512 * half],
                                              start=True, stop=True)
                            else:
                                w = W["q"] if part == 0 else W["kv"]
                                rhs = row(R.XNT, u) if part == 0 else ct[:, d, :]
                                for i in range(4):
                                    c = 4 * half + i
                                    mm = T.matmul(bank[:, i * P:(i + 1) * P], w[:, c * P:(c + 1) * P], rhs,
                                                  start=True, stop=True)
                            mm.then_inc(s[done], 1)
                    return fn

                def project_q(u, d, g):
                    wait(pe, s["qe"], u)
                    T.matmul(R.bank[0][:, 0:P], W["q"][:, :], row(R.XNT, u), start=True, stop=True).then_inc(s["q"], 1)

                def project_k(u, d, g):
                    context_here(u, d)
                    wait(pe, s["ve"], u)
                    T.matmul(R.bank[1][:, 0:P], W["kv"][:, 0:P], ct[:, d, :], start=True, stop=True) \
                        .then_inc(s["k"], 1)

                def project_v(u, d, g):
                    if kind == 2:
                        pe.wait_ge(s["ke"], u + 1)
                        bank = R.bank[1]
                    else:
                        pe.wait_ge(s["ke"], u + 1)
                        bank = R.bank[0]
                    T.matmul(bank[:, 256:384], ct[:, d, :], W["kv"][:, P:2 * P], start=True, stop=True) \
                        .then_inc(s["v"], 1)

                def project_qk(u, d, g):
                    context_here(u, d)
                    pe.wait_ge(s["xs"], u + 1)
                    wait(pe, s["qk_var"], u)
                    T.matmul(R.bank[1][:, 0:P], xs[:, d, :], W["q"][:, :], start=True, stop=True)
                    T.matmul(R.bank[1][:, P:2 * P], ct[:, d, :], W["kv"][:, 0:P], start=True, stop=True) \
                        .then_inc(s["q"], 1)

                def turn_qk(u, d, g):
                    pe.wait_ge(s["qkn"], u + 1)
                    wait(pe, s["ve"], u)
                    for i in range(2):
                        mm = T.transpose(R.bank[0][:, i * P:(i + 1) * P], cen[:, d, i * P:(i + 1) * P], R.ident[:, :])
                    mm.then_inc(s["qkT"], 1)

                def scores(u, d, g):
                    k, b = quad(u, g), g % 2
                    if g == 0:
                        pe.wait_ge(s["qe"], 3 * u + 2 if wide else u + 1)
                        pe.wait_ge(s["ke"], 3 * u + 2 if wide else u + 1)
                    wait(pe, s["exped"], k - 1)
                    if wide:
                        for i in range(HQ):
                            c, r = 4 * (g // 2) + i, slice(HD * (g % 2), HD * (g % 2) + HD)
                            mm = T.matmul(R.bank[2 + b][:, i * P:(i + 1) * P], qT[r, d, c, :], kT[r, d, c, :],
                                          start=True, stop=True)
                    else:
                        r = slice(32 * g, 32 * g + 32)
                        mm = T.matmul(R.bank[2 + b][:, :], qT[r, d, 0, :],
                                      kT[r, d, :, :].rearrange("p h t -> p (h t)"), start=True, stop=True)
                    mm.then_inc(s["scores"], 1)

                def turn_prob(u, d, g):
                    k, b = quad(u, g), g % 2
                    pe.wait_ge(s["exped"], k + 1)
                    wait(pe, s["ptc"], k - 1)
                    for i in range(HQ):
                        mm = T.transpose(R.bank[4 + b][:, i * P:(i + 1) * P], prob[:, b, i * P:(i + 1) * P],
                                         R.ident[:, :])
                    mm.then_inc(s["ptr"], 1)

                def values(u, d, g):
                    k, b = quad(u, g), g % 2
                    pe.wait_ge(s["ptc"], k + 1)
                    if wide:
                        pe.wait_ge(s["qe"], 3 * u + 3)
                        pe.wait_ge(s["ke"], 3 * u + 3)
                        wait(pe, s["o"], k)
                    elif g == 0:
                        pe.wait_ge(s["ve"], u + 1)
                        wait(pe, s["o"], u)
                    for i in range(HQ):
                        h = head_no(g, i)
                        out = R.bank[6][:, i * OH:(i + 1) * OH] if wide else R.bank[6][:, 0:WIDE_ROW]
                        own_at = h * (OWN if wide else WIDE_ROW)
                        mm = T.matmul(out, probT[:, b, i * P:(i + 1) * P], vals[:, d, own_at:own_at + WIDE_ROW],
                                      start=wide or h == 0, stop=wide or h == NH - 1)
                    mm.then_inc(s["pv"], 1)

                def turn_heads(part):
                    def fn(u, d, g):
                        if part == 0:
                            pe.wait_ge(s["o"], (u + 1) * (NQ // PV_PER_O))
                            wait(pe, norm.stored, u)
                        else:
                            pe.wait_ge(s["oTc"], PARTS * u + part)
                        n = min(4, C)
                        for i in range(n):
                            c = 4 * part + i
                            mm = T.transpose(R.bank[7][:, i * P:(i + 1) * P], heads[:, d, c * P:(c + 1) * P],
                                             R.ident[:, :])
                        mm.then_inc(s["oT"], 1)
                    return fn

                def project_out(u, d, g):
                    pe.wait_ge(s["oTc"], PARTS * (u + 1))
                    for c in range(C):
                        mm = T.matmul(R.bank[7][:, 0:D], headsT[:, c * P:(c + 1) * P], W["o"][:, c * D:(c + 1) * D],
                                      start=c == 0, stop=c == C - 1)
                    mm.then_inc(s["y"], 1)

                for name in W["loaded"]:
                    R.arrived(pe, f"l{kind}_{name}")
                pe.wait_ge(s["ones"], 2)
                if wide:
                    st = [(project_wide(0), 0, 0), (project_wide(1), 0, 1), (project_wide(2), 0, 3)]
                elif kind == 2:
                    st = [(project_q, 0, 0), (project_k, 0, 0), (project_v, 0, 3)]
                else:
                    st = [(project_qk, 1, 0), (turn_qk, 6, 0)]
                st = [(scores, S)] + st + [(turn_prob, S + 2), (project_out, Y, 3)]
                st += [(turn_heads(p), S + 5 + p, 3) for p in range(PARTS)]
                st += [(values, S + 3)] + ([(project_v, 4, 3)] if kind == 3 else []) + [(lambda u, d, g: norm.transpose(pe, u, d), Y + 1, 3)]
                run_ticks(pe, B, NQ, st)

            @block.scalar
            def _(act):
                def evac_wide(part):
                    def fn(u, d, g):
                        act.wait_ge(s["q"], 3 * u + part + 1)
                        if part < 2:
                            wait(act, s["scores"], 4 * u - 4)
                            dst = (qT, kT)[part][:, d, 0:4, :].rearrange("p c t -> p (c t)")
                            src = R.bank[0][:, :]
                        else:
                            wait(act, s["pv"], 4 * u - 4)
                            dst = own(d, 0, 8)
                            src = R.bank[0][:, :].rearrange("p (h e) -> p h e", e=HD)
                        nc.scalar.activation(dst, src, ACT.Identity, scale=scale if part == 0 else 1.0) \
                            .then_inc(s["qe"], 1)
                    return fn

                def evac_q(u, d, g):
                    act.wait_ge(s["q"], u + 1)
                    wait(act, s["scores"], 4 * u - 4)
                    nc.scalar.activation(qT[:, d, 0, :], R.bank[0][:, 0:P], ACT.Identity, scale=scale,
                                         bias=scaled_q[:, 0:1]) \
                        .then_inc(s["qe"], 1)

                def evac_qk(u, d, g):
                    act.wait_ge(s["qkT"], u + 1)
                    wait(act, s["scores"], 4 * u - 4)
                    nc.scalar.activation(qT[:, d, 0, :], R.bank[0][:, 0:P], ACT.Identity, scale=scaled_q[:, 0:1],
                                         bias=scaled_q[:, 1:2]).then_inc(s["qe"], 1)
                    for j in range(HQ):
                        ins = nc.scalar.activation(kT[:, d, j, :], R.bank[0][:, P:2 * P], ACT.Identity,
                                                   scale=gb_head[:, 0, j:j + 1], bias=gb_head[:, 1, j:j + 1])
                    ins.then_inc(s["ke"], 1)

                def exp(u, d, g):
                    k, b = quad(u, g), g % 2
                    act.wait_ge(s["maxed"], k + 1)
                    wait(act, s["ptr"], k - 1)
                    for i in range(HQ):
                        ins = nc.scalar.activation(prob[:, b, i * P:(i + 1) * P],
                                                   R.bank[2 + b][:, i * P:(i + 1) * P], ACT.Exp,
                                                   bias=neg_max[:, b, i:i + 1])
                    ins.then_inc(s["exped"], 1)

                def copy_prob(u, d, g):
                    k, b = quad(u, g), g % 2
                    act.wait_ge(s["ptr"], k + 1)
                    wait(act, s["pv"], k - 1)
                    nc.scalar.activation(probT[:, b, :], R.bank[4 + b][:, :], ACT.Identity).then_inc(s["ptc"], 1)

                def copy_heads(part):
                    def fn(u, d, g):
                        act.wait_ge(s["oT"], PARTS * u + part + 1)
                        wait(act, s["y"], u)
                        n = min(4, C) * P
                        nc.scalar.activation(headsT[:, part * n:(part + 1) * n], R.bank[7][:, 0:n], ACT.Identity) \
                            .then_inc(s["oTc"], 1)
                    return fn

                nc.scalar.preload_act_table(ACT.Exp)
                if wide:
                    R.arrived(act, "l1_gate")
                    nc.scalar.activation(W["gate"][:, 0:1], W["gate"][:, 0:1], ACT.Tanh).then_inc(s["gate"], 1)
                    st = [(evac_wide(0), 0, 0), (evac_wide(1), 0, 1), (evac_wide(2), 0, 3)]
                elif kind == 2:
                    act.wait_ge(s["bias"], 1)
                    st = [(evac_q, 0, 0)]
                else:
                    act.wait_ge(s["bias"], 3)
                    st = [(evac_qk, 6, 0)]
                act.wait_ge(s["ones"], 2)
                st = [(lambda u, d, g: norm.store(act, u, d), Y + 2, 3)] + st + [(copy_prob, S + 2)]
                st += [(copy_heads(p), S + 5 + p, 3) for p in range(PARTS)] + [(exp, S)]
                run_ticks(act, B, NQ, st)
        m.clear_semaphores()


def phase_l1_ffn(nc, R, A):
    E, HC = 8, 4
    U, TT = B // 4, 4
    with ExitStack() as ctx:
        m = Memory(nc, ctx, "mlp")
        wr = m.sb("router", E)
        wg, sq, nrm, wgT = m.sb("wg", 16), m.sb("sq", 16), m.sb("nrm", 2), m.sb("wgT", E)
        lg, gate, mask = m.sb("lg", B, E), m.sb("gate", B, E), m.sb("mask", B, E)
        best, score, taken = m.sb("best", B), m.sb("score", B), m.sb("taken", B)
        s_pe, s_dve, s_act, s_pool, s_r = (m.sem(n) for n in ("pe", "dve", "act", "pool", "r"))
        W = R.w["f1"]
        with nc.Block() as block:
            @block.tensor
            def _(pe):
                T = nc.tensor
                pe.wait_ge(s_dve, 6)
                T.transpose(R.bank[0][0:16, 0:E], wg[0:E, :], R.ident[0:E, 0:E]).then_inc(s_pe, 1)
                pe.wait_ge(s_dve, 7)
                R.arrived(pe, "f1_wg_red")
                T.matmul(R.bank[1][:, 0:E], W["wg_red"][0:16, :], wgT[0:16, :], start=True, stop=True) \
                    .then_inc(s_pe, 1)
                pe.wait_ge(s_dve, 8)
                for b in range(B):
                    mm = T.matmul(R.bank[2][:, b * E:(b + 1) * E], R.XNT[:, b, :], wr[:, :], start=True, stop=True)
                mm.then_inc(s_pe, 1)

            @block.gpsimd
            def _(pool):
                pool.wait_ge(s_dve, 3)
                nc.gpsimd.tensor_tensor(nrm[0:E, 1:2], nrm[0:E, 0:1], R.minus_half[0:E, 0:1], ALU.pow) \
                    .then_inc(s_pool, 1)

            @block.scalar
            def _(act):
                nc.scalar.preload_act_table(ACT.Exp)
                act.wait_ge(s_dve, 10)
                nc.scalar.activation(gate[:, :, :], lg[:, :, :], ACT.Exp).then_inc(s_act, 1)

            @block.vector
            def _(dve):
                V = nc.vector
                link = Chain(dve, s_dve)
                R.arrived(dve, "f1_wg")
                link(V.tensor_tensor(sq[0:E, :], W["wg"][0:E, :], W["wg"][0:E, :], ALU.mult))
                link(V.tensor_reduce(nrm[0:E, 0:1], sq[0:E, :], AX.X, ALU.add))
                link(V.tensor_scalar(nrm[0:E, 0:1], nrm[0:E, 0:1], 1e-8, None, ALU.max))
                dve.wait_ge(s_pool, 1)
                link(V.tensor_scalar(wg[0:E, :], W["wg"][0:E, :], nrm[0:E, 1:2], None, ALU.mult))
                link(V.memset(taken[:, :], 0.0))
                link(V.memset(mask[:, :, :], 0.0))
                dve.wait_ge(s_pe, 1)
                link(V.tensor_copy(wgT[0:16, :], R.bank[0][0:16, 0:E]))
                dve.wait_ge(s_pe, 2)
                link(V.tensor_copy(wr[:, :], R.bank[1][:, 0:E]))
                dve.wait_ge(s_pe, 3)
                logits = R.bank[2][:, 0:B * E].rearrange("p (b e) -> p b e", e=E)
                link(V.tensor_reduce(best[:, :], logits, AX.X, ALU.max))
                link(V.tensor_tensor(lg[:, :, :], logits, bcast_last(best[:, :], E), ALU.subtract))
                dve.wait_ge(s_act, 1)
                link(V.tensor_reduce(score[:, :], gate[:, :, :], AX.X, ALU.add))
                link(V.reciprocal(score[:, :], score[:, :]))
                link(V.tensor_scalar(gate[:, :, :], gate[:, :, :], 1.0, None, ALU.is_ge))
                for e in range(E):
                    link(V.tensor_tensor(mask[:, :, e], gate[:, :, e], taken[:, :], ALU.is_gt))
                    link(V.tensor_tensor(taken[:, :], taken[:, :], gate[:, :, e], ALU.max))

        norm = NextNorm(nc, m, R, R.bank[7][:, 128:256])
        h, acc = m.sb("h", 2, TT * P), m.sb("acc", TT, D)
        s_up, s_gelu, s_down, s_acc, s_x = (m.sem(n) for n in ("up", "gelu", "down", "acc", "x"))
        TICKS = E * HC
        with nc.Block() as block:
            def batch(u, t):
                return u * TT + t

            @block.tensor
            def _(pe):
                T = nc.tensor

                def up(u, d, g):
                    k = u * TICKS + g
                    wait(pe, s_gelu, k - 1)
                    e, c = g // HC, g % HC
                    rhs = R.XNT[:, u * TT:(u + 1) * TT, :] if isinstance(u, int) else R.XNT[:, bass.ds(u * TT, TT), :]
                    T.matmul(R.bank[g % 2][:, :], W["w1"][:, e, c * P:(c + 1) * P], rhs.rearrange("p b t -> p (b t)"),
                             start=True, stop=True).then_inc(s_up, 1)

                def down(u, d, g):
                    k = u * TICKS + g
                    e, c = g // HC, g % HC
                    pe.wait_ge(s_gelu, k + 1)
                    if c == 0:
                        wait(pe, s_acc, u * 2 * E + 2 * e - 2)
                    for t in range(TT):
                        mm = T.matmul(R.bank[2 + e % 2][:, t * D:(t + 1) * D], h[:, g % 2, t * P:(t + 1) * P],
                                      W["w2"][:, e, c, :], start=c == 0 and t == 0, stop=c == HC - 1,
                                      skip_group_check=True)
                    mm.then_inc(s_down, 1)

                R.arrived(pe, "f1_w1")
                R.arrived(pe, "f1_w2")
                st = [(up, 0), (down, 2)]
                for t in range(TT):
                    st.append((lambda u, d, g, t=t: norm.transpose(pe, batch(u, t), t % 2), TICKS + 6 + 3 * t, 0))
                run_ticks(pe, U, TICKS, st, body_units=1, head=2)

            @block.scalar
            def _(act):
                def gelu(u, d, g):
                    k = u * TICKS + g
                    act.wait_ge(s_up, k + 1)
                    wait(act, s_down, k - 1)
                    nc.scalar.activation(h[:, g % 2, :], R.bank[g % 2][:, :], ACT.Gelu, bias=W["b1"][:, g:g + 1]) \
                        .then_inc(s_gelu, 1)

                nc.scalar.preload_act_table(ACT.Gelu)
                R.arrived(act, "f1_b1")
                st = [(gelu, 0)]
                for t in range(TT):
                    st.append((lambda u, d, g, t=t: norm.store(act, batch(u, t), t % 2), TICKS + 6 + 3 * t, 0))
                run_ticks(act, U, TICKS, st, body_units=1, head=2)

            @block.gpsimd
            def _(pool):
                run_ticks(pool, U, TICKS, [
                    (lambda u, d, g, t=t: norm.root(pool, batch(u, t), t % 2), TICKS + 4 + 3 * t, 0)
                    for t in range(TT)], body_units=1, head=2)

            @block.vector
            def _(dve):
                V = nc.vector
                R.arrived(dve, "f1_b2")

                def add_expert(u, d, g):
                    e = g // HC
                    link = Chain(dve, s_acc, 2 * E, u)
                    link.k = 2 * e
                    for t in range(TT):
                        w = mask[:, u * TT + t, e:e + 1] if isinstance(u, int) else \
                            mask[:, bass.ds(u * TT + t, 1), e:e + 1].rearrange("p a b -> p (a b)")
                        if e == 0:
                            ins = V.tensor_scalar(acc[:, t, :], W["b2"][:, e, :], w, None, ALU.mult)
                        else:
                            ins = V.scalar_tensor_tensor(out=acc[:, t, :], in0=W["b2"][:, e, :], scalar=w,
                                                         in1=acc[:, t, :], op0=ALU.mult, op1=ALU.add)
                    link(ins)
                    dve.wait_ge(s_down, u * TICKS + HC * (e + 1))
                    for t in range(TT):
                        w = mask[:, u * TT + t, e:e + 1] if isinstance(u, int) else \
                            mask[:, bass.ds(u * TT + t, 1), e:e + 1].rearrange("p a b -> p (a b)")
                        ins = V.scalar_tensor_tensor(out=acc[:, t, :], in0=R.bank[2 + e % 2][:, t * D:(t + 1) * D],
                                                     scalar=w, in1=acc[:, t, :], op0=ALU.mult, op1=ALU.add)
                    link(ins)

                def residual(u, d, g):
                    for t in range(TT):
                        b = batch(u, t)
                        w = score[:, b:b + 1] if isinstance(u, int) else score[:, bass.ds(b, 1)]
                        ins = V.scalar_tensor_tensor(out=row(R.X, b), in0=acc[:, t, :], scalar=w, in1=row(R.X, b),
                                                     op0=ALU.mult, op1=ALU.add)
                    ins.then_inc(s_x, 1)

                def stats(t):
                    def fn(u, d, g):
                        wait_alone(dve, R, s_x, u + 1)
                        norm.statistics(dve, batch(u, t), t % 2)
                    return fn

                st = [(add_expert, 3, e * HC + 3) for e in range(E)] + [(residual, TICKS + 3, 0)]
                for t in range(TT):
                    st.append((stats(t), TICKS + 4 + 3 * t, 0))
                    st.append((lambda u, d, g, t=t: norm.normalise(dve, batch(u, t), t % 2), TICKS + 6 + 3 * t, 0))
                run_ticks(dve, U, TICKS, st, body_units=1, head=2)
        m.clear_semaphores()


def phase_gated_ffn(nc, R, A, kind):
    E, G, I, TOP, TOPG = 16, 4, 64, 4, 2
    with ExitStack() as ctx:
        m = Memory(nc, ctx, f"mlp{kind}")
        W = R.w[f"g{kind}"]
        combine = m.sb("combine", B, E)
        s_pe, s_dve, s_act, s_pool = (m.sem(n) for n in ("pe", "dve", "act", "pool"))
        with ExitStack() as ctx2:
            m2 = Memory(nc, ctx2, f"r{kind}")
            score, choice, tmp, rank = (m2.sb(n, B, E) for n in ("score", "choice", "tmp", "rank"))
            later, cnt = m2.sb("later", B, E), m2.sb("cnt", B, E)
            group, pair, grank, gtmp, gcnt = (m2.sb(n, B, G) for n in ("group", "pair", "grank", "gtmp", "gcnt"))
            total = m2.sb("total", B)
            with nc.Block() as block:
                @block.gpsimd
                def _(pool):
                    for e in range(E):
                        nc.gpsimd.memset(later[:, :, e], float(E - 1 - e)).then_inc(s_pool, 1)

                @block.tensor
                def _(pe):
                    R.arrived(pe, f"g{kind}_router")
                    for b in range(B):
                        mm = nc.tensor.matmul(R.bank[0][:, b * E:(b + 1) * E], R.XNT[:, b, :], W["router"][:, :],
                                              start=True, stop=True)
                    mm.then_inc(s_pe, 1)

                @block.scalar
                def _(act):
                    act.wait_ge(s_pe, 1)
                    nc.scalar.activation(score[:, :, :].rearrange("p b e -> p (b e)"), R.bank[0][:, :], ACT.Sigmoid) \
                        .then_inc(s_act, 1)

                @block.vector
                def _(dve):
                    V = nc.vector
                    link = Chain(dve, s_dve)

                    def rank_of(v, n, rank, tmp, cnt):
                        link(V.memset(rank[:, :, :], 0.0))
                        link(V.memset(cnt[:, :, n - 1], 0.0))
                        for e in range(n - 1):
                            k = n - 1 - e
                            link(V.tensor_tensor(tmp[:, :, e + 1:], bcast_last(v[:, :, e], k), v[:, :, e + 1:],
                                                 ALU.is_ge))
                            V.tensor_tensor(rank[:, :, e + 1:], rank[:, :, e + 1:], tmp[:, :, e + 1:], ALU.add) \
                                .then_inc(s_dve, 1)
                            link.k += 1
                            link(V.tensor_reduce(cnt[:, :, e], tmp[:, :, e + 1:], AX.X, ALU.add))
                        link(V.tensor_tensor(rank[:, :, :], rank[:, :, :], cnt[:, :, :], ALU.subtract))
                        link(V.tensor_tensor(rank[:, :, :], rank[:, :, :], later[:, :, E - n:], ALU.add))

                    dve.wait_ge(s_pool, E)
                    R.arrived(dve, f"g{kind}_bias")
                    dve.wait_ge(s_act, 1)
                    link(V.tensor_tensor(choice[:, :, :], score[:, :, :], bcast_mid(W["bias"][:, :], B), ALU.add))
                    c4 = choice[:, :, :].rearrange("p b (g k) -> p (b g) k", g=G)
                    gr, pr = (t[:, :, :].rearrange("p b g -> p (b g)") for t in (group, pair))
                    link(V.tensor_tensor(gr, c4[:, :, 0], c4[:, :, 1], ALU.add))
                    for i, j in ((0, 2), (0, 3), (1, 2), (1, 3), (2, 3)):
                        link(V.tensor_tensor(pr, c4[:, :, i], c4[:, :, j], ALU.add))
                        link(V.tensor_tensor(gr, gr, pr, ALU.max))
                    rank_of(group, G, grank, gtmp, gcnt)
                    link(V.tensor_scalar(grank[:, :, :], grank[:, :, :], float(TOPG), None, ALU.is_lt))
                    kept = bcast_last(grank[:, :, :].rearrange("p b g -> p (b g)"), E // G)
                    link(V.tensor_tensor(c4, c4, kept, ALU.mult))
                    if kind == 3:
                        link(V.tensor_scalar(gtmp[:, :, :], grank[:, :, :], 1e9, -1e9, ALU.mult, ALU.add))
                        link(V.tensor_tensor(c4, c4, bcast_last(gtmp[:, :, :].rearrange("p b g -> p (b g)"), E // G),
                                             ALU.add))
                    rank_of(choice, E, rank, tmp, cnt)
                    link(V.tensor_scalar(rank[:, :, :], rank[:, :, :], float(TOP), None, ALU.is_lt))
                    link(V.tensor_tensor(score[:, :, :], score[:, :, :], rank[:, :, :], ALU.mult))
                    link(V.tensor_reduce(total[:, :], score[:, :, :], AX.X, ALU.add))
                    link(V.tensor_scalar(total[:, :], total[:, :], 1e-20, None, ALU.add))
                    link(V.reciprocal(total[:, :], total[:, :]))
                    if kind == 3:
                        link(V.tensor_scalar(total[:, :], total[:, :], 2.5, None, ALU.mult))
                    V.tensor_tensor(combine[:, :, :], score[:, :, :], bcast_last(total[:, :], E), ALU.mult)

        last = kind == 3
        norm = None if last else NextNorm(nc, m, R, R.bank[7][:, 128:256])
        H = E // 2 * I
        xs, sil, act_t, wact, wactT = (m.sb("xs", 2, P), m.sb("sil", 2, H), m.sb("act", 2, H), m.sb("wact", 2, H),
                                       m.sb("wactT", 2, H))
        s = {n: m.sem(n) for n in "xs gate up silu mul weigh turn copy y x out".split()}
        with nc.Block() as block:
            @block.tensor
            def _(pe):
                T = nc.tensor

                def gate_up(u, d, g):
                    k = 2 * u + g
                    if g == 0:
                        pe.wait_ge(s["xs"], u + 1)
                    wait(pe, s["silu"], k - 1)
                    T.matmul(R.bank[g][:, :], xs[:, d, :], W["gate"][:, g * H:(g + 1) * H], start=True, stop=True) \
                        .then_inc(s["gate"], 1)
                    wait(pe, s["mul"], k - 1)
                    T.matmul(R.bank[2 + g][:, :], xs[:, d, :], W["up"][:, g * H:(g + 1) * H], start=True, stop=True) \
                        .then_inc(s["up"], 1)

                def turn(u, d, g):
                    k = 2 * u + g
                    pe.wait_ge(s["weigh"], k + 1)
                    wait(pe, s["copy"], k - 1)
                    for i in range(4):
                        mm = T.transpose(R.bank[4 + g][:, i * P:(i + 1) * P], wact[:, g, i * P:(i + 1) * P],
                                         R.ident[:, :])
                    mm.then_inc(s["turn"], 1)

                def down(u, d, g):
                    k = 2 * u + g
                    pe.wait_ge(s["copy"], k + 1)
                    if g == 0:
                        wait(pe, s["x"], u)
                    for i in range(4):
                        c = 4 * g + i
                        mm = T.matmul(R.bank[6][:, 0:D], wactT[:, g, i * P:(i + 1) * P], W["down"][:, c, :],
                                      start=c == 0, stop=c == 7)
                    mm.then_inc(s["y"], 1)

                for name in ("gate", "up", "down"):
                    R.arrived(pe, f"g{kind}_{name}")
                st = [(gate_up, 0), (turn, 2), (down, 3)]
                if not last:
                    st.append((lambda u, d, g: norm.transpose(pe, u, d), 6, 1))
                run_ticks(pe, B, 2, st)

            @block.scalar
            def _(act):
                def silu(u, d, g):
                    k = 2 * u + g
                    act.wait_ge(s["gate"], k + 1)
                    wait(act, s["mul"], k - 1)
                    nc.scalar.activation(sil[:, g, :], R.bank[g][:, :], ACT.Silu).then_inc(s["silu"], 1)

                def copy(u, d, g):
                    k = 2 * u + g
                    act.wait_ge(s["turn"], k + 1)
                    wait(act, s["y"], k - 1)
                    nc.scalar.activation(wactT[:, g, :], R.bank[4 + g][:, :], ACT.Identity).then_inc(s["copy"], 1)

                nc.scalar.preload_act_table(ACT.Silu)
                st = [(silu, 0), (copy, 2)]
                if not last:
                    st.append((lambda u, d, g: norm.store(act, u, d), 6, 1))
                run_ticks(act, B, 2, st)

            @block.gpsimd
            def _(pool):
                def weigh(u, d, g):
                    k = 2 * u + g
                    pool.wait_ge(s["mul"], k + 1)
                    wait(pool, s["turn"], k - 1)
                    w = combine[:, u, 8 * g:8 * g + 8] if isinstance(u, int) else \
                        combine[:, bass.ds(u, 1), 8 * g:8 * g + 8].rearrange("p a e -> p (a e)")
                    nc.gpsimd.tensor_tensor(wact[:, g, :].rearrange("p (e i) -> p e i", i=I),
                                            act_t[:, g, :].rearrange("p (e i) -> p e i", i=I), bcast_last(w, I),
                                            ALU.mult).then_inc(s["weigh"], 1)

                st = [(weigh, 0)]
                if not last:
                    st.append((lambda u, d, g: norm.root(pool, u, d), 4, 1))
                run_ticks(pool, B, 2, st)

            @block.vector
            def _(dve):
                V = nc.vector

                def copy_x(u, d, g):
                    wait(dve, s["up"], 2 * (u - 1))
                    V.tensor_scalar(xs[:, d, :], row(R.XNT, u), 1.0, None, ALU.mult).then_inc(s["xs"], 1)

                def multiply(u, d, g):
                    k = 2 * u + g
                    dve.wait_ge(s["silu"], k + 1)
                    dve.wait_ge(s["up"], k + 1)
                    wait(dve, s["weigh"], k - 1)
                    V.tensor_tensor(act_t[:, g, :], R.bank[2 + g][:, :], sil[:, g, :], ALU.mult).then_inc(s["mul"], 1)

                def residual(u, d, g):
                    dve.wait_ge(s["y"], 2 * (u + 1))
                    V.tensor_tensor(row(R.X, u), row(R.X, u), R.bank[6][:, 0:D], ALU.add).then_inc(s["x"], 1)
                    if not last:
                        wait_alone(dve, R, s["x"], u + 1)
                        norm.statistics(dve, u, d)

                st = [(copy_x, 0, 0), (multiply, 0), (residual, 4, 1)]
                if not last:
                    st.append((lambda u, d, g: norm.normalise(dve, u, d), 6, 1))
                run_ticks(dve, B, 2, st)

            @block.sync
            def _(sp):
                if last:
                    def store(u, d, g):
                        sp.wait_ge(s["x"], u + 1)
                        sp.dma_start(row(A["out"], u), row(R.X, u)).then_inc(s["out"], 16)
                    run_ticks(sp, B, 1, [(store, 0)])
                    sp.wait_ge(s["out"], 16 * B)
        m.clear_semaphores()


def phase_output(nc, R, A):
    with nc.semaphore("stored") as stored, nc.Block() as block:
        @block.sync
        def _(sp):
            sp.dma_start(A["out"], R.X[:, :, :]).then_inc(stored, 16)
            sp.wait_ge(stored, 16)
            for name in R.loads:
                R.arrived(sp, name)


def build(nc, A, phases):
    with ExitStack() as ctx:
        R = Resident()

        def sb(name, *shape, dt=F32):
            return ctx.enter_context(nc.sbuf_tensor(name, [P, *shape], dt))

        R.X, R.XNT = sb("X", B, D), sb("XNT", B, P)
        R.bank = [ctx.enter_context(nc.psum_tensor(f"bank{i}", [P, 512], F32)) for i in range(8)]
        R.ident, R.upto, R.future, R.ones = sb("ident", P), sb("upto", P), sb("future", P), sb("ones", P)
        R.pick = sb("pick", P)
        R.carrier = sb("carrier", 1)
        R.minus_half = sb("minus_half", 64)
        R.head_of4, R.head_of_quad = sb("head_of4", 4, P), sb("head_of_quad", 4, P)
        R.token_sums = sb("token_sums", B)
        R.constants = ctx.enter_context(nc.semaphore("constants"))
        R.loads, R.w, R.load_sem, R.load_count = {}, {}, {}, {}

        def weight(name, *shape, rows=P):
            t = sb(name, *shape)
            src = A[name]
            if len(src.shape) == 1:
                src = src.partition_broadcast(P)
            dst = t[tuple([slice(0, rows)] + [slice(None)] * len(shape))]
            phase, _, part = name.partition("_")
            if phase not in R.load_sem:
                R.load_sem[phase], R.load_count[phase] = ctx.enter_context(nc.semaphore(f"load_{phase}")), 0
            R.load_count[phase] += 16
            R.loads[name] = (dst, src, R.load_sem[phase])
            R.w.setdefault(phase, {"loaded": ("q", "kv", "o")})[part] = t
            return t

        R.gate_w, R.gate_b, R.rms = weight("gate_w", 3, 8), weight("gate_b", 8), weight("rms", 32)
        R.hyper, R.l1_gb = weight("hyper", 6), weight("l1_gb", 2)
        weight("l1_q", 1024), weight("l1_kv", 2048), weight("l1_o", 1024), weight("l1_bo", D), weight("l1_gate", 1)
        weight("f1_wg", 16, rows=8), weight("f1_wg_red", P, rows=16)
        weight("f1_w1", 8, 512), weight("f1_b1", 32), weight("f1_w2", 8, 4, D), weight("f1_b2", 8 * D)
        R.w["f1"]["b2"] = R.w["f1"]["b2"][:, :].rearrange("p (e n) -> p e n", e=8)
        for k in (2, 3):
            weight(f"l{k}_q", P), weight(f"l{k}_kv", 2 * P), weight(f"l{k}_o", D), weight(f"l{k}_bo", D)
            if k == 2:
                weight("l2_bqk", 2), weight("l2_bv", P)
            else:
                weight("l3_gb", 2)
            weight(f"g{k}_router", 16), weight(f"g{k}_bias", 16)
            weight(f"g{k}_gate", 1024), weight(f"g{k}_up", 1024), weight(f"g{k}_down", 8, D)

        def arrived(eng, name):
            phase = name.partition("_")[0]
            eng.wait_ge(R.load_sem[phase], R.load_count[phase])

        R.arrived = arrived
        for phase in phases:
            phase(nc, R, A)
        if len(phases) < 9:
            phase_output(nc, R, A)


def l1_xattn(nc, R, A):
    phase_attention(nc, R, A, 1)


def l2_xattn(nc, R, A):
    phase_attention(nc, R, A, 2)


def l3_xattn(nc, R, A):
    phase_attention(nc, R, A, 3)


def l2_ffn(nc, R, A):
    phase_gated_ffn(nc, R, A, 2)


def l3_ffn(nc, R, A):
    phase_gated_ffn(nc, R, A, 3)


PHASES = [phase_input, phase_l0_xattn, phase_l0_ffn, l1_xattn, phase_l1_ffn, l2_xattn, l2_ffn, l3_xattn, l3_ffn]


def kernel(**inputs):
    import numpy as np
    import concourse.bacc as bacc
    from concourse.bass_utils import run_bass_kernel_spmd

    def n(name):
        return np.asarray(inputs[name])

    c = np.ascontiguousarray
    arrays = {
        "x": c(n("x").transpose(1, 0, 2)),
        "ctx": c(n("ctx_1024").transpose(1, 0, 2)),
        "ctxT": c(n("ctx_1024").transpose(2, 0, 1)),
        "gate_w": c(np.concatenate([n("L0_xattn_igate_kernel"), n("L0_xattn_fgate_kernel")], 1)
                    .reshape(3, 128, 8).transpose(1, 0, 2)),
        "gate_b": np.concatenate([n("L0_xattn_igate_bias"), n("L0_xattn_fgate_bias")]),
        "rms": n("L0_xattn_rms_scale"),
        "hyper": n("L0_ffn_hyperplanes"),
        "experts": n("L0_ffn_expert_weights"),
        "l1_gb": c(np.stack([n("L1_xattn_ln_gamma"), n("L1_xattn_ln_beta")], 1)),
        "l1_q": n("L1_xattn_w_q"), "l1_kv": n("L1_xattn_w_kv"),
        "l1_o": c(n("L1_xattn_w_out").reshape(8, 128, 128).transpose(1, 0, 2).reshape(128, 1024)),
        "l1_bo": n("L1_xattn_b_out"), "l1_gate": n("L1_xattn_gate"),
        "f1_wg": n("L1_ffn_wg"), "f1_wg_red": n("L1_ffn_wg_red"),
        "f1_w1": c(n("L1_ffn_w1").transpose(1, 0, 2)),
        "f1_b1": c(n("L1_ffn_b1").reshape(32, 128).T),
        "f1_w2": c(n("L1_ffn_w2").reshape(8, 4, 128, 128).transpose(2, 0, 1, 3)),
        "f1_b2": n("L1_ffn_b2").reshape(-1),
        "l2_q": c(n("L2_xattn_Wq").transpose(1, 0, 2).reshape(128, 128)),
        "l2_kv": c(np.concatenate([n("L2_xattn_Wk").transpose(1, 0, 2).reshape(128, 128),
                                   n("L2_xattn_Wv").transpose(1, 0, 2).reshape(128, 128)], 1)),
        "l2_o": n("L2_xattn_Wo"), "l2_bo": n("L2_xattn_bo"), "l2_bv": n("L2_xattn_bv").reshape(-1),
        "l2_bqk": c(np.stack([n("L2_xattn_bq").reshape(-1), n("L2_xattn_bk").reshape(-1)], 1)),
        "l3_q": n("L3_xattn_Wq"), "l3_kv": n("L3_xattn_Wkv"), "l3_o": n("L3_xattn_Wp"), "l3_bo": n("L3_xattn_bp"),
        "l3_gb": c(np.stack([np.tile(n("L3_xattn_ln_g"), 16), np.tile(n("L3_xattn_ln_b"), 16)], 1)),
        "g2_router": c(n("L2_ffn_gate_weight").T), "g2_bias": n("L2_ffn_e_bias"),
        "g3_router": c(n("L3_ffn_router_weight").T), "g3_bias": n("L3_ffn_router_bias"),
    }
    for k, (gate, up, down) in {"g2": ("L2_ffn_gate_proj", "L2_ffn_up_proj", "L2_ffn_down_proj"),
                                "g3": ("L3_ffn_w_gate", "L3_ffn_w_up", "L3_ffn_w_down")}.items():
        arrays[f"{k}_gate"] = c(n(gate).reshape(1024, 128).T)
        arrays[f"{k}_up"] = c(n(up).reshape(1024, 128).T)
        arrays[f"{k}_down"] = c(n(down).transpose(0, 2, 1).reshape(8, 128, 128).transpose(1, 0, 2))
    nc = bacc.Bacc("TRN2", target_bir_lowering=False, num_devices=1)
    A = {k: nc.dram_tensor(f"in_{k}", v.shape, mybir.dt.from_np(v.dtype), kind="ExternalInput").ap()
         for k, v in arrays.items()}
    A["out"] = nc.dram_tensor("out_0", (P, B, D), F32, kind="ExternalOutput").ap()
    build(nc, A, PHASES)
    r = run_bass_kernel_spmd(nc, [{f"in_{k}": v for k, v in arrays.items()}], core_ids=[0])
    return r.results[0]["out_0"].transpose(1, 0, 2)
```

```python
from contextlib import ExitStack

import concourse.bass as bass
from concourse import mybir

P = 128
B = 32
D = 128
F32 = mybir.dt.float32
F32R = mybir.dt.float32r
I32 = mybir.dt.int32
ALU = mybir.AluOpType
ACT = mybir.ActivationFunctionType
AX = mybir.AxisListType
LN_EPS = 1e-5


def run_ticks(eng, units, ticks, stages, body_units=2, head=None):
    stages = [(s + (None,))[:3] for s in stages]
    lag_max = max(lag for _, lag, _ in stages)
    if head is None:
        head = -(-(lag_max + 2 * ticks) // (ticks * body_units)) * body_units
    total = units * ticks

    def step(u0, t, base):
        for fn, lag, at in stages:
            k = t - lag
            if isinstance(u0, int) and not 0 <= u0 * ticks + k < total:
                continue
            du, g = k // ticks, k % ticks
            if at is None or g == at:
                u = u0 + du if du > 0 else (u0 - (-du) if du < 0 else u0)
                fn(u, (base + du) % 2, g)

    for u in range(head):
        for t in range(ticks):
            step(u, t, u)
    turns = (units - head) // body_units
    if turns > 0:
        with eng.Fori(head, head + (turns - 1) * body_units + 1, body_units) as u:
            for j in range(body_units):
                for t in range(ticks):
                    step(u, t + j * ticks, 0)
    done = head + turns * body_units
    for u in range(done, units + -(-lag_max // ticks)):
        for t in range(ticks):
            step(u, t, u)


def wait(eng, sem, value):
    if isinstance(value, int) and value <= 0:
        return
    eng.wait_ge(sem, value)


class Chain:

    def __init__(self, eng, sem, per_unit=0, unit=0):
        self.eng, self.sem, self.base, self.k = eng, sem, unit * per_unit, 0

    def __call__(self, ins, alone=None):
        self.k += 1
        ins.then_inc(self.sem, 1)
        if alone is not None:
            wait_alone(self.eng, alone, self.sem, self.base + self.k)
        else:
            self.eng.wait_ge(self.sem, self.base + self.k)


def row(t, u):
    if isinstance(u, int):
        return t[:, u, :]
    return t[:, bass.ds(u, 1), :].rearrange("p a b -> p (a b)")


def cols(t, u, n, first=0, count=None):
    count = n if count is None else count
    if isinstance(u, int):
        return t[:, u * n + first:u * n + first + count]
    return t[:, bass.ds(u * n + first, count)]


def bcast_last(ap, n):
    return ap.unsqueeze(2).broadcast_to([ap.shape[0], ap.shape[1], n])


def bcast_mid(ap, m):
    return ap.unsqueeze(1).broadcast_to([ap.shape[0], m, ap.shape[1]])


def wait_alone(dve, R, sem, value):
    wait(dve, sem, value)
    if not isinstance(value, int):
        dve.memset(R.carrier[:, :], 0.0)


class Memory:

    def __init__(self, nc, ctx, tag):
        self.nc, self.ctx, self.tag, self.sems = nc, ctx, tag, []

    def sb(self, name, *shape, dt=F32):
        return self.ctx.enter_context(self.nc.sbuf_tensor(f"{self.tag}_{name}", [P, *shape], dt))

    def sem(self, name):
        sem = self.ctx.enter_context(self.nc.semaphore(f"{self.tag}_{name}"))
        self.sems.append(sem)
        return sem

    def clear_semaphores(self):
        nums = sorted(sem.num for sem in self.sems)
        with self.nc.Block() as block:
            @block.gpsimd
            def _(pool):
                first = nums[0]
                for a, b in zip(nums, nums[1:] + [None]):
                    if b != a + 1:
                        pool.sem_clear(range(first, a + 1))
                        first = b


class NextNorm:

    def __init__(self, nc, m, R, bank, gamma_beta=None, sums=None):
        self.nc, self.R, self.tp, self.gb, self.sums = nc, R, bank, gamma_beta, sums
        self.rounds = 2 if gamma_beta is not None else 1
        self.stats = m.sb("ln_stats", 2, 6)
        self.mean_var = m.sb("ln_mean_var", 2, 2 * self.rounds)
        self.var = m.sb("ln_var", 2, self.rounds)
        self.rstd = m.sb("ln_rstd", 2, self.rounds)
        self.xn = m.sb("ln_xn", 2, D)
        self.chain = [m.sem(f"ln_chain{r}") for r in range(self.rounds)]
        self.var_ready = [m.sem(f"ln_var_ready{r}") for r in range(self.rounds)]
        self.rstd_ready = [m.sem(f"ln_rstd_ready{r}") for r in range(self.rounds)]
        self.xn1_ready = m.sem("ln_xn1_ready")
        self.xn_ready = m.sem("ln_xn_ready")
        self.transposed = m.sem("ln_transposed")
        self.stored = m.sem("ln_stored")

    def statistics(self, eng, u, d, r=0):
        nc = self.nc
        link = Chain(eng, self.chain[r], 2, u)
        if r:
            wait_alone(eng, self.R, self.xn1_ready, u + 1)
        src = self.xn[:, d, :] if r else row(self.R.X, u)
        link(nc.vector.bn_stats(self.stats[:, d, :], src), alone=self.R)
        link(nc.vector.bn_aggr(self.mean_var[:, d, 2 * r:2 * r + 2], self.stats[:, d, :]))
        nc.vector.tensor_scalar(self.var[:, d, r:r + 1], self.mean_var[:, d, 2 * r + 1:2 * r + 2], LN_EPS, None,
                                ALU.add).then_inc(self.var_ready[r], 1)

    def root(self, eng, u, d, r=0):
        eng.wait_ge(self.var_ready[r], u + 1)
        self.nc.gpsimd.tensor_tensor(self.rstd[:, d, r:r + 1], self.var[:, d, r:r + 1], self.R.minus_half[:, 0:1],
                                     ALU.pow).then_inc(self.rstd_ready[r], 1)

    def normalise(self, eng, u, d, r=0):
        last = r == self.rounds - 1
        if r == 0:
            wait(eng, self.transposed, u - 1)
        eng.wait_ge(self.rstd_ready[r], u + 1)
        src = self.xn[:, d, :] if r else row(self.R.X, u)
        self.nc.vector.tensor_scalar(self.xn[:, d, :], src, self.mean_var[:, d, 2 * r:2 * r + 1],
                                     self.rstd[:, d, r:r + 1], ALU.subtract, ALU.mult) \
            .then_inc(self.xn_ready if last else self.xn1_ready, 1)

    def transpose(self, eng, u, d):
        eng.wait_ge(self.xn_ready, u + 1)
        wait(eng, self.stored, u)
        self.nc.tensor.transpose(self.tp, self.xn[:, d, :], self.R.ident[:, :]).then_inc(self.transposed, 1)

    def store(self, eng, u, d):
        eng.wait_ge(self.transposed, u + 1)
        kw = {}
        if self.gb is not None:
            kw = dict(scale=self.gb[:, 0:1], bias=self.gb[:, 1:2])
        if self.sums is not None:
            kw = dict(accum_out=cols(self.sums, u, 1))
        self.nc.scalar.activation(row(self.R.XNT, u), self.tp, ACT.Identity, **kw).then_inc(self.stored, 1)


class Resident:
    pass


def phase_input(nc, R, A):
    PARTS = 4
    N = B // PARTS
    with ExitStack() as ctx:
        m = Memory(nc, ctx, "in")
        stats, mean_var, var, rstd = (m.sb("stats", B, 6), m.sb("mean_var", B, 2), m.sb("var", B), m.sb("rstd", B))
        xn = m.sb("xn", 2, N, D)
        ctxT_all = m.sb("ctxT_all", B, P)
        gate_kv = m.sb("gate_kv", 8)
        x_in = [m.sem(f"x_in{c}") for c in range(PARTS)]
        ctx_in, made, gate_w = m.sem("ctx_in"), m.sem("made"), m.sem("gate_w")
        measured, gathered, var_ready, rstd_ready, xn_ready, turned, stored = (
            m.sem(n) for n in ("measured", "gathered", "var_ready", "rstd_ready", "xn_ready", "turned", "stored"))
        gates_done = m.sem("gates_done")
        with nc.Block() as block:
            @block.sync
            def _(sp):
                for c in range(PARTS):
                    sp.dma_start(R.X[:, c * N:(c + 1) * N, :], A["x"][:, c * N:(c + 1) * N, :]).then_inc(x_in[c], 16)
                for i, (name, (dst, src, sem)) in enumerate(R.loads.items()):
                    if i == 1:
                        sp.dma_start(ctxT_all[:, :, :], A["ctxT"]).then_inc(ctx_in, 16)
                    sp.dma_start(dst, src).then_inc(sem, 16)

            @block.gpsimd
            def _(pool):
                link = Chain(pool, made)
                pool.wait_ge(R.constants, 1)
                link(nc.gpsimd.memset(R.ones[:, :], 1.0))
                link(nc.gpsimd.affine_select(out=R.ident[:, :], in_=R.ones[:, :], compare_op=ALU.is_equal, fill=0.0,
                                             base=0, pattern=[[1, P]], channel_multiplier=-1))
                for c in range(PARTS):
                    part = slice(c * N, (c + 1) * N)
                    pool.wait_ge(var_ready, c + 1)
                    nc.gpsimd.tensor_tensor(rstd[:, part], var[:, part], R.minus_half[:, 0:N], ALU.pow) \
                        .then_inc(rstd_ready, 1)

                link(nc.gpsimd.affine_select(out=R.upto[:, :], in_=R.ones[:, :], compare_op=ALU.is_ge, fill=0.0,
                                             base=0, pattern=[[1, P]], channel_multiplier=-1))
                link(nc.gpsimd.memset(R.future[:, :], 0.0))
                link(nc.gpsimd.affine_select(out=R.future[:, :], in_=R.future[:, :], compare_op=ALU.is_ge, fill=1e30,
                                             base=0, pattern=[[1, P]], channel_multiplier=-1))
                link(nc.gpsimd.memset(R.head_of4[:, :, :], 1.0))
                link(nc.gpsimd.affine_select(out=R.head_of4[:, :, :], in_=R.head_of4[:, :, :], compare_op=ALU.is_ge,
                                             fill=0.0, base=0, pattern=[[-32, 4], [0, P]], channel_multiplier=1))
                link(nc.gpsimd.affine_select(out=R.head_of4[:, :, :], in_=R.head_of4[:, :, :], compare_op=ALU.is_ge,
                                             fill=0.0, base=31, pattern=[[32, 4], [0, P]], channel_multiplier=-1))
                link(nc.gpsimd.memset(R.head_of_quad[:, :, :], 0.0))
                for g in range(4):
                    for j in range(4):
                        link(nc.gpsimd.affine_select(out=R.pick[:, :], in_=R.ones[:, :], compare_op=ALU.is_ge, fill=0.0,
                                                     base=-(32 * g + 8 * j), pattern=[[0, P]], channel_multiplier=1))
                        link(nc.gpsimd.affine_select(out=R.pick[:, :], in_=R.pick[:, :], compare_op=ALU.is_ge, fill=0.0,
                                                     base=32 * g + 8 * j + 7, pattern=[[0, P]], channel_multiplier=-1))
                        link(nc.gpsimd.tensor_tensor(R.head_of_quad[:, j, :], R.head_of_quad[:, j, :], R.pick[:, :],
                                                     ALU.add))

            @block.vector
            def _(dve):
                V = nc.vector
                V.memset(R.minus_half[:, :], -0.5).then_inc(R.constants, 1)

                def measure(c):
                    part = slice(c * N, (c + 1) * N)
                    dve.wait_ge(x_in[c], 16)
                    for b in range(c * N, (c + 1) * N):
                        ins = V.bn_stats(stats[:, b, :], R.X[:, b, :])
                    ins.then_inc(measured, 1)
                    dve.wait_ge(measured, c + 1)
                    for b in range(c * N, (c + 1) * N):
                        ins = V.bn_aggr(mean_var[:, b, :], stats[:, b, :])
                    ins.then_inc(gathered, 1)
                    dve.wait_ge(gathered, c + 1)
                    V.tensor_scalar(var[:, part], mean_var[:, part, 1], LN_EPS, None, ALU.add).then_inc(var_ready, 1)

                def normalise(c):
                    dve.wait_ge(rstd_ready, c + 1)
                    wait(dve, turned, N * (c - 1))
                    for i in range(N):
                        b = c * N + i
                        V.tensor_scalar(xn[:, c % 2, i, :], R.X[:, b, :], mean_var[:, b, 0:1], rstd[:, b:b + 1],
                                        ALU.subtract, ALU.mult).then_inc(xn_ready, 1)

                for c in range(PARTS):
                    measure(c)
                    if c == 0:
                        R.arrived(dve, "gate_w")
                        V.tensor_tensor(gate_kv[:, :], R.gate_w[:, 1, :], R.gate_w[:, 2, :], ALU.add) \
                            .then_inc(gate_w, 1)
                    else:
                        normalise(c - 1)
                normalise(PARTS - 1)

            @block.tensor
            def _(pe):
                T = nc.tensor
                pe.wait_ge(made, 2)
                for c in range(PARTS):
                    for half in range(2):
                        k = 2 * c + half
                        bank = R.bank[4 + k % 4]
                        wait(pe, stored, k - 3)
                        for i in range(4):
                            b = 4 * k + i
                            pe.wait_ge(xn_ready, b + 1)
                            T.transpose(bank[:, i * P:(i + 1) * P], xn[:, c % 2, 4 * half + i, :], R.ident[:, :]) \
                                .then_inc(turned, 1)
                R.arrived(pe, "gate_w")
                pe.wait_ge(gate_w, 1)
                pe.wait_ge(ctx_in, 16)
                pe.wait_ge(stored, B // 4)
                for b in range(B):
                    out = R.bank[0][:, b * 8:(b + 1) * 8]
                    T.matmul(out, R.XNT[:, b, :], R.gate_w[:, 0, :], start=True, stop=False)
                    mm = T.matmul(out, ctxT_all[:, b, :], gate_kv[:, :], start=False, stop=True)
                mm.then_inc(gates_done, 1)

            @block.scalar
            def _(act):
                nc.scalar.preload_act_table(ACT.Exp)
                for k in range(B // 4):
                    act.wait_ge(turned, 4 * (k + 1))
                    nc.scalar.activation(R.XNT[:, 4 * k:4 * k + 4, :].rearrange("p b t -> p (b t)"),
                                         R.bank[4 + k % 4][:, :], ACT.Identity).then_inc(stored, 1)
        m.clear_semaphores()


def phase_l0_xattn(nc, R, A):
    NH, HD = 4, 32
    with ExitStack() as ctx:
        m = Memory(nc, ctx, "m0")
        scratch = nc.dram_tensor("running_max_rows", (B, NH * P), F32)
        ig, fg = m.sb("ig", B * NH), m.sb("fg", B * NH)
        t0, t1, logf = m.sb("t0", B * NH), m.sb("t1", B * NH), m.sb("logf", B * NH)
        csum, gpre = m.sb("csum", B * NH), m.sb("gpre", B * NH)
        gT, maxT = m.sb("gT", P), m.sb("maxT", P)
        floor_n = m.sb("floor_n", B * NH)
        s_dve, s_act, s_pe, s_scr = m.sem("dve"), m.sem("act"), m.sem("pe"), m.sem("scr")
        gp = R.bank[0][:, 0:B * 2 * NH]
        with nc.Block() as block:
            @block.sync
            def _(sp):
                sp.wait_ge(s_dve, 10)
                sp.dma_start(scratch.ap().rearrange("b (h t) -> (b h) t", h=NH), maxT[:, :]).then_inc(s_scr, 16)
                sp.wait_ge(s_scr, 16)

            @block.tensor
            def _(pe):
                pe.wait_ge(s_dve, 6)
                nc.tensor.matmul(R.bank[1][:, 0:P], R.upto[:, :], logf[:, :], start=True, stop=True).then_inc(s_pe, 1)
                pe.wait_ge(s_dve, 8)
                nc.tensor.transpose(R.bank[2][:, 0:P], gpre[:, :], R.ident[:, :]).then_inc(s_pe, 1)
                pe.wait_ge(s_dve, 10)
                nc.tensor.transpose(R.bank[3][:, 0:P], maxT[:, :], R.ident[:, :]).then_inc(s_pe, 1)

            @block.vector
            def _(dve):
                link = Chain(dve, s_dve)
                R.arrived(dve, "gate_b")
                gv = gp.rearrange("p (b k) -> p b k", k=2 * NH)
                link(nc.vector.tensor_tensor(ig[:, :].rearrange("p (b h) -> p b h", h=NH), gv[:, :, 0:NH],
                                             bcast_mid(R.gate_b[:, 0:NH], B), ALU.add))
                link(nc.vector.tensor_tensor(fg[:, :].rearrange("p (b h) -> p b h", h=NH), gv[:, :, NH:],
                                             bcast_mid(R.gate_b[:, NH:], B), ALU.add))
                link(nc.vector.tensor_scalar(t0[:, :], fg[:, :], -1.0, None, ALU.mult))
                link(nc.vector.tensor_tensor(t0[:, :], t0[:, :], fg[:, :], ALU.min))
                link(nc.vector.tensor_scalar(fg[:, :], fg[:, :], 0.0, None, ALU.min))
                dve.wait_ge(s_act, 2)
                link(nc.vector.tensor_tensor(logf[:, :], fg[:, :], t1[:, :], ALU.subtract))
                dve.wait_ge(s_pe, 1)
                link(nc.vector.tensor_copy(csum[:, :], R.bank[1][:, 0:P]))
                link(nc.vector.tensor_tensor(gpre[:, :], ig[:, :], csum[:, :], ALU.subtract))
                dve.wait_ge(s_pe, 2)
                link(nc.vector.tensor_copy(gT[:, :], R.bank[2][:, 0:P]))
                link(nc.vector.tensor_tensor_scan(maxT[:, :], gT[:, :], gT[:, :], -3.0e38, ALU.max, ALU.max))
                dve.wait_ge(s_pe, 3)
                nc.vector.tensor_tensor(t0[:, :], R.bank[3][:, 0:P], csum[:, :], ALU.add).then_inc(s_dve, 1)
                dve.wait_ge(s_act, 3)
                nc.vector.tensor_scalar(floor_n[:, :], floor_n[:, :], 1e-6, None, ALU.add)

            @block.scalar
            def _(act):
                act.wait_ge(s_dve, 4)
                nc.scalar.activation(t1[:, :], t0[:, :], ACT.Exp).then_inc(s_act, 1)
                act.wait_ge(s_act, 1)
                nc.scalar.activation(t1[:, :], t1[:, :], ACT.Ln, bias=1.0).then_inc(s_act, 1)
                act.wait_ge(s_dve, 11)
                nc.scalar.activation(floor_n[:, :], t0[:, :], ACT.Exp, scale=-1.0).then_inc(s_act, 1)

        norm = NextNorm(nc, m, R, R.bank[7][:, 128:256], sums=R.token_sums)
        ct, cn, mb = m.sb("ct", 2, P), m.sb("cn", 2, D), m.sb("mb", 2, NH * P)
        mbm, dT, qm, cT = (m.sb(n, 2, NH * P) for n in ("mbm", "dT", "qm", "cT"))
        vaug = m.sb("vaug", 2, NH, HD + 1)
        den, sq, hn, ss, vv, rr = (m.sb("den", 2, NH), m.sb("sq", 2, D), m.sb("hn", 2, D), m.sb("ss", 2, NH),
                                   m.sb("vv", 2, NH), m.sb("rr", 2, NH))
        scaled, s_scaled = m.sb("scaled", 2, D), m.sem("scaled")
        s_in = [m.sem("in0"), m.sem("in1")]
        s_ones, s_v, s_mbm, s_dT, s_qm, s_sc, s_cT, s_hp, s_hn, s_vv, s_rr, s_l0, s_l1, s_res, s_rms = (
            m.sem(n) for n in ("ones", "v", "mbm", "dT", "qm", "sc", "cT", "hp", "hn", "vv", "rr", "l0", "l1",
                               "res", "rms"))
        INV = 1.0 / float(32) ** 0.5
        with nc.Block() as block:
            @block.sync
            def _(sp):
                def load(u, d, g):
                    wait(sp, s_sc, u - 1)
                    wait(sp, s_v, u - 1)
                    wait(sp, s_mbm, u - 1)
                    sp.dma_start(ct[:, d, :], row(A["ctxT"], u)).then_inc(s_in[d], 16)
                    sp.dma_start(cn[:, d, :], row(A["ctx"], u)).then_inc(s_in[d], 16)
                    src = scratch.ap()[u, :] if isinstance(u, int) else \
                        scratch.ap()[bass.ds(u, 1), :].rearrange("a n -> (a n)")
                    sp.dma_start(mb[:, d, :], src.partition_broadcast(P)).then_inc(s_in[d], 16)
                run_ticks(sp, B, 1, [(load, 0)])

            def inputs(eng, u, d):
                n = (u // 2 + 1) * 48 if isinstance(u, int) else u * 24 + (48 - 24 * d)
                eng.wait_ge(s_in[d], n)

            @block.gpsimd
            def _(pool):
                nc.gpsimd.memset(vaug[:, :, :, :], 1.0).then_inc(s_ones, 1)
                pool.wait_ge(s_ones, 1)
                pool.wait_ge(s_rms, 1)

                def prepare(u, d, g):
                    inputs(pool, u, d)
                    wait(pool, s_hp, u - 1)
                    nc.gpsimd.tensor_tensor(vaug[:, d, :, 0:HD], cn[:, d, :].rearrange("p (h e) -> p h e", h=NH),
                                            R.ones[:, :].rearrange("p (h e) -> p h e", h=NH), ALU.mult) \
                        .then_inc(s_v, 1)
                    wait(pool, s_dT, u - 1)
                    nc.gpsimd.tensor_tensor(mbm[:, d, :].rearrange("p (h t) -> p h t", h=NH),
                                            mb[:, d, :].rearrange("p (h t) -> p h t", h=NH),
                                            bcast_mid(R.future[:, :], NH), ALU.add).then_inc(s_mbm, 1)

                def scale_heads(u, d, g):
                    pool.wait_ge(s_hn, u + 1)
                    wait(pool, s_l1, 2 * (u - 1))
                    nc.gpsimd.tensor_tensor(scaled[:, d, :].rearrange("p (h e) -> p h e", h=NH),
                                            hn[:, d, :].rearrange("p (h e) -> p h e", h=NH),
                                            bcast_mid(R.rms[:, 0:HD], NH), ALU.mult).then_inc(s_scaled, 1)

                def root(u, d, g):
                    pool.wait_ge(s_vv, u + 1)
                    nc.gpsimd.tensor_tensor(rr[:, d, :], vv[:, d, :], R.minus_half[:, 0:NH], ALU.pow) \
                        .then_inc(s_rr, 1)

                run_ticks(pool, B, 1, [(prepare, 0), (scale_heads, 2), (root, 2), (lambda u, d, g: norm.root(pool, u, d), 3)])

            @block.vector
            def _(dve):
                def weigh(u, d, g):
                    dve.wait_ge(s_sc, u + 1)
                    dve.wait_ge(s_dT, u + 1)
                    wait(dve, s_hp, u - 1)
                    nc.vector.scalar_tensor_tensor(out=cT[:, d, :], in0=R.bank[d][:, 0:NH * P], scalar=INV,
                                                   in1=dT[:, d, :], op0=ALU.mult, op1=ALU.mult).then_inc(s_cT, 1)

                def heads(u, d, g):
                    dve.wait_ge(s_hp, u + 1)
                    hp = R.bank[2 + d][:, 0:NH * (HD + 1)].rearrange("p (h e) -> p h e", h=NH)
                    link = Chain(dve, s_l0, 4, u)
                    link(nc.vector.scalar_tensor_tensor(out=den[:, d, :].unsqueeze(2), in0=hp[:, :, HD:HD + 1],
                                                        scalar=1e-6, in1=cols(floor_n, u, NH).unsqueeze(2),
                                                        op0=ALU.add, op1=ALU.max))
                    link(nc.vector.reciprocal(den[:, d, :], den[:, d, :]))
                    hv = hn[:, d, :].rearrange("p (h e) -> p h e", h=NH)
                    nc.vector.tensor_tensor(hv, hp[:, :, 0:HD], bcast_last(den[:, d, :], HD), ALU.mult) \
                        .then_inc(s_hn, 1)
                    dve.wait_ge(s_hn, u + 1)
                    link(nc.vector.tensor_tensor(sq[:, d, :], hn[:, d, :], hn[:, d, :], ALU.mult))
                    link(nc.vector.tensor_reduce(ss[:, d, :], sq[:, d, :].rearrange("p (h e) -> p h e", h=NH),
                                                 AX.X, ALU.add))
                    nc.vector.tensor_scalar(vv[:, d, :], ss[:, d, :], 1.0 / HD, 1e-6, ALU.mult, ALU.add) \
                        .then_inc(s_vv, 1)

                def residual(u, d, g):
                    dve.wait_ge(s_rr, u + 1)
                    dve.wait_ge(s_scaled, u + 1)
                    link = Chain(dve, s_l1, 2, u)
                    hv = scaled[:, d, :].rearrange("p (h e) -> p h e", h=NH)
                    link(nc.vector.tensor_tensor(hv, hv, bcast_last(rr[:, d, :], HD), ALU.mult))
                    link(nc.vector.tensor_tensor(row(R.X, u), row(R.X, u), scaled[:, d, :], ALU.add), alone=R)
                    norm.statistics(dve, u, d)

                R.arrived(dve, "rms")
                nc.vector.tensor_scalar(R.rms[:, :], R.rms[:, :], 1.0, None, ALU.add).then_inc(s_rms, 1)
                dve.wait_ge(s_rms, 1)
                run_ticks(dve, B, 1, [(weigh, 1), (heads, 2), (residual, 3),
                                      (lambda u, d, g: norm.normalise(dve, u, d), 4)])

            @block.tensor
            def _(pe):
                def scores(u, d, g):
                    inputs(pe, u, d)
                    pe.wait_ge(s_qm, u + 1)
                    wait(pe, s_cT, u - 1)
                    nc.tensor.matmul(R.bank[d][:, 0:NH * P], ct[:, d, :], qm[:, d, :], start=True, stop=True) \
                        .then_inc(s_sc, 1)

                def values(u, d, g):
                    pe.wait_ge(s_cT, u + 1)
                    pe.wait_ge(s_v, u + 1)
                    wait(pe, s_hn, u - 1)
                    for h in range(NH):
                        mm = nc.tensor.matmul(R.bank[2 + d][:, h * (HD + 1):(h + 1) * (HD + 1)],
                                              cT[:, d, h * P:(h + 1) * P], vaug[:, d, h, :], start=True, stop=True)
                    mm.then_inc(s_hp, 1)

                run_ticks(pe, B, 1, [(scores, 0), (values, 1), (lambda u, d, g: norm.transpose(pe, u, d), 5)])

            @block.scalar
            def _(act):
                nc.scalar.preload_act_table(ACT.Exp)

                def decay(u, d, g):
                    act.wait_ge(s_mbm, u + 1)
                    wait(act, s_cT, u - 1)
                    for h in range(NH):
                        ins = nc.scalar.activation(dT[:, d, h * P:(h + 1) * P], mbm[:, d, h * P:(h + 1) * P], ACT.Exp,
                                                   scale=-1.0, bias=cols(gpre, u, NH, h, 1))
                    ins.then_inc(s_dT, 1)

                def mask_q(u, d, g):
                    wait(act, s_sc, u - 1)
                    for h in range(NH):
                        ins = nc.scalar.activation(qm[:, d, h * P:(h + 1) * P], row(R.XNT, u), ACT.Identity,
                                                   scale=R.head_of4[:, h, 0:1])
                    ins.then_inc(s_qm, 1)

                run_ticks(act, B, 1, [(mask_q, 0), (decay, 0), (lambda u, d, g: norm.store(act, u, d), 6)])
        m.clear_semaphores()


def phase_l0_ffn(nc, R, A):
    BITS = 6
    with ExitStack() as ctx:
        m = Memory(nc, ctx, "f0")
        power = m.sb("power", BITS)
        proj, bit, size, weakest, run = (m.sb(n, BITS) for n in ("proj", "bit", "size", "weakest", "run"))
        least, code = m.sb("least", 1), m.sb("code", 2)
        expert = m.sb("expert", 2 * B, dt=I32)
        s_pow, s_pe, s_dve, s_code = m.sem("pow"), m.sem("pe"), m.sem("dve"), m.sem("code")
        rows = slice(0, B)
        s_split = m.sem("split")
        with nc.Block() as block:
            @block.gpsimd
            def _(pool):
                for k in range(BITS):
                    nc.gpsimd.memset(power[rows, k:k + 1], float(2 ** k)).then_inc(s_pow, 1)
                R.arrived(pool, "l1_kv")
                w = R.w["l1"]["kv"][:, 1024:2048]
                nc.gpsimd.tensor_scalar(R.v_half[0][:, :], w, 1.0, None, ALU.mult).then_inc(s_split, 1)
                pool.wait_ge(s_split, 1)
                nc.gpsimd.tensor_tensor(R.v_half[1][:, :], w, R.v_half[0][:, :].bitcast(F32), ALU.subtract)

            @block.tensor
            def _(pe):
                R.arrived(pe, "hyper")
                nc.tensor.matmul(R.bank[0][rows, 0:BITS], R.token_sums[:, :], R.hyper[:, :], start=True, stop=True) \
                    .then_inc(s_pe, 1)
                pe.wait_ge(s_code, 1)
                for k in range(2):
                    mm = nc.tensor.transpose(R.bank[1][0:1, k * B:(k + 1) * B], code[rows, k:k + 1],
                                             R.ident[rows, rows])
                mm.then_inc(s_pe, 1)

            @block.vector
            def _(dve):
                link = Chain(dve, s_dve)
                V = nc.vector
                dve.wait_ge(s_pe, 1)
                link(V.tensor_scalar(proj[rows, :], R.bank[0][rows, 0:BITS], 1.0 / P, None, ALU.mult))
                link(V.tensor_scalar(bit[rows, :], proj[rows, :], 0.0, None, ALU.is_gt))
                link(V.tensor_scalar(size[rows, :], proj[rows, :], -1.0, None, ALU.mult))
                link(V.tensor_tensor(size[rows, :], size[rows, :], proj[rows, :], ALU.max))
                link(V.tensor_reduce(least[rows, :], size[rows, :], AX.X, ALU.min))
                link(V.tensor_scalar(weakest[rows, :], size[rows, :], least[rows, 0:1], None, ALU.is_equal))
                link(V.tensor_tensor_scan(run[rows, :], weakest[rows, :], weakest[rows, :], 0.0, ALU.add, ALU.bypass))
                link(V.tensor_scalar(run[rows, :], run[rows, :], 1.0, None, ALU.is_equal))
                link(V.tensor_tensor(weakest[rows, :], weakest[rows, :], run[rows, :], ALU.mult))
                dve.wait_ge(s_pow, BITS)
                link(V.tensor_scalar(run[rows, :], bit[rows, :], -2.0, 1.0, ALU.mult, ALU.add))
                link(V.tensor_tensor(run[rows, :], run[rows, :], weakest[rows, :], ALU.mult))
                link(V.tensor_tensor(run[rows, :], run[rows, :], bit[rows, :], ALU.add))
                link(V.tensor_tensor(run[rows, :], run[rows, :], power[rows, :], ALU.mult))
                link(V.tensor_tensor(bit[rows, :], bit[rows, :], power[rows, :], ALU.mult))
                link(V.tensor_reduce(code[rows, 0:1], bit[rows, :], AX.X, ALU.add))
                V.tensor_reduce(code[rows, 1:2], run[rows, :], AX.X, ALU.add).then_inc(s_code, 1)
                dve.wait_ge(s_pe, 2)
                V.tensor_copy(expert[0:1, :], R.bank[1][0:1, 0:2 * B])

        norm = NextNorm(nc, m, R, R.bank[7][:, 128:256], gamma_beta=R.l1_gb)
        xs, w = m.sb("xs", 2, P), m.sb("w", 2, 2, D)
        s_w = [m.sem("w0"), m.sem("w1")]
        s_xs, s_y, s_x = m.sem("xs"), m.sem("y"), m.sem("x")
        with nc.Block() as block:
            @block.sync
            def _(sp):
                def load(u, d, g):
                    wait(sp, s_y, u - 1)
                    for k in range(2):
                        at = expert[0:1, k * B + u:k * B + u + 1] if isinstance(u, int) else \
                            expert[0:1, bass.ds(u + k * B, 1)]
                        e = sp.value_load(at, min_val=0, max_val=63)
                        sp.dma_start(w[:, d, k, :], A["experts"][bass.ds(e, 1), :, :].rearrange("a p n -> p (a n)")) \
                            .then_inc(s_w[d], 16)
                run_ticks(sp, B, 1, [(load, 0)])

            @block.gpsimd
            def _(pool):
                run_ticks(pool, B, 1, [(lambda u, d, g: norm.root(pool, u, d), 1),
                                       (lambda u, d, g: norm.root(pool, u, d, 1), 2)])

            @block.vector
            def _(dve):
                def copy_x(u, d, g):
                    wait(dve, s_y, u - 1)
                    nc.vector.tensor_scalar(xs[:, d, :], row(R.XNT, u), 1.0, None, ALU.mult).then_inc(s_xs, 1)

                def residual(u, d, g):
                    dve.wait_ge(s_y, u + 1)
                    link = Chain(dve, s_x, 1, u)
                    link(nc.vector.scalar_tensor_tensor(out=row(R.X, u), in0=R.bank[d][:, 0:D], scalar=0.5,
                                                        in1=row(R.X, u), op0=ALU.mult, op1=ALU.add), alone=R)
                    norm.statistics(dve, u, d)

                def again(u, d, g):
                    norm.normalise(dve, u, d)
                    norm.statistics(dve, u, d, 1)

                run_ticks(dve, B, 1, [(copy_x, 0), (residual, 1), (again, 2),
                                      (lambda u, d, g: norm.normalise(dve, u, d, 1), 3)])

            @block.tensor
            def _(pe):
                def product(u, d, g):
                    pe.wait_ge(s_xs, u + 1)
                    n = (u // 2 + 1) * 32 if isinstance(u, int) else u * 16 + (32 - 16 * d)
                    pe.wait_ge(s_w[d], n)
                    wait(pe, s_x, u - 1)
                    for k in range(2):
                        mm = nc.tensor.matmul(R.bank[d][:, 0:D], xs[:, d, :], w[:, d, k, :], start=k == 0, stop=k == 1)
                    mm.then_inc(s_y, 1)

                run_ticks(pe, B, 1, [(product, 0), (lambda u, d, g: norm.transpose(pe, u, d), 3)])

            @block.scalar
            def _(act):
                R.arrived(act, "l1_gb")
                run_ticks(act, B, 1, [(lambda u, d, g: norm.store(act, u, d), 3)])
        m.clear_semaphores()


def phase_attention(nc, R, A, kind):
    wide = kind == 1
    HD = 64 if wide else 8
    NH, NQ, HQ = 16, 4, 4
    scale = 64 ** -0.5 if wide else (8 ** -0.5 if kind == 2 else float(8) ** 0.5)
    S = {1: 4, 2: 6, 3: 8}[kind]
    PV_PER_O = 1 if wide else 4
    PARTS = 2 if wide else 1
    Y = S + 5 + PARTS
    TURN = 1 if wide else 2
    W = R.w[f"l{kind}"]
    with ExitStack() as ctx:
        m = Memory(nc, ctx, f"a{kind}")
        norm = NextNorm(nc, m, R, R.bank[7][:, 128:256])
        C = NH * HD // P
        ct = m.sb("ct", 2, P)
        if kind != 2:
            qT = m.sb("qT", 2, C, P)
            kT = m.sb("kT", 2, C, P) if wide else m.sb("k_masked", 2, HQ, P)
        OH = HD + 1
        WIDE_ROW = OH if wide else NH * OH
        OWN = OH if wide else WIDE_ROW + OH
        vals = m.sb("vals", 2, NH * OWN)

        def own(d, h0=0, h1=NH, e0=0, e1=HD):
            return vals[:, d, h0 * OWN:h1 * OWN].rearrange("p (h e) -> p h e", e=OWN)[:, :, e0:e1]

        neg_max = m.sb("neg_max", 2, HQ)
        scaled_q = m.sb("scaled_q", 2)
        prob, probT = m.sb("prob", 2, HQ * P), m.sb("probT", 2, HQ * P)
        rden = m.sb("rden", 2, NH)
        heads, headsT = m.sb("heads", 2, NH * HD), m.sb("headsT", NH * HD)
        t_res = m.sb("t_res", 2, D)
        names = ("zeros ones q k v qe ke ve scores maxed exped ptr ptc pv o_link o oT oTc y res_link bias "
                 "half halves xs qkn qk_link qk_var qk_rstd qkT gate").split()
        s = {n: m.sem(n) for n in names}
        s_ct = [m.sem("ct0"), m.sem("ct1")]
        if wide:
            ct_half = [m.sb(f"ct_{h}", 2, P, dt=F32R) for h in ("high", "low")]
        if kind == 2:
            q_k = m.sb("q_k", 2, 2, P)
            q_half, k_half = ([m.sb(f"{n}_{h}", 2, P, dt=F32R) for h in ("high", "low")] for n in ("q", "k"))
            k_masked = [m.sb(f"k_masked_{h}", 2, HQ, P, dt=F32R) for h in ("high", "low")]
        if kind == 3:
            xs = m.sb("xs", 2, P)
            cen, sq = m.sb("cen", 2, 2 * D), m.sb("sq", 2, 2 * D)
            qk_sum, qk_var, qk_rstd = m.sb("qk_sum", 2, 32), m.sb("qk_var", 2, 32), m.sb("qk_rstd", 2, 32)
            gb_head = m.sb("gb_head", 2, HQ)

        def pair_count(u, d, n):
            return (u // 2 + 1) * n if isinstance(u, int) else u * (n // 2) + (n - n // 2 * d)

        def quad(u, g):
            return u * NQ + g

        def head_no(g, i):
            return 2 * (4 * (g // 2) + i) + g % 2 if wide else 4 * g + i

        with nc.Block() as block:
            @block.sync
            def _(sp):
                def load(u, d, g):
                    wait(sp, s["k"] if wide else s["v"], 3 * (u - 1) if wide else u - 1)
                    sp.dma_start(ct[:, d, :], row(A["ctxT"], u)).then_inc(s_ct[d], 16)
                run_ticks(sp, B, 1, [(load, 0)])

            @block.gpsimd
            def _(pool):
                nc.gpsimd.memset(vals[:, :, :], 0.0).then_inc(s["zeros"], 1)
                pool.wait_ge(s["zeros"], 1)
                for d in range(2):
                    nc.gpsimd.memset(own(d, e0=HD, e1=OH), 1.0).then_inc(s["ones"], 1)

                def qk_root(u, d, g):
                    pool.wait_ge(s["qk_var"], u + 1)
                    nc.gpsimd.tensor_tensor(qk_rstd[:, d, :], qk_var[:, d, :], R.minus_half[:, 0:32], ALU.pow) \
                        .then_inc(s["qk_rstd"], 1)

                def split_qk(u, d, g):
                    pool.wait_ge(s["qe"], u + 1)
                    wait(pool, s["scores"], 4 * u - 4)
                    T2 = nc.gpsimd.tensor_tensor
                    for n, half in enumerate((q_half, k_half)):
                        T2(half[0][:, d, :], q_k[:, d, n, :], R.ones[:, :], ALU.mult).then_inc(s["half"], 1)
                    pool.wait_ge(s["half"], 4 * u + 2)
                    for n, half in enumerate((q_half, k_half)):
                        T2(half[1][:, d, :], q_k[:, d, n, :], half[0][:, d, :].bitcast(F32), ALU.subtract) \
                            .then_inc(s["half"], 1)
                    pool.wait_ge(s["half"], 4 * u + 4)
                    for n in range(2):
                        ins = T2(k_masked[n][:, d, :, :], bcast_mid(k_half[n][:, d, :].bitcast(F32), HQ),
                                 R.head_of_quad[:, :, :], ALU.mult)
                    ins.then_inc(s["ke"], 1)

                st = [(lambda u, d, g: norm.root(pool, u, d), Y, 3)]
                if kind == 2:
                    st += [(split_qk, 1, 0)]
                if kind == 3:
                    st += [(qk_root, 2, 0)]
                run_ticks(pool, B, NQ, st)

            @block.vector
            def _(dve):
                V = nc.vector

                def evac_wide(part):
                    def fn(u, d, g):
                        dve.wait_ge(s["k"], 3 * u + part + 1)
                        if part < 2:
                            wait(dve, s["scores"], 4 * u - 4)
                            dst = (qT, kT)[part][:, d, 4:8, :].rearrange("p c t -> p (c t)")
                            src = R.bank[1][:, :]
                        else:
                            wait(dve, s["pv"], 4 * u - 4)
                            dst = own(d, 8, 16)
                            src = R.bank[1][:, :].rearrange("p (h e) -> p h e", e=HD)
                        if part == 0:
                            V.tensor_scalar(dst, src, scale, None, ALU.mult).then_inc(s["ke"], 1)
                        else:
                            V.tensor_copy(dst, src).then_inc(s["ke"], 1)
                    return fn

                def split_context(u, d, g):
                    dve.wait_ge(s_ct[d], pair_count(u, d, 16))
                    wait(dve, s["k"], 3 * (u - 1))
                    V.tensor_scalar(ct_half[0][:, d, :], ct[:, d, :], 1.0, None, ALU.mult).then_inc(s["half"], 1)
                    dve.wait_ge(s["half"], u + 1)
                    V.tensor_tensor(ct_half[1][:, d, :], ct[:, d, :], ct_half[0][:, d, :].bitcast(F32),
                                    ALU.subtract).then_inc(s["halves"], 1)

                v_bank = R.bank[1][:, 0:P] if kind == 2 else R.bank[0][:, 256:384]

                def evac_v(u, d, g):
                    dve.wait_ge(s["v"], u + 1)
                    wait(dve, s["pv"], 4 * u - 4)
                    src = v_bank.rearrange("p (h e) -> p h e", e=HD)
                    if kind == 2:
                        V.tensor_tensor(own(d), src, W["bv"][:, :].rearrange("p (h e) -> p h e", e=HD),
                                        ALU.add).then_inc(s["ve"], 1)
                    else:
                        V.tensor_copy(own(d), src).then_inc(s["ve"], 1)

                def copy_x(u, d, g):
                    wait(dve, s["q"], u - 1)
                    V.tensor_scalar(xs[:, d, :], row(R.XNT, u), 1.0, None, ALU.mult).then_inc(s["xs"], 1)

                def qk_stats(u, d, g):
                    dve.wait_ge(s["q"], u + 1)
                    wait(dve, s["qkT"], u - 1)
                    link = Chain(dve, s["qk_link"], 4, u)
                    qk = R.bank[1][:, 0:2 * D].rearrange("p (n e) -> p n e", e=HD)
                    c3, s3 = (t[:, d, :].rearrange("p (n e) -> p n e", e=HD) for t in (cen, sq))
                    link(V.tensor_reduce(qk_sum[:, d, :], qk, AX.X, ALU.add))
                    link(V.scalar_tensor_tensor(out=c3, in0=qk, scalar=float(HD), in1=bcast_last(qk_sum[:, d, :], HD),
                                                op0=ALU.mult, op1=ALU.subtract))
                    link(V.tensor_tensor(s3, c3, c3, ALU.mult))
                    link(V.tensor_reduce(qk_var[:, d, :], s3, AX.X, ALU.add))
                    V.tensor_scalar(qk_var[:, d, :], qk_var[:, d, :], 1.0 / HD ** 3, LN_EPS, ALU.mult, ALU.add) \
                        .then_inc(s["qk_var"], 1)

                def qk_norm(u, d, g):
                    dve.wait_ge(s["qk_rstd"], u + 1)
                    c3 = cen[:, d, :].rearrange("p (n e) -> p n e", e=HD)
                    V.tensor_tensor(c3, c3, bcast_last(qk_rstd[:, d, :], HD), ALU.mult).then_inc(s["qkn"], 1)

                def row_max(u, d, g):
                    k, b = quad(u, g), g % 2
                    dve.wait_ge(s["scores"], k + 1)
                    wait(dve, s["exped"], k - 1)
                    sc = R.bank[2 + b][:, :].rearrange("p (h t) -> p h t", h=HQ)
                    V.tensor_reduce(neg_max[:, b, :], sc, AX.X, ALU.max, negate=True).then_inc(s["maxed"], 1)

                def normalise_heads(u, d, g):
                    k = quad(u, g)
                    n = u * (NQ // PV_PER_O) + (g if wide else 0)
                    dve.wait_ge(s["pv"], k + 1)
                    if g == 0 or not wide:
                        wait(dve, s["oT"], PARTS * (u - 1))
                    link = Chain(dve, s["o_link"], 1, n)
                    hs = HQ if wide else NH
                    o = R.bank[6][:, 0:hs * (HD + 1)].rearrange("p (h e) -> p h e", e=HD + 1)
                    r = rden[:, d, 4 * g:4 * g + 4] if wide else rden[:, d, :]
                    link(V.reciprocal(r.unsqueeze(2), o[:, :, HD:HD + 1]))
                    if wide:
                        dst = heads[:, d, :].rearrange("p (c two e) -> p c two e", two=2, e=HD)[
                            :, 4 * (g // 2):4 * (g // 2) + 4, g % 2, :]
                    else:
                        dst = heads[:, d, :].rearrange("p (h e) -> p h e", e=HD)
                    V.tensor_tensor(dst, o[:, :, 0:HD], bcast_last(r, HD), ALU.mult).then_inc(s["o"], 1)

                def residual(u, d, g):
                    dve.wait_ge(s["y"], u + 1)
                    link = Chain(dve, s["res_link"], 2, u)
                    y = R.bank[7][:, 0:D]
                    if wide:
                        link(V.scalar_tensor_tensor(out=t_res[:, d, :], in0=y, scalar=W["gate"][:, 0:1],
                                                    in1=W["bo"][:, :], op0=ALU.mult, op1=ALU.add))
                    else:
                        link(V.tensor_tensor(t_res[:, d, :], y, W["bo"][:, :], ALU.add))
                    link(V.tensor_tensor(row(R.X, u), row(R.X, u), t_res[:, d, :], ALU.add), alone=R)
                    norm.statistics(dve, u, d)

                R.arrived(dve, f"l{kind}_bo")
                if wide:
                    dve.wait_ge(s["gate"], 1)
                    V.tensor_scalar(W["bo"][:, :], W["bo"][:, :], W["gate"][:, 0:1], None, ALU.mult) \
                        .then_inc(s["bias"], 1)
                    dve.wait_ge(s["bias"], 1)
                    st = [(evac_wide(0), 0, 0), (evac_wide(1), 0, 1), (split_context, 0, 2), (evac_wide(2), 0, 3)]
                elif kind == 2:
                    R.arrived(dve, "l2_bqk")
                    V.tensor_scalar(scaled_q[:, 0:1], W["bqk"][:, 0:1], scale, None, ALU.mult).then_inc(s["bias"], 1)
                    R.arrived(dve, "l2_bv")
                    st = [(evac_v, 2, 3)]
                else:
                    R.arrived(dve, "l3_gb")
                    for i, once in enumerate((1.0 / HD, 1.0)):
                        V.tensor_scalar(scaled_q[:, i:i + 1], W["gb"][:, i:i + 1], scale * once, None, ALU.mult) \
                            .then_inc(s["bias"], 1)
                        V.tensor_scalar(gb_head[:, i, :], R.head_of_quad[:, :, 0:1].rearrange("p h t -> p (h t)"),
                                        W["gb"][:, i:i + 1], once, ALU.mult, ALU.mult).then_inc(s["bias"], 1)
                    st = [(copy_x, 0, 0), (qk_stats, 2, 0), (qk_norm, 5, 0)]
                dve.wait_ge(s["ones"], 2)
                tail = [(lambda u, d, g: norm.normalise(dve, u, d), Y + 1, 3), (row_max, S)]
                if wide:
                    st = [(normalise_heads, S + 4)] + tail + st + [(residual, Y, 3)]
                else:
                    st = tail + [(normalise_heads, S + 3, 3)] + st + [(residual, Y, 3)]
                st += [(evac_v, 4, 3)] if kind == 3 else []
                run_ticks(dve, B, NQ, st)

            @block.tensor
            def _(pe):
                T = nc.tensor

                def context_here(u, d):
                    pe.wait_ge(s_ct[d], pair_count(u, d, 16))

                def project_wide(part):
                    def fn(u, d, g):
                        if part == 0:
                            context_here(u, d)
                        elif part == 2:
                            pe.wait_ge(s["halves"], u + 1)
                        for half, (free, done) in enumerate((("qe", "q"), ("ke", "k"))):
                            wait(pe, s[free], 3 * u + part)
                            bank = R.bank[half]
                            if part == 2:
                                for n, (i, j) in enumerate(((0, 0), (0, 1), (1, 0))):
                                    mm = T.matmul(bank[:, :], ct_half[i][:, d, :],
                                                  R.v_half[j][:, 512 * half:512 * half + 512],
                                                  start=n == 0, stop=n == 2)
                            else:
                                w = W["q"] if part == 0 else W["kv"]
                                rhs = row(R.XNT, u) if part == 0 else ct[:, d, :]
                                for i in range(4):
                                    c = 4 * half + i
                                    mm = T.matmul(bank[:, i * P:(i + 1) * P], w[:, c * P:(c + 1) * P], rhs,
                                                  start=True, stop=True)
                            mm.then_inc(s[done], 1)
                    return fn

                def project_q_k(u, d, g):
                    context_here(u, d)
                    wait(pe, s["qe"], u)
                    T.matmul(R.bank[0][:, 0:P], W["q"][:, :], row(R.XNT, u), start=True, stop=True)
                    T.matmul(R.bank[0][:, P:2 * P], W["kv"][:, 0:P], ct[:, d, :], start=True, stop=True) \
                        .then_inc(s["q"], 1)

                def project_v(u, d, g):
                    if kind == 2:
                        wait(pe, s["ve"], u)
                        out = R.bank[1][:, 0:P]
                    else:
                        pe.wait_ge(s["ke"], u + 1)
                        out = R.bank[0][:, 256:384]
                    T.matmul(out, ct[:, d, :], W["kv"][:, P:2 * P], start=True, stop=True).then_inc(s["v"], 1)

                def project_qk(u, d, g):
                    context_here(u, d)
                    pe.wait_ge(s["xs"], u + 1)
                    wait(pe, s["qk_var"], u)
                    T.matmul(R.bank[1][:, 0:P], xs[:, d, :], W["q"][:, :], start=True, stop=True)
                    T.matmul(R.bank[1][:, P:2 * P], ct[:, d, :], W["kv"][:, 0:P], start=True, stop=True) \
                        .then_inc(s["q"], 1)

                def turn_qk(u, d, g):
                    pe.wait_ge(s["qkn"], u + 1)
                    wait(pe, s["ve"], u)
                    for i in range(2):
                        mm = T.transpose(R.bank[0][:, i * P:(i + 1) * P], cen[:, d, i * P:(i + 1) * P], R.ident[:, :])
                    mm.then_inc(s["qkT"], 1)

                def scores(u, d, g):
                    k, b = quad(u, g), g % 2
                    if g == 0:
                        if kind != 2:
                            pe.wait_ge(s["qe"], 3 * u + 2 if wide else u + 1)
                        pe.wait_ge(s["ke"], 3 * u + 2 if wide else u + 1)
                    wait(pe, s["exped"], k - 1)
                    if wide:
                        for i in range(HQ):
                            c, r = 4 * (g // 2) + i, slice(HD * (g % 2), HD * (g % 2) + HD)
                            mm = T.matmul(R.bank[2 + b][:, i * P:(i + 1) * P], qT[r, d, c, :], kT[r, d, c, :],
                                          start=True, stop=True)
                    elif kind == 2:
                        r = slice(32 * g, 32 * g + 32)
                        for n, (i, j) in enumerate(((0, 0), (0, 1), (1, 0))):
                            mm = T.matmul(R.bank[2 + b][:, :], q_half[i][r, d, :],
                                          k_masked[j][r, d, :, :].rearrange("p h t -> p (h t)"),
                                          start=n == 0, stop=n == 2)
                    else:
                        r = slice(32 * g, 32 * g + 32)
                        mm = T.matmul(R.bank[2 + b][:, :], qT[r, d, 0, :],
                                      kT[r, d, :, :].rearrange("p h t -> p (h t)"), start=True, stop=True)
                    mm.then_inc(s["scores"], 1)

                def turn_prob(u, d, g):
                    k, b = quad(u, g), g % 2
                    pe.wait_ge(s["exped"], k + 1)
                    wait(pe, s["ptc"], k - 1)
                    for i in range(HQ):
                        mm = T.transpose(R.bank[4 + b][:, i * P:(i + 1) * P], prob[:, b, i * P:(i + 1) * P],
                                         R.ident[:, :])
                    mm.then_inc(s["ptr"], 1)

                def values(u, d, g):
                    k, b = quad(u, g), g % 2
                    pe.wait_ge(s["ptc"], k + 1)
                    if wide:
                        pe.wait_ge(s["qe"], 3 * u + 3)
                        pe.wait_ge(s["ke"], 3 * u + 3)
                        wait(pe, s["o"], k)
                    elif g == 0:
                        pe.wait_ge(s["ve"], u + 1)
                        wait(pe, s["o"], u)
                    for i in range(HQ):
                        h = head_no(g, i)
                        out = R.bank[6][:, i * OH:(i + 1) * OH] if wide else R.bank[6][:, 0:WIDE_ROW]
                        own_at = h * (OWN if wide else WIDE_ROW)
                        mm = T.matmul(out, probT[:, b, i * P:(i + 1) * P], vals[:, d, own_at:own_at + WIDE_ROW],
                                      start=wide or h == 0, stop=wide or h == NH - 1)
                    mm.then_inc(s["pv"], 1)

                def turn_heads(part):
                    def fn(u, d, g):
                        if part == 0:
                            pe.wait_ge(s["o"], (u + 1) * (NQ // PV_PER_O))
                            wait(pe, norm.stored, u)
                        else:
                            pe.wait_ge(s["oTc"], PARTS * u + part)
                        n = min(4, C)
                        for i in range(n):
                            c = 4 * part + i
                            mm = T.transpose(R.bank[7][:, i * P:(i + 1) * P], heads[:, d, c * P:(c + 1) * P],
                                             R.ident[:, :])
                        mm.then_inc(s["oT"], 1)
                    return fn

                def project_out(u, d, g):
                    pe.wait_ge(s["oTc"], PARTS * (u + 1))
                    for c in range(C):
                        mm = T.matmul(R.bank[7][:, 0:D], headsT[:, c * P:(c + 1) * P], W["o"][:, c * D:(c + 1) * D],
                                      start=c == 0, stop=c == C - 1)
                    mm.then_inc(s["y"], 1)

                for name in W["loaded"]:
                    R.arrived(pe, f"l{kind}_{name}")
                pe.wait_ge(s["ones"], 2)
                if wide:
                    st = [(project_wide(0), 0, 0), (project_wide(1), 0, 1), (project_wide(2), 0, 3)]
                elif kind == 2:
                    st = [(project_q_k, 0, 0), (project_v, 2, 3)]
                else:
                    st = [(project_qk, 1, 0), (turn_qk, 6, 0)]
                st = [(scores, S)] + st + [(turn_prob, S + 2), (project_out, Y, 3)]
                st += [(turn_heads(p), S + 5 + p, 3) for p in range(PARTS)]
                st += [(values, S + 3)] + ([(project_v, 4, 3)] if kind == 3 else [])
                turn = [(lambda u, d, g: norm.transpose(pe, u, d), Y + TURN, 3)]
                st = st + turn if wide else turn + st
                run_ticks(pe, B, NQ, st)

            @block.scalar
            def _(act):
                def evac_wide(part):
                    def fn(u, d, g):
                        act.wait_ge(s["q"], 3 * u + part + 1)
                        if part < 2:
                            wait(act, s["scores"], 4 * u - 4)
                            dst = (qT, kT)[part][:, d, 0:4, :].rearrange("p c t -> p (c t)")
                            src = R.bank[0][:, :]
                        else:
                            wait(act, s["pv"], 4 * u - 4)
                            dst = own(d, 0, 8)
                            src = R.bank[0][:, :].rearrange("p (h e) -> p h e", e=HD)
                        nc.scalar.activation(dst, src, ACT.Identity, scale=scale if part == 0 else 1.0) \
                            .then_inc(s["qe"], 1)
                    return fn

                def evac_q_k(u, d, g):
                    act.wait_ge(s["q"], u + 1)
                    wait(act, s["ke"], u - 1)
                    nc.scalar.activation(q_k[:, d, 0, :], R.bank[0][:, 0:P], ACT.Identity, scale=scale,
                                         bias=scaled_q[:, 0:1])
                    nc.scalar.activation(q_k[:, d, 1, :], R.bank[0][:, P:2 * P], ACT.Identity, bias=W["bqk"][:, 1:2]) \
                        .then_inc(s["qe"], 1)

                def mask_k(heads_of_quad):
                    def fn(u, d, g):
                        act.wait_ge(s["qkT"], u + 1)
                        for j in heads_of_quad:
                            ins = nc.scalar.activation(kT[:, d, j, :], R.bank[0][:, P:2 * P], ACT.Identity,
                                                       scale=gb_head[:, 0, j:j + 1], bias=gb_head[:, 1, j:j + 1])
                        if heads_of_quad[-1] == HQ - 1:
                            ins.then_inc(s["ke"], 1)
                    return fn

                def evac_q_normed(u, d, g):
                    act.wait_ge(s["qkT"], u + 1)
                    wait(act, s["scores"], 4 * u - 4)
                    nc.scalar.activation(qT[:, d, 0, :], R.bank[0][:, 0:P], ACT.Identity, scale=scaled_q[:, 0:1],
                                         bias=scaled_q[:, 1:2]).then_inc(s["qe"], 1)

                def exp(u, d, g):
                    k, b = quad(u, g), g % 2
                    act.wait_ge(s["maxed"], k + 1)
                    wait(act, s["ptr"], k - 1)
                    for i in range(HQ):
                        ins = nc.scalar.activation(prob[:, b, i * P:(i + 1) * P],
                                                   R.bank[2 + b][:, i * P:(i + 1) * P], ACT.Exp,
                                                   bias=neg_max[:, b, i:i + 1])
                    ins.then_inc(s["exped"], 1)

                def copy_prob(u, d, g):
                    k, b = quad(u, g), g % 2
                    act.wait_ge(s["ptr"], k + 1)
                    wait(act, s["pv"], k - 1)
                    nc.scalar.activation(probT[:, b, :], R.bank[4 + b][:, :], ACT.Identity).then_inc(s["ptc"], 1)

                def copy_heads(part):
                    def fn(u, d, g):
                        act.wait_ge(s["oT"], PARTS * u + part + 1)
                        wait(act, s["y"], u)
                        n = min(4, C) * P
                        nc.scalar.activation(headsT[:, part * n:(part + 1) * n], R.bank[7][:, 0:n], ACT.Identity) \
                            .then_inc(s["oTc"], 1)
                    return fn

                nc.scalar.preload_act_table(ACT.Exp)
                if wide:
                    R.arrived(act, "l1_gate")
                    nc.scalar.activation(W["gate"][:, 0:1], W["gate"][:, 0:1], ACT.Tanh).then_inc(s["gate"], 1)
                    st = [(evac_wide(0), 0, 0), (evac_wide(1), 0, 1), (evac_wide(2), 0, 3)]
                elif kind == 2:
                    act.wait_ge(s["bias"], 1)
                    R.arrived(act, "l2_bqk")
                    st = [(evac_q_k, 0, 0)]
                else:
                    act.wait_ge(s["bias"], 4)
                    st = [(evac_q_normed, 6, 0), (mask_k((0, 1)), 6, 0), (mask_k((2, 3)), 7, 0)]
                act.wait_ge(s["ones"], 2)
                st += [(copy_prob, S + 2)] + [(copy_heads(p), S + 5 + p, 3) for p in range(PARTS)]
                st += [(lambda u, d, g: norm.store(act, u, d), Y + TURN, 3), (exp, S)]
                run_ticks(act, B, NQ, st)
        m.clear_semaphores()


def phase_l1_ffn(nc, R, A):
    E, HC = 8, 4
    U, TT = B // 4, 4
    with ExitStack() as ctx:
        m = Memory(nc, ctx, "mlp")
        wr = m.sb("router", E)
        wg, sq, nrm, wgT = m.sb("wg", 16), m.sb("sq", 16), m.sb("nrm", 2), m.sb("wgT", E)
        lg, gate, mask = m.sb("lg", B, E), m.sb("gate", B, E), m.sb("mask", B, E)
        best, score, taken = m.sb("best", B), m.sb("score", B), m.sb("taken", B)
        s_pe, s_dve, s_act, s_pool, s_r = (m.sem(n) for n in ("pe", "dve", "act", "pool", "r"))
        W = R.w["f1"]
        norm = NextNorm(nc, m, R, R.bank[7][:, 128:256])
        h, acc = m.sb("h", 2, TT * P), m.sb("acc", TT, D)
        w1_half = [m.sb(f"w1_{n}", E, HC * P, dt=F32R) for n in ("high", "low")]
        x_half = [m.sb(f"x_{n}", 2, TT * P, dt=F32R) for n in ("high", "low")]
        s_w1, s_xh, s_xs = m.sem("w1"), m.sem("xh"), m.sem("xs")
        s_up, s_gelu, s_down, s_acc, s_x = (m.sem(n) for n in ("up", "gelu", "down", "acc", "x"))
        TICKS = E * HC
        with nc.Block() as block:
            def batch(u, t):
                return u * TT + t

            @block.tensor
            def _(pe):
                T = nc.tensor

                def up(u, d, g):
                    k = u * TICKS + g
                    wait(pe, s_gelu, k - 1)
                    e, c = g // HC, g % HC
                    if g == 0:
                        pe.wait_ge(s_xs, u + 1)
                    if c == 0 and isinstance(u, int) and u == 0:
                        pe.wait_ge(s_w1, 2 * e + 2)
                    for n, (i, j) in enumerate(((0, 0), (0, 1), (1, 0))):
                        mm = T.matmul(R.bank[g % 2][:, :], w1_half[i][:, e, c * P:(c + 1) * P], x_half[j][:, d, :],
                                      start=n == 0, stop=n == 2)
                    mm.then_inc(s_up, 1)

                def down(u, d, g):
                    k = u * TICKS + g
                    e, c = g // HC, g % HC
                    pe.wait_ge(s_gelu, k + 1)
                    if c == 0:
                        wait(pe, s_acc, u * 2 * E + 2 * e - 2)
                    for t in range(TT):
                        mm = T.matmul(R.bank[2 + e % 2][:, t * D:(t + 1) * D], h[:, g % 2, t * P:(t + 1) * P],
                                      W["w2"][:, e, c, :], start=c == 0 and t == 0, stop=c == HC - 1,
                                      skip_group_check=True)
                    mm.then_inc(s_down, 1)

                pe.wait_ge(s_dve, 6)
                T.transpose(R.bank[4][0:16, 0:E], wg[0:E, :], R.ident[0:E, 0:E]).then_inc(s_pe, 1)
                pe.wait_ge(s_dve, 7)
                R.arrived(pe, "f1_wg_red")
                T.matmul(R.bank[5][:, 0:E], W["wg_red"][0:16, :], wgT[0:16, :], start=True, stop=True) \
                    .then_inc(s_pe, 1)
                pe.wait_ge(s_dve, 8)
                for b in range(B):
                    mm = T.matmul(R.bank[6][:, b * E:(b + 1) * E], R.XNT[:, b, :], wr[:, :], start=True, stop=True)
                mm.then_inc(s_pe, 1)

                R.arrived(pe, "f1_w2")
                st = [(up, 0), (down, 2)]
                for t in range(TT):
                    st.append((lambda u, d, g, t=t: norm.transpose(pe, batch(u, t), t % 2), TICKS + 6 + 3 * t, 0))
                run_ticks(pe, U, TICKS, st, head=2)

            @block.scalar
            def _(act):
                def gelu(u, d, g):
                    k = u * TICKS + g
                    act.wait_ge(s_up, k + 1)
                    wait(act, s_down, k - 1)
                    nc.scalar.activation(h[:, g % 2, :], R.bank[g % 2][:, :], ACT.Gelu, bias=W["b1"][:, g:g + 1]) \
                        .then_inc(s_gelu, 1)

                nc.scalar.preload_act_table(ACT.Exp)
                act.wait_ge(s_dve, 10)
                nc.scalar.activation(gate[:, :, :], lg[:, :, :], ACT.Exp).then_inc(s_act, 1)

                nc.scalar.preload_act_table(ACT.Gelu)
                R.arrived(act, "f1_b1")
                st = [(gelu, 0)]
                for t in range(TT):
                    st.append((lambda u, d, g, t=t: norm.store(act, batch(u, t), t % 2), TICKS + 6 + 3 * t, 0))
                run_ticks(act, U, TICKS, st, head=2)

            @block.gpsimd
            def _(pool):
                pool.wait_ge(s_dve, 3)
                nc.gpsimd.tensor_tensor(nrm[0:E, 1:2], nrm[0:E, 0:1], R.minus_half[0:E, 0:1], ALU.pow) \
                    .then_inc(s_pool, 1)

                run_ticks(pool, U, TICKS, [
                    (lambda u, d, g, t=t: norm.root(pool, batch(u, t), t % 2), TICKS + 4 + 3 * t, 0)
                    for t in range(TT)], head=2)

            @block.vector
            def _(dve):
                V = nc.vector
                R.arrived(dve, "f1_w1")

                def split_x(u, d, g):
                    wait(dve, s_up, (u - 1) * TICKS)
                    x = R.XNT[:, u * TT:(u + 1) * TT, :] if isinstance(u, int) else R.XNT[:, bass.ds(u * TT, TT), :]
                    x = x.rearrange("p b t -> p (b t)")
                    if not isinstance(u, int):
                        dve.memset(R.carrier[:, :], 0.0)
                    V.tensor_scalar(x_half[0][:, d, :], x, 1.0, None, ALU.mult).then_inc(s_xh, 1)
                    wait_alone(dve, R, s_xh, u + 1)
                    V.tensor_tensor(x_half[1][:, d, :], x, x_half[0][:, d, :].bitcast(F32), ALU.subtract) \
                        .then_inc(s_xs, 1)

                split_x(0, 0, 0)
                for e in range(E):
                    V.tensor_scalar(w1_half[0][:, e, :], W["w1"][:, e, :], 1.0, None, ALU.mult).then_inc(s_w1, 1)
                    dve.wait_ge(s_w1, 2 * e + 1)
                    V.tensor_tensor(w1_half[1][:, e, :], W["w1"][:, e, :], w1_half[0][:, e, :].bitcast(F32),
                                    ALU.subtract).then_inc(s_w1, 1)
                link = Chain(dve, s_dve)
                R.arrived(dve, "f1_wg")
                link(V.tensor_tensor(sq[0:E, :], W["wg"][0:E, :], W["wg"][0:E, :], ALU.mult))
                link(V.tensor_reduce(nrm[0:E, 0:1], sq[0:E, :], AX.X, ALU.add))
                link(V.tensor_scalar(nrm[0:E, 0:1], nrm[0:E, 0:1], 1e-8, None, ALU.max))
                dve.wait_ge(s_pool, 1)
                link(V.tensor_scalar(wg[0:E, :], W["wg"][0:E, :], nrm[0:E, 1:2], None, ALU.mult))
                link(V.memset(taken[:, :], 0.0))
                link(V.memset(mask[:, :, :], 0.0))
                dve.wait_ge(s_pe, 1)
                link(V.tensor_copy(wgT[0:16, :], R.bank[4][0:16, 0:E]))
                dve.wait_ge(s_pe, 2)
                link(V.tensor_copy(wr[:, :], R.bank[5][:, 0:E]))
                dve.wait_ge(s_pe, 3)
                logits = R.bank[6][:, 0:B * E].rearrange("p (b e) -> p b e", e=E)
                link(V.tensor_reduce(best[:, :], logits, AX.X, ALU.max))
                link(V.tensor_tensor(lg[:, :, :], logits, bcast_last(best[:, :], E), ALU.subtract))
                dve.wait_ge(s_act, 1)
                link(V.tensor_reduce(score[:, :], gate[:, :, :], AX.X, ALU.add))
                link(V.reciprocal(score[:, :], score[:, :]))
                link(V.tensor_scalar(gate[:, :, :], gate[:, :, :], 1.0, None, ALU.is_ge))
                for e in range(E):
                    link(V.tensor_tensor(mask[:, :, e], gate[:, :, e], taken[:, :], ALU.is_gt))
                    link(V.tensor_tensor(taken[:, :], taken[:, :], gate[:, :, e], ALU.max))

                R.arrived(dve, "f1_b2")

                def add_expert(u, d, g):
                    e = g // HC
                    link = Chain(dve, s_acc, 2 * E, u)
                    link.k = 2 * e
                    for t in range(TT):
                        w = mask[:, u * TT + t, e:e + 1] if isinstance(u, int) else \
                            mask[:, bass.ds(u * TT + t, 1), e:e + 1].rearrange("p a b -> p (a b)")
                        if e == 0:
                            ins = V.tensor_scalar(acc[:, t, :], W["b2"][:, e, :], w, None, ALU.mult)
                        else:
                            ins = V.scalar_tensor_tensor(out=acc[:, t, :], in0=W["b2"][:, e, :], scalar=w,
                                                         in1=acc[:, t, :], op0=ALU.mult, op1=ALU.add)
                    link(ins)
                    dve.wait_ge(s_down, u * TICKS + HC * (e + 1))
                    for t in range(TT):
                        w = mask[:, u * TT + t, e:e + 1] if isinstance(u, int) else \
                            mask[:, bass.ds(u * TT + t, 1), e:e + 1].rearrange("p a b -> p (a b)")
                        ins = V.scalar_tensor_tensor(out=acc[:, t, :], in0=R.bank[2 + e % 2][:, t * D:(t + 1) * D],
                                                     scalar=w, in1=acc[:, t, :], op0=ALU.mult, op1=ALU.add)
                    link(ins)

                def residual(u, d, g):
                    for t in range(TT):
                        b = batch(u, t)
                        w = score[:, b:b + 1] if isinstance(u, int) else score[:, bass.ds(b, 1)]
                        ins = V.scalar_tensor_tensor(out=row(R.X, b), in0=acc[:, t, :], scalar=w, in1=row(R.X, b),
                                                     op0=ALU.mult, op1=ALU.add)
                    ins.then_inc(s_x, 1)

                def stats(t):
                    def fn(u, d, g):
                        wait_alone(dve, R, s_x, u + 1)
                        norm.statistics(dve, batch(u, t), t % 2)
                    return fn

                AHEAD = 8
                st = [(lambda u, d, g: split_x(u, d, g) if not isinstance(u, int) or u else None, 0, 0)]
                st += [(add_expert, AHEAD + 3, e * HC + 3) for e in range(E)] + [(residual, AHEAD + TICKS + 3, 0)]
                for t in range(TT):
                    st.append((stats(t), AHEAD + TICKS + 4 + 3 * t, 0))
                    st.append((lambda u, d, g, t=t: norm.normalise(dve, batch(u, t), t % 2),
                               AHEAD + TICKS + 6 + 3 * t, 0))
                run_ticks(dve, U, TICKS, st, head=2)
        m.clear_semaphores()


def phase_gated_ffn(nc, R, A, kind):
    E, G, I, TOP, TOPG = 16, 4, 64, 4, 2
    with ExitStack() as ctx:
        m = Memory(nc, ctx, f"mlp{kind}")
        W = R.w[f"g{kind}"]
        combine = m.sb("combine", B, E)
        gate_half, up_half = ([m.sb(f"{n}_{h}", E * I, dt=F32R) for h in ("high", "low")] for n in ("gate", "up"))
        s_split = m.sem("split")
        s_pe, s_dve, s_act, s_pool = (m.sem(n) for n in ("pe", "dve", "act", "pool"))
        with ExitStack() as ctx2:
            m2 = Memory(nc, ctx2, f"r{kind}")
            score, choice, tmp, rank = (m2.sb(n, B, E) for n in ("score", "choice", "tmp", "rank"))
            later, cnt = m2.sb("later", B, E), m2.sb("cnt", B, E)
            group, pair, grank, gtmp, gcnt = (m2.sb(n, B, G) for n in ("group", "pair", "grank", "gtmp", "gcnt"))
            total = m2.sb("total", B)
            with nc.Block() as block:
                @block.gpsimd
                def _(pool):
                    for e in range(E):
                        nc.gpsimd.memset(later[:, :, e], float(E - 1 - e)).then_inc(s_pool, 1)
                    R.arrived(pool, f"g{kind}_gate")
                    for n, (half, w) in enumerate(((gate_half, W["gate"]), (up_half, W["up"]))):
                        nc.gpsimd.tensor_scalar(half[0][:, :], w[:, :], 1.0, None, ALU.mult).then_inc(s_split, 1)
                        pool.wait_ge(s_split, 2 * n + 1)
                        nc.gpsimd.tensor_tensor(half[1][:, :], w[:, :], half[0][:, :].bitcast(F32), ALU.subtract) \
                            .then_inc(s_split, 1)

                @block.tensor
                def _(pe):
                    R.arrived(pe, f"g{kind}_router")
                    for b in range(B):
                        mm = nc.tensor.matmul(R.bank[0][:, b * E:(b + 1) * E], R.XNT[:, b, :], W["router"][:, :],
                                              start=True, stop=True)
                    mm.then_inc(s_pe, 1)

                @block.scalar
                def _(act):
                    act.wait_ge(s_pe, 1)
                    nc.scalar.activation(score[:, :, :].rearrange("p b e -> p (b e)"), R.bank[0][:, :], ACT.Sigmoid) \
                        .then_inc(s_act, 1)

                @block.vector
                def _(dve):
                    V = nc.vector
                    link = Chain(dve, s_dve)

                    def rank_of(v, n, rank, tmp, cnt):
                        link(V.memset(rank[:, :, :], 0.0))
                        link(V.memset(cnt[:, :, n - 1], 0.0))
                        for e in range(n - 1):
                            k = n - 1 - e
                            link(V.tensor_tensor(tmp[:, :, e + 1:], bcast_last(v[:, :, e], k), v[:, :, e + 1:],
                                                 ALU.is_ge))
                            V.tensor_tensor(rank[:, :, e + 1:], rank[:, :, e + 1:], tmp[:, :, e + 1:], ALU.add) \
                                .then_inc(s_dve, 1)
                            link.k += 1
                            link(V.tensor_reduce(cnt[:, :, e], tmp[:, :, e + 1:], AX.X, ALU.add))
                        link(V.tensor_tensor(rank[:, :, :], rank[:, :, :], cnt[:, :, :], ALU.subtract))
                        link(V.tensor_tensor(rank[:, :, :], rank[:, :, :], later[:, :, E - n:], ALU.add))

                    dve.wait_ge(s_pool, E)
                    R.arrived(dve, f"g{kind}_bias")
                    dve.wait_ge(s_act, 1)
                    link(V.tensor_tensor(choice[:, :, :], score[:, :, :], bcast_mid(W["bias"][:, :], B), ALU.add))
                    c4 = choice[:, :, :].rearrange("p b (g k) -> p (b g) k", g=G)
                    gr, pr = (t[:, :, :].rearrange("p b g -> p (b g)") for t in (group, pair))
                    link(V.tensor_tensor(gr, c4[:, :, 0], c4[:, :, 1], ALU.add))
                    for i, j in ((0, 2), (0, 3), (1, 2), (1, 3), (2, 3)):
                        link(V.tensor_tensor(pr, c4[:, :, i], c4[:, :, j], ALU.add))
                        link(V.tensor_tensor(gr, gr, pr, ALU.max))
                    rank_of(group, G, grank, gtmp, gcnt)
                    link(V.tensor_scalar(grank[:, :, :], grank[:, :, :], float(TOPG), None, ALU.is_lt))
                    kept = bcast_last(grank[:, :, :].rearrange("p b g -> p (b g)"), E // G)
                    link(V.tensor_tensor(c4, c4, kept, ALU.mult))
                    if kind == 3:
                        link(V.tensor_scalar(gtmp[:, :, :], grank[:, :, :], 1e9, -1e9, ALU.mult, ALU.add))
                        link(V.tensor_tensor(c4, c4, bcast_last(gtmp[:, :, :].rearrange("p b g -> p (b g)"), E // G),
                                             ALU.add))
                    rank_of(choice, E, rank, tmp, cnt)
                    link(V.tensor_scalar(rank[:, :, :], rank[:, :, :], float(TOP), None, ALU.is_lt))
                    link(V.tensor_tensor(score[:, :, :], score[:, :, :], rank[:, :, :], ALU.mult))
                    link(V.tensor_reduce(total[:, :], score[:, :, :], AX.X, ALU.add))
                    link(V.tensor_scalar(total[:, :], total[:, :], 1e-20, None, ALU.add))
                    link(V.reciprocal(total[:, :], total[:, :]))
                    if kind == 3:
                        link(V.tensor_scalar(total[:, :], total[:, :], 2.5, None, ALU.mult))
                    V.tensor_tensor(combine[:, :, :], score[:, :, :], bcast_last(total[:, :], E), ALU.mult)

        last = kind == 3
        norm = None if last else NextNorm(nc, m, R, R.bank[7][:, 128:256])
        H = E // 2 * I
        x_half = [m.sb(f"x_{n}", 2, P, dt=F32R) for n in ("high", "low")]
        sil, act_t, wact, wactT = (m.sb("sil", 2, H), m.sb("act", 2, H), m.sb("wact", 2, H),
                                       m.sb("wactT", 2, H))
        s = {n: m.sem(n) for n in "xh xs gate up silu mul weigh turn copy y x out".split()}
        with nc.Block() as block:
            @block.tensor
            def _(pe):
                T = nc.tensor

                def product(bank, d, g, w_half):
                    for n, (i, j) in enumerate(((0, 0), (0, 1), (1, 0))):
                        mm = T.matmul(bank[:, :], x_half[i][:, d, :], w_half[j][:, g * H:(g + 1) * H],
                                      start=n == 0, stop=n == 2)
                    return mm

                def gate_up(u, d, g):
                    k = 2 * u + g
                    if g == 0:
                        pe.wait_ge(s["xs"], u + 1)
                    wait(pe, s["silu"], k - 1)
                    product(R.bank[g], d, g, gate_half).then_inc(s["gate"], 1)
                    wait(pe, s["mul"], k - 1)
                    product(R.bank[2 + g], d, g, up_half).then_inc(s["up"], 1)

                def turn(u, d, g):
                    k = 2 * u + g
                    pe.wait_ge(s["weigh"], k + 1)
                    wait(pe, s["copy"], k - 1)
                    for i in range(4):
                        mm = T.transpose(R.bank[4 + g][:, i * P:(i + 1) * P], wact[:, g, i * P:(i + 1) * P],
                                         R.ident[:, :])
                    mm.then_inc(s["turn"], 1)

                def down(u, d, g):
                    k = 2 * u + g
                    pe.wait_ge(s["copy"], k + 1)
                    if g == 0:
                        wait(pe, s["x"], u)
                    for i in range(4):
                        c = 4 * g + i
                        mm = T.matmul(R.bank[6][:, 0:D], wactT[:, g, i * P:(i + 1) * P], W["down"][:, c, :],
                                      start=c == 0, stop=c == 7)
                    mm.then_inc(s["y"], 1)

                R.arrived(pe, f"g{kind}_down")
                pe.wait_ge(s_split, 4)
                st = [(gate_up, 1), (turn, 3), (down, 4)]
                if not last:
                    st.append((lambda u, d, g: norm.transpose(pe, u, d), 7, 1))
                run_ticks(pe, B, 2, st)

            @block.scalar
            def _(act):
                def silu(u, d, g):
                    k = 2 * u + g
                    act.wait_ge(s["gate"], k + 1)
                    wait(act, s["mul"], k - 1)
                    nc.scalar.activation(sil[:, g, :], R.bank[g][:, :], ACT.Silu).then_inc(s["silu"], 1)

                def copy(u, d, g):
                    k = 2 * u + g
                    act.wait_ge(s["turn"], k + 1)
                    wait(act, s["y"], k - 1)
                    nc.scalar.activation(wactT[:, g, :], R.bank[4 + g][:, :], ACT.Identity).then_inc(s["copy"], 1)

                nc.scalar.preload_act_table(ACT.Silu)
                st = [(silu, 1), (copy, 3)]
                if not last:
                    st.append((lambda u, d, g: norm.store(act, u, d), 7, 1))
                run_ticks(act, B, 2, st)

            @block.gpsimd
            def _(pool):
                if not last:
                    run_ticks(pool, B, 2, [(lambda u, d, g: norm.root(pool, u, d), 5, 1)])

            @block.vector
            def _(dve):
                V = nc.vector

                def split_x(u, d, g):
                    wait(dve, s["up"], 2 * (u - 1))
                    V.tensor_scalar(x_half[0][:, d, :], row(R.XNT, u), 1.0, None, ALU.mult).then_inc(s["xh"], 1)
                    wait_alone(dve, R, s["xh"], u + 1)
                    V.tensor_tensor(x_half[1][:, d, :], row(R.XNT, u), x_half[0][:, d, :].bitcast(F32),
                                    ALU.subtract).then_inc(s["xs"], 1)

                def multiply(u, d, g):
                    k = 2 * u + g
                    dve.wait_ge(s["silu"], k + 1)
                    dve.wait_ge(s["up"], k + 1)
                    V.tensor_tensor(act_t[:, g, :], R.bank[2 + g][:, :], sil[:, g, :], ALU.mult).then_inc(s["mul"], 1)

                def weigh(u, d, g):
                    k = 2 * u + g
                    dve.wait_ge(s["mul"], k + 1)
                    wait(dve, s["turn"], k - 1)
                    w = combine[:, u, 8 * g:8 * g + 8] if isinstance(u, int) else \
                        combine[:, bass.ds(u, 1), 8 * g:8 * g + 8].rearrange("p a e -> p (a e)")
                    if not isinstance(u, int):
                        dve.memset(R.carrier[:, :], 0.0)
                    V.tensor_tensor(wact[:, g, :].rearrange("p (e i) -> p e i", i=I),
                                    act_t[:, g, :].rearrange("p (e i) -> p e i", i=I), bcast_last(w, I),
                                    ALU.mult).then_inc(s["weigh"], 1)

                def residual(u, d, g):
                    dve.wait_ge(s["y"], 2 * (u + 1))
                    V.tensor_tensor(row(R.X, u), row(R.X, u), R.bank[6][:, 0:D], ALU.add).then_inc(s["x"], 1)
                    if not last:
                        wait_alone(dve, R, s["x"], u + 1)
                        norm.statistics(dve, u, d)

                st = [(residual, 5, 1), (split_x, 0, 0), (multiply, 1), (weigh, 1)]
                if not last:
                    st.append((lambda u, d, g: norm.normalise(dve, u, d), 6, 1))
                run_ticks(dve, B, 2, st)

            @block.sync
            def _(sp):
                if last:
                    def store(u, d, g):
                        sp.wait_ge(s["x"], u + 1)
                        sp.dma_start(row(A["out"], u), row(R.X, u)).then_inc(s["out"], 16)
                    run_ticks(sp, B, 1, [(store, 0)])
                    sp.wait_ge(s["out"], 16 * B)
        m.clear_semaphores()


def build(nc, A, phases):
    with ExitStack() as ctx:
        R = Resident()

        def sb(name, *shape, dt=F32):
            return ctx.enter_context(nc.sbuf_tensor(name, [P, *shape], dt))

        R.X, R.XNT = sb("X", B, D), sb("XNT", B, P)
        R.bank = [ctx.enter_context(nc.psum_tensor(f"bank{i}", [P, 512], F32)) for i in range(8)]
        R.ident, R.upto, R.future, R.ones = sb("ident", P), sb("upto", P), sb("future", P), sb("ones", P)
        R.pick = sb("pick", P)
        R.carrier = sb("carrier", 1)
        R.v_half = [sb(f"v_{n}", 1024, dt=F32R) for n in ("high", "low")]
        R.minus_half = sb("minus_half", 64)
        R.head_of4, R.head_of_quad = sb("head_of4", 4, P), sb("head_of_quad", 4, P)
        R.token_sums = sb("token_sums", B)
        R.constants = ctx.enter_context(nc.semaphore("constants"))
        R.loads, R.w, R.load_sem, R.load_count = {}, {}, {}, {}

        def weight(name, *shape, rows=P):
            t = sb(name, *shape)
            src = A[name]
            if len(src.shape) == 1:
                src = src.partition_broadcast(P)
            dst = t[tuple([slice(0, rows)] + [slice(None)] * len(shape))]
            phase, _, part = name.partition("_")
            if phase not in R.load_sem:
                R.load_sem[phase], R.load_count[phase] = ctx.enter_context(nc.semaphore(f"load_{phase}")), 0
            R.load_count[phase] += 16
            R.loads[name] = (dst, src, R.load_sem[phase])
            R.w.setdefault(phase, {"loaded": ("q", "kv", "o")})[part] = t
            return t

        R.gate_w, R.gate_b, R.rms = weight("gate_w", 3, 8), weight("gate_b", 8), weight("rms", 32)
        R.hyper, R.l1_gb = weight("hyper", 6), weight("l1_gb", 2)
        weight("l1_q", 1024), weight("l1_kv", 2048), weight("l1_o", 1024), weight("l1_bo", D), weight("l1_gate", 1)
        weight("f1_wg", 16, rows=8), weight("f1_wg_red", P, rows=16)
        weight("f1_w1", 8, 512), weight("f1_b1", 32), weight("f1_w2", 8, 4, D), weight("f1_b2", 8 * D)
        R.w["f1"]["b2"] = R.w["f1"]["b2"][:, :].rearrange("p (e n) -> p e n", e=8)
        for k in (2, 3):
            weight(f"l{k}_q", P), weight(f"l{k}_kv", 2 * P), weight(f"l{k}_o", D), weight(f"l{k}_bo", D)
            if k == 2:
                weight("l2_bqk", 2), weight("l2_bv", P)
            else:
                weight("l3_gb", 2)
            weight(f"g{k}_router", 16), weight(f"g{k}_bias", 16)
            weight(f"g{k}_gate", 1024), weight(f"g{k}_up", 1024), weight(f"g{k}_down", 8, D)

        def arrived(eng, name):
            phase = name.partition("_")[0]
            eng.wait_ge(R.load_sem[phase], R.load_count[phase])

        R.arrived = arrived
        for phase in phases:
            phase(nc, R, A)


def l1_xattn(nc, R, A):
    phase_attention(nc, R, A, 1)


def l2_xattn(nc, R, A):
    phase_attention(nc, R, A, 2)


def l3_xattn(nc, R, A):
    phase_attention(nc, R, A, 3)


def l2_ffn(nc, R, A):
    phase_gated_ffn(nc, R, A, 2)


def l3_ffn(nc, R, A):
    phase_gated_ffn(nc, R, A, 3)


PHASES = [phase_input, phase_l0_xattn, phase_l0_ffn, l1_xattn, phase_l1_ffn, l2_xattn, l2_ffn, l3_xattn, l3_ffn]


def kernel(**inputs):
    import numpy as np
    import concourse.bacc as bacc
    from concourse.bass_utils import run_bass_kernel_spmd

    def n(name):
        return np.asarray(inputs[name])

    c = np.ascontiguousarray
    arrays = {
        "x": c(n("x").transpose(1, 0, 2)),
        "ctx": c(n("ctx_1024").transpose(1, 0, 2)),
        "ctxT": c(n("ctx_1024").transpose(2, 0, 1)),
        "gate_w": c(np.concatenate([n("L0_xattn_igate_kernel"), n("L0_xattn_fgate_kernel")], 1)
                    .reshape(3, 128, 8).transpose(1, 0, 2)),
        "gate_b": np.concatenate([n("L0_xattn_igate_bias"), n("L0_xattn_fgate_bias")]),
        "rms": n("L0_xattn_rms_scale"),
        "hyper": n("L0_ffn_hyperplanes"),
        "experts": n("L0_ffn_expert_weights"),
        "l1_gb": c(np.stack([n("L1_xattn_ln_gamma"), n("L1_xattn_ln_beta")], 1)),
        "l1_q": n("L1_xattn_w_q"), "l1_kv": n("L1_xattn_w_kv"),
        "l1_o": c(n("L1_xattn_w_out").reshape(8, 128, 128).transpose(1, 0, 2).reshape(128, 1024)),
        "l1_bo": n("L1_xattn_b_out"), "l1_gate": n("L1_xattn_gate"),
        "f1_wg": n("L1_ffn_wg"), "f1_wg_red": n("L1_ffn_wg_red"),
        "f1_w1": c(n("L1_ffn_w1").transpose(1, 0, 2)),
        "f1_b1": c(n("L1_ffn_b1").reshape(32, 128).T),
        "f1_w2": c(n("L1_ffn_w2").reshape(8, 4, 128, 128).transpose(2, 0, 1, 3)),
        "f1_b2": n("L1_ffn_b2").reshape(-1),
        "l2_q": c(n("L2_xattn_Wq").transpose(1, 0, 2).reshape(128, 128)),
        "l2_kv": c(np.concatenate([n("L2_xattn_Wk").transpose(1, 0, 2).reshape(128, 128),
                                   n("L2_xattn_Wv").transpose(1, 0, 2).reshape(128, 128)], 1)),
        "l2_o": n("L2_xattn_Wo"), "l2_bo": n("L2_xattn_bo"), "l2_bv": n("L2_xattn_bv").reshape(-1),
        "l2_bqk": c(np.stack([n("L2_xattn_bq").reshape(-1), n("L2_xattn_bk").reshape(-1)], 1)),
        "l3_q": n("L3_xattn_Wq"), "l3_kv": n("L3_xattn_Wkv"), "l3_o": n("L3_xattn_Wp"), "l3_bo": n("L3_xattn_bp"),
        "l3_gb": c(np.stack([np.tile(n("L3_xattn_ln_g"), 16), np.tile(n("L3_xattn_ln_b"), 16)], 1)),
        "g2_router": c(n("L2_ffn_gate_weight").T), "g2_bias": n("L2_ffn_e_bias"),
        "g3_router": c(n("L3_ffn_router_weight").T), "g3_bias": n("L3_ffn_router_bias"),
    }
    for k, (gate, up, down) in {"g2": ("L2_ffn_gate_proj", "L2_ffn_up_proj", "L2_ffn_down_proj"),
                                "g3": ("L3_ffn_w_gate", "L3_ffn_w_up", "L3_ffn_w_down")}.items():
        arrays[f"{k}_gate"] = c(n(gate).reshape(1024, 128).T)
        arrays[f"{k}_up"] = c(n(up).reshape(1024, 128).T)
        arrays[f"{k}_down"] = c(n(down).transpose(0, 2, 1).reshape(8, 128, 128).transpose(1, 0, 2))
    nc = bacc.Bacc("TRN2", target_bir_lowering=False, num_devices=1)
    A = {k: nc.dram_tensor(f"in_{k}", v.shape, mybir.dt.from_np(v.dtype), kind="ExternalInput").ap()
         for k, v in arrays.items()}
    A["out"] = nc.dram_tensor("out_0", (P, B, D), F32, kind="ExternalOutput").ap()
    build(nc, A, PHASES)
    r = run_bass_kernel_spmd(nc, [{f"in_{k}": v for k, v in arrays.items()}], core_ids=[0])
    return r.results[0]["out_0"].transpose(1, 0, 2)
```
